# Optimizing a Trainium2 kernel written in Bass

```python
import numpy as np
import jax
import jax.numpy as jnp

def _softmax(x, axis=-1):
    return jax.nn.softmax(x, axis=axis)

def _gelu(x):
    return jax.nn.gelu(x, approximate=True)

def _silu(x):
    return jax.nn.silu(x)

def _sigmoid(x):
    return jax.nn.sigmoid(x)

def _layernorm(x, axis=-1, eps=1e-05):
    m = jnp.mean(x, axis=axis, keepdims=True)
    v = jnp.var(x, axis=axis, keepdims=True)
    return (x - m) / jnp.sqrt(v + eps)

def _scatter_add(tgt, idx, src, axis=0):
    return tgt.at[idx].add(src)

def _segment_sum(src, seg, n):
    return jax.ops.segment_sum(src, seg, n)
kernel_name = 'mk_xattn_ffn_d2_seqx_r4_4afe63'

def setup_inputs(seed: int=0):
    np.random.seed(seed)
    _w = jnp.asarray

    def _rec_inputs():
        import jax
        import jax.numpy as jnp
        _rk = jax.random.key(seed)
        x = -0.0003929 + 0.9999 * jax.random.normal(jax.random.fold_in(_rk, 1), (16, 128, 512), jnp.float32)
        _lenS = 128 - jax.random.randint(jax.random.fold_in(_rk, 7), (16,), 0, max(1, 128 // 4) + 1, jnp.int32)
        _lenS2 = 128 - jax.random.randint(jax.random.fold_in(_rk, 8), (16,), 0, max(1, 128 // 4) + 1, jnp.int32)
        _ctx_1024P = jax.random.normal(jax.random.fold_in(_rk, 11), (16, 16, 256), jnp.float32)
        _ctx_1024c = jax.random.dirichlet(jax.random.fold_in(_rk, 511), 0.3 * jnp.ones((16,), jnp.float32), (16, 128))
        _ctx_1024t = jnp.einsum('bsk,bkd->bsd', _ctx_1024c, _ctx_1024P)
        _ctx_1024t = _ctx_1024t * jax.lax.rsqrt(jnp.mean(jnp.square(_ctx_1024t)) + 1e-12) * 0.953939
        ctx_1024 = 0.000227908 + 0.99994 * (_ctx_1024t + 0.3 * jax.random.normal(jax.random.fold_in(_rk, 611), (16, 128, 256), jnp.float32))
        fside_BxSx2_0 = jax.random.uniform(jax.random.fold_in(_rk, 12), (16, 128, 2), jnp.float32, 0.0, 0.999707)
        return (x, ctx_1024, fside_BxSx2_0)
    x, ctx_1024, fside_BxSx2_0 = _rec_inputs()

    def _L0_xattn_setup():
        import jax, jax.numpy as jnp
        import numpy as np
        EPS = 1e-05

        def rmsnorm(x, g, eps=EPS):
            var = jnp.mean(jnp.square(x), axis=-1, keepdims=True)
            return x * jax.lax.rsqrt(var + eps) * g
        key = jax.random.key(seed)
        ks = jax.random.split(key, 8)
        B, Sq, Skv = (2, 1024, 128)
        dim, cdim, H, D = (512, 256, 16, 128)
        inner = H * D
        s = lambda f: 1.0 / np.sqrt(f)
        return {'hidden_states': jax.random.normal(ks[0], (B, Sq, dim), jnp.float32), 'encoder_hidden_states': jax.random.normal(ks[1], (B, Skv, cdim), jnp.float32), 'Wq': jax.random.normal(ks[2], (dim, inner), jnp.float32) * s(dim), 'Wk': jax.random.normal(ks[3], (cdim, inner), jnp.float32) * s(cdim), 'Wv': jax.random.normal(ks[4], (cdim, inner), jnp.float32) * s(cdim), 'Wo': jax.random.normal(ks[5], (inner, dim), jnp.float32) * s(inner), 'gq': jnp.ones((D,), jnp.float32), 'gk': jnp.ones((D,), jnp.float32)}
    _L0_xattn_all = _L0_xattn_setup()
    _L0_xattn_in = {k: v for k, v in _L0_xattn_all.items() if k in ('Wq', 'Wk', 'Wv', 'Wo', 'gq', 'gk')}
    del _L0_xattn_all

    def _L0_ffn_setup():
        import jax, jax.numpy as jnp
        import numpy as np
        B, P = (32, 64)
        DIMS = [512, 1024, 1024, 512]
        key = jax.random.key(seed)
        ks = jax.random.split(key, 7)

        def lin(k, fan_out, fan_in):
            s = 1.0 / np.sqrt(fan_in)
            return jax.random.uniform(k, (fan_out, fan_in), jnp.float32, -s, s)
        return {'classifier_input': jax.random.normal(ks[0], (B, P, DIMS[0]), jnp.float32), 'W1': lin(ks[1], DIMS[1], DIMS[0]), 'b1': jax.random.uniform(ks[2], (DIMS[1],), jnp.float32, -0.02, 0.02), 'W2': lin(ks[3], DIMS[2], DIMS[1]), 'b2': jax.random.uniform(ks[4], (DIMS[2],), jnp.float32, -0.02, 0.02), 'W3': lin(ks[5], DIMS[3], DIMS[2]), 'b3': jax.random.uniform(ks[6], (DIMS[3],), jnp.float32, -0.02, 0.02)}
    _L0_ffn_all = _L0_ffn_setup()
    _L0_ffn_in = {k: v for k, v in _L0_ffn_all.items() if k in ('W1', 'b1', 'W2', 'b2', 'W3', 'b3')}
    del _L0_ffn_all

    def _L1_xattn_setup():
        import jax, jax.numpy as jnp
        import numpy as np
        DIM = 512
        CTX_DIM = 256
        N_HEADS = 32
        HEAD_DIM = DIM // N_HEADS
        POS_DIM = 2
        B, N, CTXN = (2, 512, 512)
        ROPE_BASE = 10000.0

        def apply_axial_rope(x, pos):
            b, n, h, d = x.shape
            p = pos.shape[-1]
            dpa = d // p
            half = dpa // 2
            freqs = ROPE_BASE ** (-jnp.arange(half, dtype=x.dtype) / half)
            ang = pos[..., :, None] * freqs
            cos = jnp.cos(ang)[:, :, None, :, :]
            sin = jnp.sin(ang)[:, :, None, :, :]
            xr = x.reshape(b, n, h, p, half, 2)
            x1, x2 = (xr[..., 0], xr[..., 1])
            out = jnp.stack([x1 * cos - x2 * sin, x1 * sin + x2 * cos], axis=-1)
            return out.reshape(b, n, h, d)
        key = jax.random.key(seed)
        ks = jax.random.split(key, 8)
        x = jax.random.normal(ks[0], (B, N, DIM), jnp.float32)
        ctx = jax.random.normal(ks[1], (B, CTXN, CTX_DIM), jnp.float32)
        pos_map = jax.random.uniform(ks[2], (B, N, POS_DIM), jnp.float32)
        ctx_pos_map = jax.random.uniform(ks[3], (B, CTXN, POS_DIM), jnp.float32)
        Wq = jax.random.normal(ks[4], (DIM, DIM), jnp.float32) / np.sqrt(DIM)
        Wkv = jax.random.normal(ks[5], (CTX_DIM, 2 * DIM), jnp.float32) / np.sqrt(CTX_DIM)
        Wout = jax.random.normal(ks[6], (DIM, DIM), jnp.float32) / np.sqrt(DIM)
        bout = jnp.zeros((DIM,), jnp.float32)
        return {'x': x, 'ctx': ctx, 'pos_map': pos_map, 'ctx_pos_map': ctx_pos_map, 'Wq': Wq, 'Wkv': Wkv, 'Wout': Wout, 'bout': bout}
    _L1_xattn_all = _L1_xattn_setup()
    _L1_xattn_in = {k: v for k, v in _L1_xattn_all.items() if k in ('Wq', 'Wkv', 'Wout', 'bout')}
    del _L1_xattn_all

    def _L1_ffn_setup():
        import jax, jax.numpy as jnp
        import numpy as np
        HIDDEN = 512
        INTER = 2048
        RETRIEVAL = 128
        NUM_EXPERTS = 1024
        NUM_KEYS = 64
        TOP_K = 8
        B, S = (4, 512)
        key = jax.random.key(seed)
        ks = jax.random.split(key, 8)
        sc = 0.02
        return {'hidden_states': jax.random.normal(ks[0], (B, S, HIDDEN), jnp.float32), 'W_q': jax.random.normal(ks[1], (HIDDEN, RETRIEVAL), jnp.float32) * sc, 'keys': jax.random.normal(ks[2], (2, RETRIEVAL // 2, NUM_KEYS), jnp.float32) * sc, 'down_embed': jax.random.normal(ks[3], (NUM_EXPERTS, HIDDEN), jnp.float32) * sc, 'up_embed': jax.random.normal(ks[4], (NUM_EXPERTS, HIDDEN), jnp.float32) * sc, 'gate_w': jax.random.normal(ks[5], (HIDDEN, INTER), jnp.float32) * sc, 'up_w': jax.random.normal(ks[6], (HIDDEN, INTER), jnp.float32) * sc, 'down_w': jax.random.normal(ks[7], (INTER, HIDDEN), jnp.float32) * sc}
    _L1_ffn_all = _L1_ffn_setup()
    _L1_ffn_in = {k: v for k, v in _L1_ffn_all.items() if k in ('W_q', 'keys', 'down_embed', 'up_embed', 'gate_w', 'up_w', 'down_w')}
    del _L1_ffn_all
    return {'x': x, 'ctx_1024': ctx_1024, 'fside_BxSx2_0': fside_BxSx2_0, 'L0_xattn_Wq': _L0_xattn_in['Wq'], 'L0_xattn_Wk': _L0_xattn_in['Wk'], 'L0_xattn_Wv': _L0_xattn_in['Wv'], 'L0_xattn_Wo': _L0_xattn_in['Wo'], 'L0_xattn_gq': _L0_xattn_in['gq'], 'L0_xattn_gk': _L0_xattn_in['gk'], 'L0_ffn_W1': _L0_ffn_in['W1'], 'L0_ffn_b1': _L0_ffn_in['b1'], 'L0_ffn_W2': _L0_ffn_in['W2'], 'L0_ffn_b2': _L0_ffn_in['b2'], 'L0_ffn_W3': _L0_ffn_in['W3'], 'L0_ffn_b3': _L0_ffn_in['b3'], 'L1_xattn_Wq': _L1_xattn_in['Wq'], 'L1_xattn_Wkv': _L1_xattn_in['Wkv'], 'L1_xattn_Wout': _L1_xattn_in['Wout'], 'L1_xattn_bout': _L1_xattn_in['bout'], 'L1_ffn_W_q': _L1_ffn_in['W_q'], 'L1_ffn_keys': _L1_ffn_in['keys'], 'L1_ffn_down_embed': _L1_ffn_in['down_embed'], 'L1_ffn_up_embed': _L1_ffn_in['up_embed'], 'L1_ffn_gate_w': _L1_ffn_in['gate_w'], 'L1_ffn_up_w': _L1_ffn_in['up_w'], 'L1_ffn_down_w': _L1_ffn_in['down_w']}

def reference(x, ctx_1024, fside_BxSx2_0, L0_xattn_Wq, L0_xattn_Wk, L0_xattn_Wv, L0_xattn_Wo, L0_xattn_gq, L0_xattn_gk, L0_ffn_W1, L0_ffn_b1, L0_ffn_W2, L0_ffn_b2, L0_ffn_W3, L0_ffn_b3, L1_xattn_Wq, L1_xattn_Wkv, L1_xattn_Wout, L1_xattn_bout, L1_ffn_W_q, L1_ffn_keys, L1_ffn_down_embed, L1_ffn_up_embed, L1_ffn_gate_w, L1_ffn_up_w, L1_ffn_down_w):
    import jax
    import jax.numpy as jnp

    def _L0_xattn_ref(hidden_states, encoder_hidden_states, Wq, Wk, Wv, Wo, gq, gk):
        import jax, jax.numpy as jnp
        import numpy as np
        EPS = 1e-05

        def rmsnorm(x, g, eps=EPS):
            var = jnp.mean(jnp.square(x), axis=-1, keepdims=True)
            return x * jax.lax.rsqrt(var + eps) * g
        B, Sq, _ = hidden_states.shape
        Skv = encoder_hidden_states.shape[1]
        D = gq.shape[0]
        H = Wq.shape[1] // D
        scale = 1.0 / np.sqrt(D)
        q = (hidden_states @ Wq).reshape(B, Sq, H, D)
        k = (encoder_hidden_states @ Wk).reshape(B, Skv, H, D)
        v = (encoder_hidden_states @ Wv).reshape(B, Skv, H, D)
        q = rmsnorm(q, gq)
        k = rmsnorm(k, gk)
        scores = jnp.einsum('bqhd,bkhd->bhqk', q, k) * scale
        attn = jax.nn.softmax(scores, axis=-1)
        out = jnp.einsum('bhqk,bkhd->bqhd', attn, v)
        out = out.reshape(B, Sq, H * D)
        return out @ Wo

    def _L0_ffn_ref(classifier_input, W1, b1, W2, b2, W3, b3):
        import jax, jax.numpy as jnp
        import numpy as np
        B, P = (32, 64)
        DIMS = [512, 1024, 1024, 512]
        x = classifier_input
        x = jax.nn.relu(jnp.einsum('bpd,hd->bph', x, W1) + b1)
        x = jax.nn.relu(jnp.einsum('bpd,hd->bph', x, W2) + b2)
        out = jnp.einsum('bpd,od->bpo', x, W3) + b3
        return out

    def _L1_xattn_ref(x, ctx, pos_map, ctx_pos_map, Wq, Wkv, Wout, bout):
        import jax, jax.numpy as jnp
        import numpy as np
        DIM = 512
        CTX_DIM = 256
        N_HEADS = 32
        HEAD_DIM = DIM // N_HEADS
        POS_DIM = 2
        B, N, CTXN = (2, 512, 512)
        ROPE_BASE = 10000.0

        def apply_axial_rope(x, pos):
            b, n, h, d = x.shape
            p = pos.shape[-1]
            dpa = d // p
            half = dpa // 2
            freqs = ROPE_BASE ** (-jnp.arange(half, dtype=x.dtype) / half)
            ang = pos[..., :, None] * freqs
            cos = jnp.cos(ang)[:, :, None, :, :]
            sin = jnp.sin(ang)[:, :, None, :, :]
            xr = x.reshape(b, n, h, p, half, 2)
            x1, x2 = (xr[..., 0], xr[..., 1])
            out = jnp.stack([x1 * cos - x2 * sin, x1 * sin + x2 * cos], axis=-1)
            return out.reshape(b, n, h, d)
        b, n, _ = x.shape
        ctx_n = ctx.shape[1]
        q = (x @ Wq).reshape(b, n, N_HEADS, HEAD_DIM)
        k, v = jnp.split(ctx @ Wkv, 2, axis=-1)
        k = k.reshape(b, ctx_n, N_HEADS, HEAD_DIM)
        v = v.reshape(b, ctx_n, N_HEADS, HEAD_DIM)
        q = apply_axial_rope(q, pos_map)
        k = apply_axial_rope(k, ctx_pos_map)
        scale = 1.0 / np.sqrt(HEAD_DIM).astype(np.float32)
        logits = jnp.einsum('bqhd,bkhd->bhqk', q, k) * scale
        w = jax.nn.softmax(logits, axis=-1)
        attn = jnp.einsum('bhqk,bkhd->bqhd', w, v)
        attn = attn.reshape(b, n, N_HEADS * HEAD_DIM)
        return attn @ Wout + bout

    def _L1_ffn_ref(hidden_states, W_q, keys, down_embed, up_embed, gate_w, up_w, down_w):
        import jax, jax.numpy as jnp
        import numpy as np
        HIDDEN = 512
        INTER = 2048
        RETRIEVAL = 128
        NUM_EXPERTS = 1024
        NUM_KEYS = 64
        TOP_K = 8
        B, S = (4, 512)
        b, s, h = hidden_states.shape
        n = b * s
        queries = (hidden_states @ W_q).reshape(2, n, RETRIEVAL // 2)
        routing = jnp.einsum('tnd,tdk->tnk', queries, keys)
        scores2, idx2 = jax.lax.top_k(routing, TOP_K)
        sx, sy = (scores2[0], scores2[1])
        ix, iy = (idx2[0], idx2[1])
        all_scores = (sx[:, :, None] + sy[:, None, :]).reshape(n, TOP_K * TOP_K)
        all_idx = (ix[:, :, None] * NUM_KEYS + iy[:, None, :]).reshape(n, TOP_K * TOP_K)
        scores, pk = jax.lax.top_k(all_scores, TOP_K)
        indices = jnp.take_along_axis(all_idx, pk, axis=-1)
        de = down_embed[indices]
        ue = up_embed[indices]
        x = hidden_states.reshape(n, h)
        ew = jnp.einsum('nh,nkh->nk', x, de)
        ew = jax.nn.silu(ew) * jax.nn.softmax(scores, axis=-1)
        experts_states = jnp.einsum('nk,nkh->nh', ew, ue).reshape(b, s, h)
        mlp = jax.nn.silu(x @ gate_w) * (x @ up_w) @ down_w
        return mlp.reshape(b, s, h) + experts_states
    x = x + _L0_xattn_ref(_layernorm(x, axis=-1), ctx_1024, L0_xattn_Wq, L0_xattn_Wk, L0_xattn_Wv, L0_xattn_Wo, L0_xattn_gq, L0_xattn_gk)
    x = x + _L0_ffn_ref(_layernorm(x, axis=-1), L0_ffn_W1, L0_ffn_b1, L0_ffn_W2, L0_ffn_b2, L0_ffn_W3, L0_ffn_b3)
    x = x + _L1_xattn_ref(_layernorm(x, axis=-1), ctx_1024, fside_BxSx2_0, fside_BxSx2_0, L1_xattn_Wq, L1_xattn_Wkv, L1_xattn_Wout, L1_xattn_bout)
    x = x + _L1_ffn_ref(_layernorm(x, axis=-1), L1_ffn_W_q, L1_ffn_keys, L1_ffn_down_embed, L1_ffn_up_embed, L1_ffn_gate_w, L1_ffn_up_w, L1_ffn_down_w)
    return x

_drawn_inputs = setup_inputs


def setup_inputs(seed=0):
    import zlib

    import numpy as np

    out = dict(_drawn_inputs(seed))
    spreads = {'L0_xattn_gq': (1.0, 0.2), 'L0_xattn_gk': (1.0, 0.2), 'L1_xattn_bout': (0.0, 0.1)}
    factors = {'L0_ffn_b1': 34.51,
     'L0_ffn_b2': 8.0,
     'L0_ffn_b3': 6.01,
     'L1_ffn_W_q': 8.0,
     'L1_ffn_keys': 8.0,
     'L1_ffn_down_embed': 8.0,
     'L1_ffn_up_embed': 8.0}
    for name, (base, spread) in spreads.items():
        noise = np.random.default_rng([zlib.crc32(name.encode()), seed]).standard_normal(out[name].shape)
        drawn = base * np.exp(spread * noise) if base else spread * noise
        out[name] = jnp.asarray(drawn.astype(out[name].dtype))
    for name, factor in factors.items():
        out[name] = (out[name] * factor).astype(out[name].dtype)
    return out
```

```python
from contextlib import ExitStack

import concourse.bass as bass
from concourse import mybir

ALU = mybir.AluOpType
ACT = mybir.ActivationFunctionType
AX = mybir.AxisListType
F32 = mybir.dt.float32
F32R = mybir.dt.float32r
I32 = mybir.dt.int32
U32 = mybir.dt.uint32

P = 128
T = 2048
NB = 16
DM = 512
KD = DM // P
CD = 256
KC = CD // P
EPS = 1e-5
RSQRT_MAGIC = 0x5F3759DF


def part_products(parts_a, parts_b):
    (ah, al), (bh, bl) = parts_a, parts_b
    return ((ah, bh), (ah, bl), (al, bh))


def product(pe, out, pairs, first=True, last=True):
    terms = [t for a, b in pairs for t in part_products(a, b)]
    for n, (st, mv) in enumerate(terms):
        mm = pe.matmul(out, st, mv, start=first and n == 0, stop=last and n == len(terms) - 1)
    return mm


def rsqrt_steps(dve, then, out, v, t_int, t_a):
    then(dve.tensor_scalar(t_int, v.bitcast(I32), 1, None, ALU.logical_shift_right))
    then(dve.tensor_scalar(out.bitcast(I32), t_int, -1.0, float(RSQRT_MAGIC), ALU.mult, ALU.add))
    for _ in range(3):
        then(dve.tensor_tensor(t_a, out, out, ALU.mult))
        then(dve.scalar_tensor_tensor(t_a, t_a, -0.5, v, ALU.mult, ALU.mult))
        then(dve.scalar_tensor_tensor(out, t_a, 1.5, out, ALU.add, ALU.mult))


def l0_attention(nc, sb, sem, bank, ident, x, ctxT, wq, wk, wv, wo, gq, gk, x1):
    H, D, HALF, G = 16, 128, 8, 4
    W = HALF * D
    STEPS = 2 * NB

    def parts(name, shape):
        return sb(name + "_hi", shape, F32R), sb(name + "_lo", shape, F32R)

    wqp, wkp, wvp, wop = parts("wq", [P, KD, W]), parts("wk", [P, KC, W]), parts("wv", [P, KC, W]), parts("wo", [P, HALF, DM])
    stage = [sb(f"stage{i}", [P, 2048], F32) for i in range(2)]
    xres = sb("xres", [P, NB, DM], F32)
    x_in = sb("x_in", [P, DM], F32)
    xn = sb("xn", [P, DM], F32)
    xTp = parts("xT", [P, KD, P])
    ctx_in = sb("ctx_in", [P, KC, P], F32)
    ctxp = parts("ctx", [P, KC, P])
    q_sb = [sb(f"q_sb{g}", [P, G * D], F32) for g in range(2)]
    k_sb = [sb(f"k_sb{g}", [P, G * D], F32) for g in range(2)]
    v_sb = [sb(f"v_sb{g}", [P, G * D], F32) for g in range(2)]
    qT_sb = sb("qT_sb", [P, G * P], F32)
    kT_sb = sb("kT_sb", [P, G * P], F32)
    junk = sb("junk", [P, 2 * G, P], mybir.dt.bfloat16)
    prob = [sb(f"prob{g}", [P, G, P], F32) for g in range(2)]
    pT_sb = sb("pT_sb", [P, G * P], F32)
    oTp = [parts(f"oT{g}", [P, G, P]) for g in range(2)]
    bn = sb("bn", [P, 6], F32)
    mv = sb("mv", [P, 2], F32)
    rs_ln = sb("rs_ln", [P, 3], F32)
    gqk = sb("gqk", [P, 3], F32)
    ssq = [sb(f"ssq{g}", [P, 2, G], F32) for g in range(2)]
    rms = [sb(f"rms{g}", [P, 4, 2 * G], F32) for g in range(2)]
    mx = [sb(f"mx{g}", [P, 2, G], F32) for g in range(2)]
    den = [sb(f"den{g}", [P, 2, G], F32) for g in range(2)]

    names = """x_loaded ctx_loaded xres_loaded g_loaded gqk_ready xn_ready xT_turned xT_hi xT_lo ctx_hi ctx_split
        w_hi w_staged0 w_staged1 w_cut qkv_weights o_weights stored s_turn y_ready y_added""".split()
    names += [f"{n}{g}" for g in range(2) for n in """q_made k_made v_made q_copied k_copied v_copied squared
        rms_ready k_normed q_turned k_turned qT_copied kT_copied scored bias_ready exped normed p_turned pT_copied
        mixed oT_hi oT_lo""".split()]
    S = {n: sem("a_" + n) for n in names}

    def at(n, s):
        return S[n], s + 1

    block = nc.Block()
    with block:
        @block.sync
        def _(sp):
            sp.dma_start(x_in[:], x[0:P, :]).then_inc(S["x_loaded"], 16)
            sp.dma_start(ctx_in[:], ctxT[:, :, 0:P]).then_inc(S["ctx_loaded"], 16)
            sp.dma_start(gqk[:, 0:1], gq).then_inc(S["g_loaded"], 16)
            sp.dma_start(gqk[:, 1:2], gk).then_inc(S["g_loaded"], 16)
            sp.dma_start(xres[:], x.rearrange("(b p) d -> p b d", p=P)).then_inc(S["xres_loaded"], 16)

            def step(s, last=False, final=False):
                if not last:
                    row = sp.snap(((s + 1) % NB) * P)
                    sp.wait_ge(S["ctx_split"], s + 1)
                    sp.wait_ge(S["xn_ready"], s + 1)
                    sp.dma_start(x_in[:], x[bass.ds(row, P), :]).then_inc(S["x_loaded"], 16)
                    sp.dma_start(ctx_in[:], ctxT[:, :, bass.ds(row, P)]).then_inc(S["ctx_loaded"], 16)
                if final:
                    row, col = sp.snap((s - NB) * P), sp.snap((s - NB) * DM)
                    sp.wait_ge(S["y_added"], s + 1)
                    sp.dma_start(x1[bass.ds(row, P), :], xres[:].rearrange("p b d -> p (b d)")[:, bass.ds(col, DM)]).then_inc(S["stored"], 16)

            with sp.Fori(0, NB) as s:
                step(s)
            with sp.Fori(NB, STEPS - 1) as s:
                step(s, final=True)
            step(STEPS - 1, last=True, final=True)
            sp.wait_ge(S["stored"], 16 * NB)

        @block.gpsimd
        def _(pool):
            CUT = 2048
            def pieces(h):
                q = wq[h].rearrange("(k p) w -> p k w", p=P)
                k = wk[h].rearrange("(k p) w -> p k w", p=P)
                v = wv[h].rearrange("(k p) w -> p k w", p=P)
                o = wo[h].rearrange("(k p) w -> p k w", p=P)
                return [(q[:, 0:2], wqp, 0, None), (q[:, 2:4], wqp, 1, None), (k, wkp, 0, None),
                        (v, wvp, 0, "qkv_weights"), (o[:, 0:4], wop, 0, None), (o[:, 4:8], wop, 1, "o_weights")]

            def fetch(h, n):
                src = pieces(h)[n][0]
                if h or n >= 2:
                    pool.wait_ge(S["w_cut"], 6 * h + n - 1)
                pool.dma_start(stage[n % 2][:], src).then_inc(S[f"w_staged{n % 2}"], 16)

            def cut(h, n):
                _, (hi, lo), c, done = pieces(h)[n]
                hi = hi[:].rearrange("p k w -> p (k w)")[:, c * CUT:(c + 1) * CUT]
                lo = lo[:].rearrange("p k w -> p (k w)")[:, c * CUT:(c + 1) * CUT]
                pool.wait_ge(S[f"w_staged{n % 2}"], 16 * (3 * h + n // 2 + 1))
                if h and n == 0:
                    pool.wait_ge(*at("v_made1", NB - 1))
                if h and n == 4:
                    pool.wait_ge(*at("y_ready", NB - 1))
                pool.tensor_copy(hi, stage[n % 2][:]).then_inc(S["w_hi"], 1)
                pool.wait_ge(S["w_hi"], 6 * h + n + 1)
                pool.tensor_tensor(lo, stage[n % 2][:], hi, ALU.subtract).then_inc(S["w_cut"], 1)
                if done:
                    pool.wait_ge(S["w_cut"], 6 * h + n + 1)
                    pool.sem_inc(S[done], NB)

            def split_ctx(s):
                pool.wait_ge(*at("ctx_hi", s))
                pool.tensor_tensor(ctxp[1][:], ctx_in[:], ctxp[0][:], ALU.subtract).then_inc(S["ctx_split"], 1)

            def norm_k(s, g):
                pool.wait_ge(*at(f"rms_ready{g}", s))
                k3 = k_sb[g][:].rearrange("p (h d) -> p h d", h=G)
                pool.tensor_tensor(k3, k3, rms[g][:, 0, G:2 * G].unsqueeze(2).to_broadcast([P, G, D]),
                                   ALU.mult).then_inc(S[f"k_normed{g}"], 1)

            def step(s, last=False):
                norm_k(s, 0)
                norm_k(s, 1)
                if not last:
                    split_ctx(s + 1)

            split_ctx(0)
            fetch(0, 0)
            for n in range(6):
                if n < 5:
                    fetch(0, n + 1)
                cut(0, n)
            with pool.Fori(0, NB) as s:
                step(s)
            fetch(1, 0)
            for n in range(6):
                if n < 5:
                    fetch(1, n + 1)
                cut(1, n)
            with pool.Fori(NB, STEPS - 1) as s:
                step(s)
            step(STEPS - 1, last=True)

        @block.tensor
        def _(pe):
            def turn(out_bank, src, what, eng_sem):
                for j in range(4):
                    t = pe.transpose(bank[out_bank][:, j * P:(j + 1) * P], src[:, j * P:(j + 1) * P], ident[:])
                t.then_inc(S[what], 1)

            def turn_x(s, first=False):
                pe.wait_ge(*at("xn_ready", s))
                if not first:
                    pe.wait_ge(*at("kT_copied0", s - 1))
                turn(6, xn, "xT_turned", None)

            def project(s, g, what, b, act, kt, wp):
                cols = slice(g * G * D, (g + 1) * G * D)
                pairs = [((act[0][:, k, :], act[1][:, k, :]), (wp[0][:, k, cols], wp[1][:, k, cols])) for k in range(kt)]
                product(pe, bank[b][:], pairs).then_inc(S[f"{what}_made{g}"], 1)

            def queries(s, g, first=False):
                if g == 0:
                    pe.wait_ge(*at("xT_lo", s))
                    pe.wait_ge(S["qkv_weights"], s + 1)
                    if not first:
                        pe.wait_ge(*at("exped0", s - 1))
                else:
                    if not first:
                        pe.wait_ge(*at("oT_lo1", s - 1))
                project(s, g, "q", (0, 4)[g], xTp, KD, wqp)

            def keys(s, g, first=False):
                if g == 0:
                    pe.wait_ge(*at("ctx_split", s))
                    if not first:
                        pe.wait_ge(*at("kT_copied1", s - 1))
                else:
                    if not first:
                        pe.wait_ge(*at("oT_lo0", s - 1))
                project(s, g, "k", (3, 7)[g], ctxp, KC, wkp)

            def values(s, g, first=False):
                if g == 0:
                    if not first:
                        pe.wait_ge(*at("pT_copied0", s - 1))
                else:
                    if not first:
                        pe.wait_ge(*at("y_added", s - 1))
                project(s, g, "v", (5, 1)[g], ctxp, KC, wvp)

            def turn_q(s, g, first=False):
                pe.wait_ge(*at(f"q_copied{g}", s))
                if g == 0:
                    pe.wait_ge(*at("v_copied0", s))
                elif not first:
                    pe.wait_ge(*at("pT_copied1", s - 1))
                turn((5, 2)[g], q_sb[g], f"q_turned{g}", None)

            def turn_k(s, g):
                pe.wait_ge(*at(f"k_normed{g}", s))
                pe.wait_ge(*(at("xT_lo", s) if g == 0 else at("k_copied0", s)))
                turn((6, 3)[g], k_sb[g], f"k_turned{g}", None)

            def score(s, g):
                pe.wait_ge(*at(f"qT_copied{g}", s))
                pe.wait_ge(*at(f"kT_copied{g}", s))
                pe.wait_ge(*at(("q_copied0", "q_copied1")[g], s))
                for j in range(G):
                    c = slice(j * P, (j + 1) * P)
                    mm = pe.matmul(bank[(0, 4)[g]][:, c], qT_sb[:, c], kT_sb[:, c], start=True, stop=True)
                mm.then_inc(S[f"scored{g}"], 1)

            def turn_p(s, g):
                pe.wait_ge(*at(f"normed{g}", s))
                pe.wait_ge(*at(("qT_copied0", "qT_copied1")[g], s))
                turn((5, 2)[g], prob[g][:].rearrange("p h k -> p (h k)"), f"p_turned{g}", None)

            def mix(s, g):
                pe.wait_ge(*at(f"pT_copied{g}", s))
                pe.wait_ge(*at(f"v_copied{g}", s))
                pe.wait_ge(*at(("k_copied1", "exped1")[g], s))
                for j in range(G):
                    c = slice(j * P, (j + 1) * P)
                    mm = pe.matmul(bank[(7, 4)[g]][:, c], v_sb[g][:, c], pT_sb[:, c], start=True, stop=True)
                mm.then_inc(S[f"mixed{g}"], 1)

            def output(s, g):
                pe.wait_ge(*at(f"oT_lo{g}", s))
                if g == 0:
                    pe.wait_ge(S["o_weights"], s + 1)
                    pe.wait_ge(*at("v_copied1", s))
                pairs = [((oTp[g][0][:, j, :], oTp[g][1][:, j, :]), (wop[0][:, g * G + j, :], wop[1][:, g * G + j, :]))
                         for j in range(G)]
                mm = product(pe, bank[1][:], pairs, first=g == 0, last=g == 1)
                if g == 1:
                    mm.then_inc(S["y_ready"], 1)

            def step(s, first=False, last=False):
                queries(s, 1, first)
                turn_q(s, 0)
                turn_k(s, 0)
                keys(s, 1, first)
                score(s, 0)
                values(s, 1, first)
                turn_q(s, 1, first)
                turn_k(s, 1)
                score(s, 1)
                turn_p(s, 0)
                if not last:
                    turn_x(s + 1)
                mix(s, 0)
                if not last:
                    queries(s + 1, 0)
                output(s, 0)
                turn_p(s, 1)
                if not last:
                    keys(s + 1, 0)
                mix(s, 1)
                if not last:
                    values(s + 1, 0)
                output(s, 1)

            turn_x(0, True)
            queries(0, 0, True)
            keys(0, 0, True)
            values(0, 0, True)
            step(0, first=True)
            with pe.Fori(1, STEPS - 1) as s:
                step(s)
            step(STEPS - 1, last=True)

        @block.scalar
        def _(act):
            def split_xT(s):
                act.wait_ge(*at("xT_turned", s))
                if not isinstance(s, int) or s > 0:
                    act.wait_ge(*at("q_made1", s - 1))
                act.activation(xTp[0][:].rearrange("p k t -> p (k t)"), bank[6][:], ACT.Copy).then_inc(S["xT_hi"], 1)

            def split_ctx(s):
                act.wait_ge(S["ctx_loaded"], 16 * (s + 1))
                act.activation(ctxp[0][:], ctx_in[:], ACT.Copy).then_inc(S["ctx_hi"], 1)

            def square(s, g, kind):
                src = (q_sb, k_sb)[kind][g]
                act.wait_ge(*at(("q_copied", "k_copied")[kind] + str(g), s))
                if g == 0 and kind == 0 and (not isinstance(s, int) or s > 0):
                    act.wait_ge(*at("rms_ready1", s - 1))
                if g == 1 and kind == 0:
                    act.wait_ge(*at("rms_ready0", s))
                for j in range(G):
                    a = act.activation(junk[:, kind * G + j, :], src[:, j * D:(j + 1) * D], ACT.Square,
                                       accum_out=ssq[g][:, kind, j:j + 1])
                a.then_inc(S[f"squared{g}"], 1)

            def copy_v(s, g):
                act.wait_ge(*at(f"v_made{g}", s))
                if not isinstance(s, int) or s > 0:
                    act.wait_ge(*at(f"mixed{g}", s - 1))
                act.activation(v_sb[g][:], bank[(5, 1)[g]][:], ACT.Copy).then_inc(S[f"v_copied{g}"], 1)

            def copy_qT(s, g):
                act.wait_ge(*at(f"q_turned{g}", s))
                if g == 1:
                    act.wait_ge(*at("scored0", s))
                act.activation(qT_sb[:], bank[(5, 2)[g]][:], ACT.Copy).then_inc(S[f"qT_copied{g}"], 1)

            def exps(s, g):
                act.wait_ge(*at(f"bias_ready{g}", s))
                for j in range(G):
                    a = act.activation(prob[g][:, j, :], bank[(0, 4)[g]][:, j * P:(j + 1) * P], ACT.Exp,
                                       bias=mx[g][:, 1, j:j + 1], scale=rms[g][:, 1, j:j + 1],
                                       accum_out=den[g][:, 0, j:j + 1])
                a.then_inc(S[f"exped{g}"], 1)

            def split_o(s, g):
                act.wait_ge(*at(f"mixed{g}", s))
                if g == 0 and (not isinstance(s, int) or s > 0):
                    act.wait_ge(*at("y_ready", s - 1))
                act.activation(oTp[g][0][:].rearrange("p h q -> p (h q)"), bank[(7, 4)[g]][:], ACT.Copy
                               ).then_inc(S[f"oT_hi{g}"], 1)

            def step(s, last=False):
                copy_qT(s, 0)
                square(s, 1, 0)
                square(s, 1, 1)
                exps(s, 0)
                copy_v(s, 1)
                if not last:
                    split_ctx(s + 1)
                copy_qT(s, 1)
                exps(s, 1)
                if not last:
                    split_xT(s + 1)
                split_o(s, 0)
                if not last:
                    square(s + 1, 0, 0)
                split_o(s, 1)
                if not last:
                    square(s + 1, 0, 1)
                    copy_v(s + 1, 0)

            split_ctx(0)
            split_xT(0)
            square(0, 0, 0)
            square(0, 0, 1)
            copy_v(0, 0)
            step(0)
            with act.Fori(1, STEPS - 1) as s:
                step(s)
            step(STEPS - 1, last=True)

        @block.vector
        def _(dve):
            chain = [0]

            def then(ins):
                chain[0] = chain[0] + 1
                ins.then_inc(S["s_turn"], 1)
                dve.wait_ge(S["s_turn"], chain[0])

            def chain_from_zero():
                dve.sem_clear(S["s_turn"])
                chain[0] = 0

            def layer_norm(s):
                dve.wait_ge(S["x_loaded"], 16 * (s + 1))
                if not isinstance(s, int) or s > 0:
                    dve.wait_ge(*at("xT_turned", s - 1))
                then(dve.bn_stats(bn[:], x_in[:]))
                then(dve.bn_aggr(mv[:], bn[:]))
                then(dve.tensor_scalar(rs_ln[:, 2:3], mv[:, 1:2], EPS, None, ALU.add))
                rsqrt_steps(dve, then, rs_ln[:, 0:1], rs_ln[:, 2:3], bn[:, 0:1].bitcast(I32), rs_ln[:, 1:2])
                dve.tensor_scalar(xn[:], x_in[:], mv[:, 0:1], rs_ln[:, 0:1], ALU.subtract, ALU.mult
                                  ).then_inc(S["xn_ready"], 1)

            def split_xT(s):
                dve.wait_ge(*at("xT_hi", s))
                hi, lo = (p[:].rearrange("p k t -> p (k t)") for p in xTp)
                dve.tensor_tensor(lo, bank[6][:], hi, ALU.subtract).then_inc(S["xT_lo"], 1)

            def copy_q(s, g):
                dve.wait_ge(*at(f"q_made{g}", s))
                dve.tensor_copy(q_sb[g][:], bank[(0, 4)[g]][:]).then_inc(S[f"q_copied{g}"], 1)

            def copy_k(s, g):
                dve.wait_ge(*at(f"k_made{g}", s))
                dve.tensor_copy(k_sb[g][:], bank[(3, 7)[g]][:]).then_inc(S[f"k_copied{g}"], 1)

            def means(s, g):
                dve.wait_ge(S[f"squared{g}"], 2 * (s + 1))
                r = rms[g]
                both = ssq[g][:].rearrange("p a h -> p (a h)")
                then(dve.tensor_scalar(r[:, 2, :], both, 1.0 / D, EPS, ALU.mult, ALU.add))
                rsqrt_steps(dve, then, r[:, 0, :], r[:, 2, :], r[:, 3, :].bitcast(I32), r[:, 1, :])
                dve.tensor_scalar(r[:, 1, 0:G], r[:, 0, 0:G], float(D) ** -0.5, None, ALU.mult
                                  ).then_inc(S[f"rms_ready{g}"], 1)

            def copy_kT(s, g):
                dve.wait_ge(*at(f"k_turned{g}", s))
                if g == 1:
                    dve.wait_ge(*at("scored0", s))
                dve.tensor_scalar(kT_sb[:], bank[(6, 3)[g]][:], gqk[:, 2:3], None, ALU.mult
                                  ).then_inc(S[f"kT_copied{g}"], 1)

            def maxima(s, g):
                dve.wait_ge(*at(f"scored{g}", s))
                then(dve.tensor_reduce(mx[g][:, 0, :], bank[(0, 4)[g]][:].rearrange("p (h k) -> p h k", h=G),
                                       AX.X, ALU.max))
                dve.scalar_tensor_tensor(mx[g][:, 1, :], mx[g][:, 0, :], -1.0, rms[g][:, 1, 0:G], ALU.mult, ALU.mult
                                         ).then_inc(S[f"bias_ready{g}"], 1)

            def normalise(s, g):
                dve.wait_ge(*at(f"exped{g}", s))
                then(dve.reciprocal(den[g][:, 1, :], den[g][:, 0, :]))
                dve.tensor_tensor(prob[g][:], prob[g][:], den[g][:, 1, :].unsqueeze(2).to_broadcast([P, G, P]),
                                  ALU.mult).then_inc(S[f"normed{g}"], 1)

            def copy_pT(s, g):
                dve.wait_ge(*at(f"p_turned{g}", s))
                if g == 1:
                    dve.wait_ge(*at("mixed0", s))
                dve.tensor_copy(pT_sb[:], bank[(5, 2)[g]][:]).then_inc(S[f"pT_copied{g}"], 1)

            def split_o(s, g):
                dve.wait_ge(*at(f"oT_hi{g}", s))
                hi, lo = (p[:].rearrange("p h q -> p (h q)") for p in oTp[g])
                dve.tensor_tensor(lo, bank[(7, 4)[g]][:], hi, ALU.subtract).then_inc(S[f"oT_lo{g}"], 1)

            def add_y(s):
                dve.wait_ge(*at("y_ready", s))
                r = xres[:].rearrange("p b d -> p (b d)")[:, bass.ds((s % NB) * DM, DM)]
                dve.tensor_tensor(r, r, bank[1][:], ALU.add).then_inc(S["y_added"], 1)

            def step(s, last=False):
                chain_from_zero()
                copy_q(s, 1)
                copy_kT(s, 0)
                copy_k(s, 1)
                maxima(s, 0)
                means(s, 1)
                if not last:
                    layer_norm(s + 1)
                normalise(s, 0)
                copy_kT(s, 1)
                maxima(s, 1)
                copy_pT(s, 0)
                if not last:
                    split_xT(s + 1)
                split_o(s, 0)
                if not last:
                    copy_q(s + 1, 0)
                normalise(s, 1)
                copy_pT(s, 1)
                if not last:
                    copy_k(s + 1, 0)
                split_o(s, 1)
                if not last:
                    means(s + 1, 0)
                add_y(s)

            dve.wait_ge(S["g_loaded"], 32)
            then(dve.tensor_tensor(gqk[:, 2:3], gqk[:, 0:1], gqk[:, 1:2], ALU.mult))
            layer_norm(0)
            split_xT(0)
            copy_q(0, 0)
            copy_k(0, 0)
            means(0, 0)
            dve.wait_ge(S["xres_loaded"], 16)
            step(0)
            with dve.Fori(1, STEPS - 1) as s:
                step(s)
            step(STEPS - 1, last=True)


def l0_ffn(nc, sb, sem, bank, ident, x1, w1, b1, w2, b2, w3, b3, x2):
    HID = 1024
    KH = HID // P
    CH = 512
    NC, TPC = T // CH, CH // P

    def parts(name, shape):
        return sb("f_" + name + "_hi", shape, F32R), sb("f_" + name + "_lo", shape, F32R)

    w1p, w2p, w3p = parts("w1", [P, KD, HID]), parts("w2", [P, KH, HID]), parts("w3", [P, KH, DM])
    PIECE = 1024
    stage = [sb(f"f_stage{i}", [P, PIECE], F32) for i in range(2)]
    x_in = [sb(f"f_x_in{i}", [P, DM], F32) for i in range(2)]
    res = [sb(f"f_res{i}", [P, DM], F32) for i in range(2)]
    xTp = parts("xT", [P, KD, CH])
    h1p = parts("h1", [P, KH, CH])
    h2p = [parts(f"h2{i}", [P, CH]) for i in range(2)]
    relu = [sb(f"f_relu{i}", [P, CH], F32) for i in range(2)]
    b12 = sb("f_b12", [P, 2, KH], F32)
    b3r = sb("f_b3", [P, DM], F32)
    bn = sb("f_bn", [P, 6], F32)
    mv = sb("f_mv", [P, 2], F32)
    rs = sb("f_rs", [P, 3], F32)

    names = """x_loaded0 x_loaded1 res_loaded0 res_loaded1 b_loaded w_staged0 w_staged1 w_hi w_cut xn_ready
        xT_turned xT_hi xT_lo h_made h_hi relu_ready h_lo y_made bias_added y_added stored0 stored1 s_turn""".split()
    S = {n: sem("f_" + n) for n in names}
    NP1, NP2, NP3 = KD * HID // PIECE, KH * HID // PIECE, KH * DM // PIECE
    HB = (4, 5, 6)

    def tile_of(c, j):
        return TPC * c + j + 1

    def hid(c, layer, m):
        return 2 * KH * c + layer * KH + m + 1

    block = nc.Block()
    with block:
        @block.sync
        def _(sp):
            def load_x(c, j):
                row = sp.snap((c * TPC + j) * P)
                if not (isinstance(c, int) and c == 0 and j < 2):
                    sp.wait_ge(S["xT_turned"], tile_of(c, j) - 2)
                sp.dma_start(x_in[j % 2][:], x1[bass.ds(row, P), :]).then_inc(S[f"x_loaded{j % 2}"], 16)

            def load_res(c, j, first):
                row = sp.snap((c * TPC + j) * P)
                if not (first and j < 2):
                    sp.wait_ge(S[f"stored{j % 2}"], 16 * (2 * c + j // 2))
                sp.dma_start(res[j % 2][:], x1[bass.ds(row, P), :]).then_inc(S[f"res_loaded{j % 2}"], 16)

            def store(c, j):
                row = sp.snap((c * TPC + j) * P)
                sp.wait_ge(S["y_added"], tile_of(c, j))
                sp.dma_start(x2[bass.ds(row, P), :], res[j % 2][:]).then_inc(S[f"stored{j % 2}"], 16)

            def step(c, first=False, last=False):
                load_res(c, 0, first)
                load_res(c, 1, first)
                if not last:
                    for j in range(TPC):
                        load_x(c + 1, j)
                for j in range(TPC):
                    store(c, j)
                    if j + 2 < TPC:
                        load_res(c, j + 2, first)

            load_x(0, 0)
            load_x(0, 1)
            sp.dma_start(b12[:, 0, :], b1).then_inc(S["b_loaded"], 16)
            sp.dma_start(b12[:, 1, :], b2).then_inc(S["b_loaded"], 16)
            sp.dma_start(b3r[:], b3).then_inc(S["b_loaded"], 16)
            load_x(0, 2)
            load_x(0, 3)
            step(0, first=True)
            with sp.Fori(1, NC - 1) as c:
                step(c)
            step(NC - 1, last=True)
            for i in range(2):
                sp.wait_ge(S[f"stored{i}"], 16 * 2 * NC)

        @block.gpsimd
        def _(pool):
            pieces = [(w1.rearrange("(k p) h -> p k h", p=P)[:, :, 256 * n:256 * (n + 1)],
                       [w[:, :, 256 * n:256 * (n + 1)] for w in w1p], KD) for n in range(NP1)]
            pieces += [(w2.rearrange("(k p) h -> p k h", p=P)[:, :, P * n:P * (n + 1)],
                        [w[:, :, P * n:P * (n + 1)] for w in w2p], KH) for n in range(NP2)]
            pieces += [(w3.rearrange("(k p) h -> p k h", p=P)[:, 2 * n:2 * n + 2, :],
                        [w[:, 2 * n:2 * n + 2, :] for w in w3p], 2) for n in range(NP3)]

            def fetch(n):
                if n >= 2:
                    pool.wait_ge(S["w_cut"], n - 1)
                pool.dma_start(stage[n % 2][:].rearrange("p (k c) -> p k c", k=pieces[n][2]), pieces[n][0]
                               ).then_inc(S[f"w_staged{n % 2}"], 16)

            fetch(0)
            for n in range(len(pieces)):
                if n + 1 < len(pieces):
                    fetch(n + 1)
                _, (hi, lo), k = pieces[n]
                raw = stage[n % 2][:].rearrange("p (k c) -> p k c", k=k)
                pool.wait_ge(S[f"w_staged{n % 2}"], 16 * (n // 2 + 1))
                pool.tensor_copy(hi, raw).then_inc(S["w_hi"], 1)
                pool.wait_ge(S["w_hi"], n + 1)
                pool.tensor_tensor(lo, raw, hi, ALU.subtract).then_inc(S["w_cut"], 1)

            def add_bias(c, j):
                pool.wait_ge(S[f"res_loaded{j % 2}"], 16 * (2 * c + j // 2 + 1))
                pool.tensor_tensor(res[j % 2][:], res[j % 2][:], b3r[:], ALU.add).then_inc(S["bias_added"], 1)

            pool.wait_ge(S["b_loaded"], 48)
            with pool.Fori(0, NC) as c:
                for j in range(TPC):
                    add_bias(c, j)

        @block.tensor
        def _(pe):
            def turn_x(c, j):
                pe.wait_ge(S["xn_ready"], tile_of(c, j))
                if not (isinstance(c, int) and c == 0 and j == 0):
                    pe.wait_ge(S["xT_lo"], tile_of(c, j) - 1)
                for k in range(KD):
                    t = pe.transpose(bank[7][:, k * P:(k + 1) * P], x_in[j % 2][:, k * P:(k + 1) * P], ident[:])
                t.then_inc(S["xT_turned"], 1)

            def hidden1(c, m, first):
                pe.wait_ge(S["w_cut"], m // 2 + 1)
                if m == 0:
                    pe.wait_ge(S["xT_lo"], tile_of(c, TPC - 1))
                if not (first and m < 3):
                    pe.wait_ge(S["relu_ready"], hid(c, 0, m) - 3)
                cols = slice(m * P, (m + 1) * P)
                pairs = [((w1p[0][:, k, cols], w1p[1][:, k, cols]), (xTp[0][:, k, :], xTp[1][:, k, :])) for k in range(KD)]
                product(pe, bank[HB[m % 3]][:], pairs).then_inc(S["h_made"], 1)

            def hidden2(c, m):
                pe.wait_ge(S["w_cut"], NP1 + m + 1)
                if m == 0:
                    pe.wait_ge(S["h_lo"], hid(c, 0, KH - 1))
                pe.wait_ge(S["relu_ready"], hid(c, 1, m) - 3)
                cols = slice(m * P, (m + 1) * P)
                pairs = [((w2p[0][:, k, cols], w2p[1][:, k, cols]), (h1p[0][:, k, :], h1p[1][:, k, :])) for k in range(KH)]
                product(pe, bank[HB[(KH + m) % 3]][:], pairs).then_inc(S["h_made"], 1)

            def output(c, m, first):
                pe.wait_ge(S["w_cut"], NP1 + NP2 + m // 2 + 1)
                pe.wait_ge(S["h_lo"], hid(c, 1, m))
                if m == 0 and not first:
                    pe.wait_ge(S["y_added"], tile_of(c, 0) - 1)
                for j in range(TPC):
                    rows = slice(j * P, (j + 1) * P)
                    mm = product(pe, bank[j][:], [((h2p[m % 2][0][:, rows], h2p[m % 2][1][:, rows]),
                                                   (w3p[0][:, m, :], w3p[1][:, m, :]))], first=m == 0, last=m == KH - 1)
                mm.then_inc(S["y_made"], 1)

            def step(c, first=False, last=False):
                for m in range(KH):
                    hidden1(c, m, first)
                for m in range(KH):
                    hidden2(c, m)
                    if m > 0:
                        output(c, m - 1, first)
                    if not last and 1 <= m <= TPC:
                        turn_x(c + 1, m - 1)
                output(c, KH - 1, first)

            for j in range(TPC):
                turn_x(0, j)
            step(0, first=True)
            with pe.Fori(1, NC - 1) as c:
                step(c)
            step(NC - 1, last=True)

        @block.scalar
        def _(act):
            def split_x(c, j):
                act.wait_ge(S["xT_turned"], tile_of(c, j))
                out = xTp[0][:, :, j * P:(j + 1) * P]
                act.activation(out, bank[7][:].rearrange("p (k t) -> p k t", k=KD), ACT.Copy).then_inc(S["xT_hi"], 1)

            def hidden(c, layer, m):
                act.wait_ge(S["h_made"], hid(c, layer, m))
                if layer == 1 and m >= 2:
                    act.wait_ge(S["y_made"], KH * c + m - 1)
                out = h1p[0][:, m, :] if layer == 0 else h2p[m % 2][0][:]
                act.activation(out, bank[HB[(layer * KH + m) % 3]][:], ACT.Relu, bias=b12[:, layer, m:m + 1]
                               ).then_inc(S["h_hi"], 1)

            def step(c, last=False):
                for m in range(KH):
                    hidden(c, 0, m)
                for m in range(KH):
                    hidden(c, 1, m)
                    if not last and 1 <= m <= TPC:
                        split_x(c + 1, m - 1)

            act.wait_ge(S["b_loaded"], 48)
            for j in range(TPC):
                split_x(0, j)
            with act.Fori(0, NC - 1) as c:
                step(c)
            step(NC - 1, last=True)

        @block.vector
        def _(dve):
            chain = [0]

            def then(ins):
                chain[0] = chain[0] + 1
                ins.then_inc(S["s_turn"], 1)
                dve.wait_ge(S["s_turn"], chain[0])

            def layer_norm(c, j):
                x = x_in[j % 2]
                dve.wait_ge(S[f"x_loaded{j % 2}"], 16 * (2 * c + j // 2 + 1))
                then(dve.bn_stats(bn[:], x[:]))
                then(dve.bn_aggr(mv[:], bn[:]))
                then(dve.tensor_scalar(rs[:, 2:3], mv[:, 1:2], EPS, None, ALU.add))
                rsqrt_steps(dve, then, rs[:, 0:1], rs[:, 2:3], bn[:, 0:1].bitcast(I32), rs[:, 1:2])
                dve.tensor_scalar(x[:], x[:], mv[:, 0:1], rs[:, 0:1], ALU.subtract, ALU.mult).then_inc(S["xn_ready"], 1)

            def split_x(c, j):
                dve.wait_ge(S["xT_hi"], tile_of(c, j))
                hi, lo = (p[:, :, j * P:(j + 1) * P] for p in xTp)
                dve.tensor_tensor(lo, bank[7][:].rearrange("p (k t) -> p k t", k=KD), hi, ALU.subtract
                                  ).then_inc(S["xT_lo"], 1)

            def hidden(c, layer, m, first=False):
                if not (first and layer == 0 and m < 2):
                    dve.wait_ge(S["h_lo"], hid(c, layer, m) - 2)
                hi, lo = (p[:, m, :] if layer == 0 else p[:] for p in (h1p if layer == 0 else h2p[m % 2]))
                dve.wait_ge(S["h_hi"], hid(c, layer, m))
                dve.tensor_scalar(relu[m % 2][:], bank[HB[(layer * KH + m) % 3]][:], b12[:, layer, m:m + 1], 0.0, ALU.add, ALU.max
                                  ).then_inc(S["relu_ready"], 1)
                dve.wait_ge(S["relu_ready"], hid(c, layer, m))
                dve.tensor_tensor(lo, relu[m % 2][:], hi, ALU.subtract).then_inc(S["h_lo"], 1)

            def add_y(c, j):
                dve.wait_ge(S["bias_added"], tile_of(c, j))
                dve.wait_ge(S["y_made"], KH * (c + 1))
                dve.tensor_tensor(res[j % 2][:], res[j % 2][:], bank[j][:], ALU.add).then_inc(S["y_added"], 1)

            def step(c, first=False, last=False):
                dve.sem_clear(S["s_turn"])
                chain[0] = 0
                for m in range(KH):
                    hidden(c, 0, m, first)
                for m in range(KH):
                    if not last and m < 2:
                        layer_norm(c + 1, m)
                    hidden(c, 1, m)
                    if not last and 1 <= m <= TPC:
                        split_x(c + 1, m - 1)
                        if m + 1 < TPC:
                            layer_norm(c + 1, m + 1)
                for j in range(TPC):
                    add_y(c, j)

            for j in range(2):
                layer_norm(0, j)
            for j in range(TPC):
                split_x(0, j)
                if j + 2 < TPC:
                    layer_norm(0, j + 2)
            dve.wait_ge(S["b_loaded"], 48)
            step(0, first=True)
            with dve.Fori(1, NC - 1) as c:
                step(c)
            step(NC - 1, last=True)


def l1_attention(nc, sb, sem, bank, ident, x2, ctxT, pos, wq, wkv, wo, bo, x3):
    H, D, PAD = 32, 16, 32
    HH = H // 2
    ROT = D // 2
    BASE = 10000.0
    TWO_PI = (6.28125, 0.0019350051879882812, 3.0199158198e-07)
    ROUND = 1.5 * 2.0 ** 23

    def parts(name, shape):
        return sb("l_" + name + "_hi", shape, F32R), sb("l_" + name + "_lo", shape, F32R)

    wqp, wkvp, wop = parts("wq", [P, KD, DM]), parts("wkv", [P, KC, 2 * DM]), parts("wo", [P, KD, DM])
    stage = [sb(f"l_stage{i}", [P, 2048], F32) for i in range(3)]
    x_in, xn, res, bor = (sb("l_" + n, [P, DM], F32) for n in ("x_in", "xn", "res", "bo"))
    xTp = parts("xT", [P, KD, P])
    ctx_in = sb("l_ctx_in", [P, KC, P], F32)
    ctxp = parts("ctx", [P, KC, P])
    pos_sb = sb("l_pos", [P, NB, 2], F32)
    ang = sb("l_ang", [P, 4, NB * ROT], F32)
    cos2 = sb("l_cos2", [P, NB, D], F32)
    sin2 = sb("l_sin2", [P, NB, D], F32)
    cos_now = sb("l_cos_now", [P, D], F32)
    qk = [sb(f"l_qk{i}", [P, H, D], F32) for i in range(2)]
    rotA = [sb(f"l_rotA{i}", [P, H, D], F32) for i in range(2)]
    rotB = [sb(f"l_rotB{i}", [P, H, D], F32) for i in range(2)]
    roped = [sb(f"l_roped{i}", [P, H * PAD], F32) for i in range(2)]
    qkT = [sb(f"l_qkT{i}", [P, 8, P], F32) for i in range(2)]
    v_sb = sb("l_v", [P, DM], F32)
    prob = [sb(f"l_prob{i}", [P, HH, P], F32) for i in range(2)]
    pT = [sb(f"l_pT{i}", [P, 4, P], F32) for i in range(2)]
    mx = sb("l_mx", [P, 2, 2, HH], F32)
    den = sb("l_den", [P, 2, H], F32)
    o_sb = sb("l_o", [P, DM], F32)
    oTp = parts("oT", [P, KD, P])
    bn, mv, rs = sb("l_bn", [P, 6], F32), sb("l_mv", [P, 2], F32), sb("l_rs", [P, 3], F32)

    names = """x_loaded ctx_loaded res_loaded b_loaded w_staged0 w_staged1 w_staged2 w_hi w_cut pad_zero
        xn_ready xT_turned xT_hi xT_lo ctx_hi ctx_lo q_made k_made v_made q_copied k_copied v_copied rotA0 rotA1 rotB0
        rotB1 roped0 roped1 t0_turned t1_turned q0_in k0_in q1_in k1_in scored0 scored1 bias0 bias1 exped
        p_turned pT_in mixed o_ready oT_turned oT_hi oT_lo y_made bo_added y_added stored s_turn a_turn cos_here""".split()
    S = {n: sem("l_" + n) for n in names}

    def at(n, s):
        return S[n], s + 1

    def later(s):
        return not isinstance(s, int) or s > 0

    block = nc.Block()
    with block:
        @block.sync
        def _(sp):
            sp.dma_start(x_in[:], x2[0:P, :]).then_inc(S["x_loaded"], 16)
            sp.dma_start(ctx_in[:], ctxT[:, :, 0:P]).then_inc(S["ctx_loaded"], 16)
            sp.dma_start(pos_sb[:], pos.rearrange("(b p) c -> p b c", p=P)).then_inc(S["b_loaded"], 16)
            sp.dma_start(bor[:], bo).then_inc(S["b_loaded"], 16)

            def step(s, last=False):
                row = sp.snap(s * P)
                if later(s):
                    sp.wait_ge(S["stored"], 16 * s)
                sp.dma_start(res[:], x2[bass.ds(row, P), :]).then_inc(S["res_loaded"], 16)
                if not last:
                    after = sp.snap((s + 1) * P)
                    sp.wait_ge(S["ctx_lo"], s + 1)
                    sp.wait_ge(S["xn_ready"], s + 1)
                    sp.dma_start(x_in[:], x2[bass.ds(after, P), :]).then_inc(S["x_loaded"], 16)
                    sp.dma_start(ctx_in[:], ctxT[:, :, bass.ds(after, P)]).then_inc(S["ctx_loaded"], 16)
                store_row = sp.snap(s * P)
                sp.wait_ge(S["y_added"], s + 1)
                sp.dma_start(x3[bass.ds(store_row, P), :], res[:]).then_inc(S["stored"], 16)

            step(0)
            with sp.Fori(1, NB - 1) as s:
                step(s)
            step(NB - 1, last=True)
            sp.wait_ge(S["stored"], 16 * NB)

        @block.gpsimd
        def _(pool):
            weights = [(wq.rearrange("(k p) w -> p k w", p=P), wqp), (wkv.rearrange("(k p) w -> p k w", p=P), wkvp),
                       (wo.rearrange("(k p) w -> p k w", p=P), wop)]
            for n, (src, _) in enumerate(weights):
                pool.dma_start(stage[n][:], src).then_inc(S[f"w_staged{n}"], 16)
            for i in range(2):
                pool.memset(roped[i][:], 0.0).then_inc(S["pad_zero"], 1)
            for n, (_, (hi, lo)) in enumerate(weights):
                flat = [w[:].rearrange("p k w -> p (k w)") for w in (hi, lo)]
                pool.wait_ge(S["w_hi"], n + 1)
                pool.tensor_tensor(flat[1], stage[n][:], flat[0], ALU.subtract).then_inc(S["w_cut"], 1)

            def split_ctx(s):
                pool.wait_ge(*at("ctx_hi", s))
                pool.tensor_tensor(ctxp[1][:], ctx_in[:], ctxp[0][:], ALU.subtract).then_inc(S["ctx_lo"], 1)

            def by_cosine(s, i):
                pool.wait_ge(*at(("q_copied", "k_copied")[i], s))
                if later(s):
                    pool.wait_ge(*at(f"roped{i}", s - 1))
                pool.wait_ge(*at("cos_here", s))
                pool.tensor_tensor(rotA[i][:], qk[i][:], cos_now[:].unsqueeze(1).to_broadcast([P, H, D]), ALU.mult).then_inc(S[f"rotA{i}"], 1)

            def add_bias(s):
                pool.wait_ge(S["res_loaded"], 16 * (s + 1))
                pool.tensor_tensor(res[:], res[:], bor[:], ALU.add).then_inc(S["bo_added"], 1)

            split_ctx(0)
            by_cosine(0, 0)
            by_cosine(0, 1)
            pool.wait_ge(S["b_loaded"], 32)
            with pool.Fori(0, NB - 1) as s:
                add_bias(s)
                split_ctx(s + 1)
                by_cosine(s + 1, 0)
                by_cosine(s + 1, 1)
            add_bias(NB - 1)

        @block.tensor
        def _(pe):
            def turn_x(s):
                pe.wait_ge(*at("xn_ready", s))
                if later(s):
                    pe.wait_ge(*at("q1_in", s - 1))
                for k in range(KD):
                    t = pe.transpose(bank[7][:, k * P:(k + 1) * P], xn[:, k * P:(k + 1) * P], ident[:])
                t.then_inc(S["xT_turned"], 1)

            def project(b, act, kt, wp, cols, what):
                pairs = [((act[0][:, k, :], act[1][:, k, :]), (wp[0][:, k, cols], wp[1][:, k, cols])) for k in range(kt)]
                product(pe, bank[b][:], pairs).then_inc(S[what], 1)

            def queries(s):
                pe.wait_ge(*at("xT_lo", s))
                pe.wait_ge(S["w_cut"], 1)
                project(7, xTp, KD, wqp, slice(0, DM), "q_made")

            def keys(s):
                pe.wait_ge(*at("ctx_lo", s))
                pe.wait_ge(S["w_cut"], 2)
                if later(s):
                    pe.wait_ge(S["exped"], 8 * s)
                project(0, ctxp, KC, wkvp, slice(0, DM), "k_made")

            def values(s):
                project(2, ctxp, KC, wkvp, slice(DM, 2 * DM), "v_made")

            def turn_qk(s, half):
                qb, kb = ((4, 5), (7, 6))[half]
                if half == 0:
                    pe.wait_ge(*at("roped0", s))
                    if later(s):
                        pe.wait_ge(S["pT_in"], 8 * s)
                else:
                    if later(s):
                        pe.wait_ge(*at("o_ready", s - 1))
                    pe.wait_ge(*at("q_copied", s))
                for i, b in ((0, qb), (1, kb)):
                    if i == 1 and half == 0:
                        pe.wait_ge(*at("roped1", s))
                    for j in range(4):
                        c = (4 * half + j) * P
                        t = pe.transpose(bank[b][:, j * P:(j + 1) * P], roped[i][:, c:c + P], ident[:])
                t.then_inc(S[f"t{half}_turned"], 1)

            def score(s, half):
                pe.wait_ge(*at(f"q{half}_in", s))
                pe.wait_ge(*at(f"k{half}_in", s))
                if half == 0:
                    pe.wait_ge(*at("k_copied", s))
                    pe.wait_ge(*at("v_copied", s))
                    if later(s):
                        pe.wait_ge(*at("y_added", s - 1))
                else:
                    pe.wait_ge(S["exped"], 8 * s + 4)
                for t in range(4):
                    for i in range(4):
                        rows = slice(PAD * i, PAD * i + D)
                        mm = pe.matmul(bank[i][:, t * P:(t + 1) * P], qkT[0][rows, 4 * half + t, :],
                                       qkT[1][rows, 4 * half + t, :], start=True, stop=True)
                mm.then_inc(S[f"scored{half}"], 1)

            def turn_p(s, g):
                pe.wait_ge(S["exped"], 8 * s + g + 1)
                if g == 0:
                    pe.wait_ge(*at("q0_in", s))
                    pe.wait_ge(*at("k0_in", s))
                if g >= 2:
                    pe.wait_ge(S["pT_in"], 8 * s + g - 1)
                for j in range(4):
                    t = pe.transpose(bank[4 + g % 2][:, j * P:(j + 1) * P], prob[g // 4][:, 4 * (g % 4) + j, :], ident[:])
                t.then_inc(S["p_turned"], 1)

            def mix(s, g):
                pe.wait_ge(S["pT_in"], 8 * s + g + 1)
                if g == 0:
                    pe.wait_ge(*at("k1_in", s))
                for j in range(4):
                    c = slice((4 * g + j) * D, (4 * g + j + 1) * D)
                    mm = pe.matmul(bank[6][:, c], pT[g % 2][:, j, :], v_sb[:, c], start=True, stop=True)
                mm.then_inc(S["mixed"], 1)

            def turn_o(s):
                pe.wait_ge(*at("o_ready", s))
                for k in range(KD):
                    t = pe.transpose(bank[1][:, k * P:(k + 1) * P], o_sb[:, k * P:(k + 1) * P], ident[:])
                t.then_inc(S["oT_turned"], 1)

            def output(s):
                pe.wait_ge(*at("oT_lo", s))
                pe.wait_ge(S["w_cut"], 3)
                project(3, oTp, KD, wop, slice(0, DM), "y_made")

            def step(s, last=False):
                score(s, 0)
                turn_qk(s, 1)
                if not last:
                    turn_x(s + 1)
                turn_p(s, 0)
                for g in range(4):
                    if g + 1 < 4:
                        turn_p(s, g + 1)
                    mix(s, g)
                score(s, 1)
                if not last:
                    queries(s + 1)
                turn_p(s, 4)
                for g in range(4, 8):
                    if g + 1 < 8:
                        turn_p(s, g + 1)
                    mix(s, g)
                if not last:
                    keys(s + 1)
                    values(s + 1)
                turn_o(s)
                output(s)
                if not last:
                    turn_qk(s + 1, 0)

            turn_x(0)
            queries(0)
            keys(0)
            values(0)
            turn_qk(0, 0)
            step(0)
            with pe.Fori(1, NB - 1) as s:
                step(s)
            step(NB - 1, last=True)

        @block.scalar
        def _(act):
            def split_ctx(s):
                act.wait_ge(S["ctx_loaded"], 16 * (s + 1))
                if later(s):
                    act.wait_ge(*at("v_made", s - 1))
                act.activation(ctxp[0][:], ctx_in[:], ACT.Copy).then_inc(S["ctx_hi"], 1)

            def split_x(s):
                act.wait_ge(*at("xT_turned", s))
                act.activation(xTp[0][:].rearrange("p k t -> p (k t)"), bank[7][:], ACT.Copy).then_inc(S["xT_hi"], 1)

            def copy_qk(s, i):
                act.wait_ge(*at(("q_made", "k_made")[i], s))
                if later(s):
                    act.wait_ge(*at(f"roped{i}", s - 1))
                act.activation(qk[i][:].rearrange("p h d -> p (h d)"), bank[(7, 0)[i]][:], ACT.Copy
                               ).then_inc(S[("q_copied", "k_copied")[i]], 1)

            def copy_v(s):
                act.wait_ge(*at("v_made", s))
                if later(s):
                    act.wait_ge(S["mixed"], 8 * s)
                act.activation(v_sb[:], bank[2][:], ACT.Copy).then_inc(S["v_copied"], 1)

            def queries_in(s, half):
                act.wait_ge(*at(f"t{half}_turned", s))
                act.activation(qkT[0][:, 4 * half:4 * half + 4, :].rearrange("p k t -> p (k t)"), bank[(4, 7)[half]][:],
                               ACT.Copy).then_inc(S[f"q{half}_in"], 1)

            def exps(s, half):
                act.wait_ge(*at(f"bias{half}", s))
                if later(s):
                    act.wait_ge(S["p_turned"], 8 * s - 4 + 4 * half)
                for t in range(4):
                    for i in range(4):
                        h = 4 * t + i
                        a = act.activation(prob[half][:, h, :], bank[i][:, t * P:(t + 1) * P], ACT.Exp,
                                           bias=mx[:, half, 1, h:h + 1], scale=D ** -0.5,
                                           accum_out=den[:, 0, HH * half + h:HH * half + h + 1])
                    a.then_inc(S["exped"], 1)

            def split_o(s):
                act.wait_ge(*at("oT_turned", s))
                act.activation(oTp[0][:].rearrange("p k t -> p (k t)"), bank[1][:], ACT.Copy).then_inc(S["oT_hi"], 1)

            def step(s, last=False):
                queries_in(s, 1)
                exps(s, 0)
                if not last:
                    split_ctx(s + 1)
                    split_x(s + 1)
                    copy_qk(s + 1, 0)
                exps(s, 1)
                if not last:
                    copy_qk(s + 1, 1)
                    copy_v(s + 1)
                split_o(s)
                if not last:
                    queries_in(s + 1, 0)

            for n, (hi, _) in enumerate((wqp, wkvp, wop)):
                act.wait_ge(S[f"w_staged{n}"], 16)
                act.activation(hi[:].rearrange("p k w -> p (k w)"), stage[n][:], ACT.Copy).then_inc(S["w_hi"], 1)
            act.wait_ge(S["a_turn"], 1)
            act.activation(ang[:, 2, :], ang[:, 0, :], ACT.Sin).then_inc(S["a_turn"], 1)
            act.activation(ang[:, 3, :], ang[:, 1, :], ACT.Sin).then_inc(S["a_turn"], 1)
            split_ctx(0)
            split_x(0)
            copy_qk(0, 0)
            copy_qk(0, 1)
            copy_v(0)
            queries_in(0, 0)
            step(0)
            with act.Fori(1, NB - 1) as s:
                step(s)
            step(NB - 1, last=True)

        @block.vector
        def _(dve):
            chain = [0]

            def then(ins):
                chain[0] = chain[0] + 1
                ins.then_inc(S["s_turn"], 1)
                dve.wait_ge(S["s_turn"], chain[0])

            def tables():
                a = ang[:, 0, :].rearrange("p (b c j) -> p b c j", b=NB, c=2)
                dve.wait_ge(S["b_loaded"], 32)
                for j in range(ROT // 2):
                    last = dve.tensor_scalar(a[:, :, :, j], pos_sb[:], BASE ** (-j / (ROT // 2)), None, ALU.mult)
                    then(last)
                turns, t = ang[:, 1, :], ang[:, 0, :]
                then(dve.tensor_scalar(turns, t, 1.0 / 6.283185307179586, ROUND, ALU.mult, ALU.add))
                then(dve.tensor_scalar(turns, turns, -ROUND, None, ALU.add))
                for part in TWO_PI:
                    then(dve.scalar_tensor_tensor(t, turns, -part, t, ALU.mult, ALU.add))
                then(dve.tensor_scalar(t, t, 3.1415925, -3.1415925, ALU.min, ALU.max))
                then(dve.scalar_tensor_tensor(turns, t, -1.0, t, ALU.mult, ALU.max))
                dve.tensor_scalar(turns, turns, -1.0, 1.5707963267948966, ALU.mult, ALU.add).then_inc(S["a_turn"], 1)
                dve.wait_ge(S["a_turn"], 3)
                for k in range(2):
                    pair = lambda x: x[:].rearrange("p b (r k) -> p (b r) k", k=2)[:, :, k]
                    then(dve.tensor_copy(pair(cos2), ang[:, 3, :]))
                    then(dve.tensor_scalar(pair(sin2), ang[:, 2, :], (-1.0, 1.0)[k], None, ALU.mult))

            def layer_norm(s):
                dve.wait_ge(S["x_loaded"], 16 * (s + 1))
                if later(s):
                    dve.wait_ge(*at("xT_turned", s - 1))
                then(dve.bn_stats(bn[:], x_in[:]))
                then(dve.bn_aggr(mv[:], bn[:]))
                then(dve.tensor_scalar(rs[:, 2:3], mv[:, 1:2], EPS, None, ALU.add))
                rsqrt_steps(dve, then, rs[:, 0:1], rs[:, 2:3], bn[:, 0:1].bitcast(I32), rs[:, 1:2])
                dve.tensor_scalar(xn[:], x_in[:], mv[:, 0:1], rs[:, 0:1], ALU.subtract, ALU.mult).then_inc(S["xn_ready"], 1)

            def copy_cosines(s):
                if later(s):
                    dve.wait_ge(*at("rotA1", s - 1))
                dve.tensor_copy(cos_now[:], cos2[:].rearrange("p b d -> p (b d)")[:, bass.ds(s * D, D)]
                                ).then_inc(S["cos_here"], 1)

            def split_x(s):
                dve.wait_ge(*at("xT_hi", s))
                hi, lo = (p[:].rearrange("p k t -> p (k t)") for p in xTp)
                dve.tensor_tensor(lo, bank[7][:], hi, ALU.subtract).then_inc(S["xT_lo"], 1)

            def by_sine(s, i):
                dve.wait_ge(*at(("q_copied", "k_copied")[i], s))
                t = sin2[:].rearrange("p b d -> p (b d)")[:, bass.ds(s * D, D)].rearrange("p (r k) -> p r k", k=2)
                for k in range(2):
                    out = rotB[i][:].rearrange("p h (r k) -> p h r k", k=2)[:, :, :, k]
                    src = qk[i][:].rearrange("p h (r k) -> p h r k", k=2)[:, :, :, 1 - k]
                    dve.tensor_tensor(out, src, t[:, :, k].unsqueeze(1).to_broadcast([P, H, ROT]), ALU.mult
                                      ).then_inc(S[f"rotB{i}"], 1)
                if later(s):
                    dve.wait_ge(*at("t1_turned", s - 1))
                dve.wait_ge(S[f"rotB{i}"], 2 * (s + 1))
                dve.wait_ge(*at(f"rotA{i}", s))
                out = roped[i][:].rearrange("p (h w) -> p h w", w=PAD)[:, :, 0:D]
                dve.tensor_tensor(out, rotA[i][:], rotB[i][:], ALU.add).then_inc(S[f"roped{i}"], 1)

            def keys_in(s, half):
                dve.wait_ge(*at(f"t{half}_turned", s))
                dve.tensor_copy(qkT[1][:, 4 * half:4 * half + 4, :].rearrange("p k t -> p (k t)"), bank[(5, 6)[half]][:]
                                ).then_inc(S[f"k{half}_in"], 1)

            def maxima(s, half):
                dve.wait_ge(*at(f"scored{half}", s))
                m = mx[:, half, 0, :].rearrange("p (t i) -> p t i", i=4)
                for i in range(4):
                    r = dve.tensor_reduce(m[:, :, i], bank[i][:].rearrange("p (t k) -> p t k", t=4), AX.X, ALU.max)
                then(r)
                dve.tensor_scalar(mx[:, half, 1, :], mx[:, half, 0, :], -(D ** -0.5), None, ALU.mult
                                  ).then_inc(S[f"bias{half}"], 1)

            def probs_in(s, g):
                dve.wait_ge(S["p_turned"], 8 * s + g + 1)
                if g >= 2 or later(s):
                    dve.wait_ge(S["mixed"], 8 * s + g - 1)
                dve.tensor_copy(pT[g % 2][:].rearrange("p h k -> p (h k)"), bank[4 + g % 2][:]).then_inc(S["pT_in"], 1)

            def normalise(s):
                dve.wait_ge(S["mixed"], 8 * (s + 1))
                then(dve.reciprocal(den[:, 1, :], den[:, 0, :]))
                dve.tensor_tensor(o_sb[:].rearrange("p (h d) -> p h d", h=H), bank[6][:].rearrange("p (h d) -> p h d", h=H),
                                  den[:, 1, :].unsqueeze(2).to_broadcast([P, H, D]), ALU.mult).then_inc(S["o_ready"], 1)

            def split_o(s):
                dve.wait_ge(*at("oT_hi", s))
                hi, lo = (p[:].rearrange("p k t -> p (k t)") for p in oTp)
                dve.tensor_tensor(lo, bank[1][:], hi, ALU.subtract).then_inc(S["oT_lo"], 1)

            def add_y(s):
                dve.wait_ge(*at("bo_added", s))
                dve.wait_ge(*at("y_made", s))
                dve.tensor_tensor(res[:], res[:], bank[3][:], ALU.add).then_inc(S["y_added"], 1)

            def step(s, last=False):
                dve.sem_clear(S["s_turn"])
                chain[0] = 0
                keys_in(s, 1)
                maxima(s, 0)
                if not last:
                    layer_norm(s + 1)
                    copy_cosines(s + 1)
                for g in range(4):
                    probs_in(s, g)
                if not last:
                    split_x(s + 1)
                maxima(s, 1)
                if not last:
                    by_sine(s + 1, 0)
                for g in range(4, 8):
                    probs_in(s, g)
                normalise(s)
                if not last:
                    by_sine(s + 1, 1)
                split_o(s)
                if not last:
                    keys_in(s + 1, 0)
                add_y(s)

            tables()
            layer_norm(0)
            copy_cosines(0)
            split_x(0)
            dve.wait_ge(S["pad_zero"], 2)
            by_sine(0, 0)
            by_sine(0, 1)
            keys_in(0, 0)
            step(0)
            with dve.Fori(1, NB - 1) as s:
                step(s)
            step(NB - 1, last=True)


def l1_ffn_front(nc, sb, sem, bank, ident, x3, wq, xT_all, hqT, y):
    def parts(name, shape):
        return sb("r_" + name + "_hi", shape, F32R), sb("r_" + name + "_lo", shape, F32R)

    wqp = parts("wq", [P, KD, P])
    stage = sb("r_stage", [P, KD, P], F32)
    x_in = [sb(f"r_x_in{i}", [P, DM], F32) for i in range(2)]
    xTp = [parts(f"xT{i}", [P, KD, P]) for i in range(2)]
    bn, mv, rs = sb("r_bn", [P, 6], F32), sb("r_mv", [P, 2], F32), sb("r_rs", [P, 3], F32)
    names = """x_loaded0 x_loaded1 y_loaded w_staged w_hi w_cut xn_ready xT_turned xT_hi xT_lo kept0 kept1 q_made q_kept s_turn""".split()
    S = {n: sem("r_" + n) for n in names}

    def nth(t, i, n=1):
        return n * (2 * t + i + 1)

    block = nc.Block()
    with block:
        @block.sync
        def _(sp):
            def load(t, i, first=False):
                row = sp.snap((2 * t + i) * P)
                if not first:
                    sp.wait_ge(S["xT_turned"], nth(t, i) - 2)
                sp.dma_start(x_in[i][:], x3[bass.ds(row, P), :]).then_inc(S[f"x_loaded{i}"], 16)

            load(0, 0, True)
            load(0, 1, True)
            sp.dma_start(stage[:], wq.rearrange("(k p) w -> p k w", p=P)).then_inc(S["w_staged"], 16)
            sp.dma_start(y[:], x3.rearrange("(b p) d -> p b d", p=P)).then_inc(S["y_loaded"], 16)

            def keep(t, i):
                col = sp.snap((2 * t + i) * P)
                sp.wait_ge(S["xT_lo"], nth(t, i))
                for part in range(2):
                    sp.dma_start(xT_all[part].bitcast(F32)[:, :, bass.ds(col, P)], xTp[i][part][:].bitcast(F32)).then_inc(S[f"kept{i}"], 16)

            with sp.Fori(0, NB // 2 - 1) as t:
                for i in range(2):
                    load(t + 1, i)
                    keep(t, i)
            keep(NB // 2 - 1, 0)
            keep(NB // 2 - 1, 1)
            sp.wait_ge(S["kept0"], 16 * NB)
            sp.wait_ge(S["kept1"], 16 * NB)
            sp.wait_ge(S["y_loaded"], 16)

        @block.tensor
        def _(pe):
            def step(t, i, first=False):
                pe.wait_ge(S["xn_ready"], nth(t, i))
                if not first:
                    pe.wait_ge(S["xT_lo"], nth(t, i) - 1)
                for k in range(KD):
                    tr = pe.transpose(bank[0][:, k * P:(k + 1) * P], x_in[i][:, k * P:(k + 1) * P], ident[:])
                tr.then_inc(S["xT_turned"], 1)
                pe.wait_ge(S["w_cut"], 1)
                if not first:
                    pe.wait_ge(S["q_kept"], nth(t, i) - 1)
                pe.wait_ge(S["xT_lo"], nth(t, i))
                pairs = [((wqp[0][:, k, :], wqp[1][:, k, :]), (xTp[i][0][:, k, :], xTp[i][1][:, k, :])) for k in range(KD)]
                product(pe, bank[1][:, 0:P], pairs).then_inc(S["q_made"], 1)

            step(0, 0, True)
            step(0, 1)
            with pe.Fori(1, NB // 2) as t:
                step(t, 0)
                step(t, 1)

        @block.scalar
        def _(act):
            def step(t, i, first=False):
                act.wait_ge(S["xT_turned"], nth(t, i))
                if not first:
                    act.wait_ge(S[f"kept{i}"], 32 * t)
                    act.wait_ge(S["q_made"], nth(t, i) - 2)
                act.activation(xTp[i][0][:].rearrange("p k t -> p (k t)"), bank[0][:], ACT.Copy).then_inc(S["xT_hi"], 1)

            act.wait_ge(S["w_staged"], 16)
            act.activation(wqp[0][:], stage[:], ACT.Copy).then_inc(S["w_hi"], 1)
            step(0, 0, True)
            step(0, 1, True)
            with act.Fori(1, NB // 2) as t:
                step(t, 0)
                step(t, 1)

        @block.gpsimd
        def _(pool):
            pool.wait_ge(S["w_hi"], 1)
            pool.tensor_tensor(wqp[1][:], stage[:], wqp[0][:], ALU.subtract).then_inc(S["w_cut"], 1)

        @block.vector
        def _(dve):
            chain = [0]

            def then(ins):
                chain[0] = chain[0] + 1
                ins.then_inc(S["s_turn"], 1)
                dve.wait_ge(S["s_turn"], chain[0])

            def norm(t, i):
                x = x_in[i]
                dve.wait_ge(S[f"x_loaded{i}"], 16 * (t + 1))
                then(dve.bn_stats(bn[:], x[:]))
                then(dve.bn_aggr(mv[:], bn[:]))
                then(dve.tensor_scalar(rs[:, 2:3], mv[:, 1:2], EPS, None, ALU.add))
                rsqrt_steps(dve, then, rs[:, 0:1], rs[:, 2:3], bn[:, 0:1].bitcast(I32), rs[:, 1:2])
                dve.tensor_scalar(x[:], x[:], mv[:, 0:1], rs[:, 0:1], ALU.subtract, ALU.mult).then_inc(S["xn_ready"], 1)

            def split(t, i):
                dve.wait_ge(S["xT_hi"], nth(t, i))
                hi, lo = (p[:].rearrange("p k t -> p (k t)") for p in xTp[i])
                dve.tensor_tensor(lo, bank[0][:], hi, ALU.subtract).then_inc(S["xT_lo"], 1)

            def keep_q(t, i):
                dve.wait_ge(S["q_made"], nth(t, i))
                dve.tensor_scalar(hqT[:, bass.ds((2 * t + i) * P, P)], bank[1][:, 0:P], 1.0, None, ALU.mult
                                  ).then_inc(S["q_kept"], 1)

            def step(t, last=False):
                dve.sem_clear(S["s_turn"])
                chain[0] = 0
                split(t, 0)
                norm(t, 1)
                keep_q(t, 0)
                split(t, 1)
                if not last:
                    norm(t + 1, 0)
                keep_q(t, 1)

            norm(0, 0)
            with dve.Fori(0, NB // 2 - 1) as t:
                step(t)
            step(NB // 2 - 1, last=True)


def l1_experts(nc, sb, sem, bank, ident, keys, iota, left, deT, ue, xT_all, hqT, y):
    K, NX, NE, TOP = 64, 16, 1024, 8
    KE = NE // P
    LOWEST = -3.0e38

    def parts(name, shape):
        return sb("e_" + name + "_hi", shape, F32R), sb("e_" + name + "_lo", shape, F32R)

    dep, uep = parts("de", [P, KD, NE]), parts("ue", [P, KE, DM])
    stage = [sb(f"e_stage{i}", [P, 1024], F32) for i in range(2)]
    key_sb = sb("e_keys", [P, 2, K], F32)
    iota_sb = sb("e_iota", [P, K], F32)
    left_sb = sb("e_left", [P, TOP], F32)
    xTp = parts("xT", [P, KD, P])
    z = sb("e_z", [P, 2, K, 2], F32)
    r = sb("e_r", [P, 2, K], F32)
    top = sb("e_top", [P, 2, TOP], F32)
    idx = sb("e_idx", [P, 2, TOP], U32)
    idf = sb("e_idf", [P, 2, TOP], F32)
    pairs = sb("e_pairs", [P, 4, TOP, TOP], F32)
    best = sb("e_best", [P, TOP], F32)
    small = sb("e_small", [P, 8, TOP], F32)
    hotx = sb("e_hotx", [P, NX, TOP], F32)
    hoty = sb("e_hoty", [P, K, TOP], F32)
    least = sb("e_least", [P, NX], F32)
    rank = sb("e_rank", [P, K], F32)
    e_all = sb("e_all", [P, 2, K], F32)
    e_top = sb("e_etop", [P, 2, TOP], F32)
    ex = sb("e_ex", [P, NX], F32)
    w = sb("e_w", [P, NX, K], F32)
    g = sb("e_g", [P, NE], F32)
    gTp = parts("gT", [P, KE, P])

    names = """c_loaded w_staged0 w_staged1 w_hi w_cut xT_in z_zero z_ready routed shift_ready exps_ready
        w_ready ew_made silu_ready g_ready g_turned gT_hi gT_lo y_made y_added s_turn hot_ready""".split()
    S = {n: sem("e_" + n) for n in names}

    def at(n, s):
        return S[n], s + 1

    def later(s):
        return not isinstance(s, int) or s > 0

    block = nc.Block()
    with block:
        @block.sync
        def _(sp):
            def load(s):
                col = sp.snap(s * P)
                if later(s):
                    sp.wait_ge(*at("ew_made", s - 1))
                for part in range(2):
                    sp.dma_start(xTp[part][:].bitcast(F32), xT_all[part].bitcast(F32)[:, :, bass.ds(col, P)]).then_inc(S["xT_in"], 16)

            load(0)
            for dst, src in ((key_sb, keys), (iota_sb, iota), (left_sb, left)):
                sp.dma_start(dst[:], src).then_inc(S["c_loaded"], 16)
            with sp.Fori(1, NB) as s:
                load(s)

        @block.gpsimd
        def _(pool):
            pool.memset(z[:], 0.0).then_inc(S["z_zero"], 1)
            src_de = deT.rearrange("(k p) e -> p k e", p=P)
            src_ue = ue.rearrange("(k p) d -> p k d", p=P)
            pieces = [(src_de[:, :, 256 * n:256 * (n + 1)], [x[:, :, 256 * n:256 * (n + 1)] for x in dep], KD) for n in range(4)]
            pieces += [(src_ue[:, 2 * n:2 * n + 2, :], [x[:, 2 * n:2 * n + 2, :] for x in uep], 2) for n in range(4)]

            def fetch(n):
                if n >= 2:
                    pool.wait_ge(S["w_cut"], n - 1)
                pool.dma_start(stage[n % 2][:].rearrange("p (k c) -> p k c", k=pieces[n][2]), pieces[n][0]
                               ).then_inc(S[f"w_staged{n % 2}"], 16)

            fetch(0)
            for n in range(len(pieces)):
                if n + 1 < len(pieces):
                    fetch(n + 1)
                _, (hi, lo), k = pieces[n]
                raw = stage[n % 2][:].rearrange("p (k c) -> p k c", k=k)
                pool.wait_ge(S[f"w_staged{n % 2}"], 16 * (n // 2 + 1))
                pool.tensor_copy(hi, raw).then_inc(S["w_hi"], 1)
                pool.wait_ge(S["w_hi"], n + 1)
                pool.tensor_tensor(lo, raw, hi, ALU.subtract).then_inc(S["w_cut"], 1)

        @block.tensor
        def _(pe):
            def route(s):
                pe.wait_ge(*at("z_ready", s))
                if later(s):
                    pe.wait_ge(*at("shift_ready", s - 1))
                for i in range(2):
                    mm = pe.matmul(bank[5][:, i * K:(i + 1) * K], z[:, i].rearrange("p k e -> p (k e)"), key_sb[:, i, :],
                                   start=True, stop=True)
                mm.then_inc(S["routed"], 1)

            def downs(s, first=False):
                pe.wait_ge(S["xT_in"], 32 * (s + 1))
                if later(s):
                    pe.wait_ge(S["silu_ready"], 2 * s)
                for b in range(2):
                    if first:
                        pe.wait_ge(S["w_cut"], 2 * b + 2)
                    cols = slice(512 * b, 512 * (b + 1))
                    mm = product(pe, bank[b][:], [((xTp[0][:, k, :], xTp[1][:, k, :]), (dep[0][:, k, cols], dep[1][:, k, cols]))
                                                  for k in range(KD)])
                mm.then_inc(S["ew_made"], 1)

            def turn_g(s):
                pe.wait_ge(*at("g_ready", s))
                if later(s):
                    pe.wait_ge(S["gT_lo"], 2 * s)
                for e in range(KE):
                    t = pe.transpose(bank[2 + e // 4][:, (e % 4) * P:(e % 4 + 1) * P], g[:, e * P:(e + 1) * P], ident[:])
                t.then_inc(S["g_turned"], 1)

            def ups(s, first=False):
                pe.wait_ge(S["gT_lo"], 2 * (s + 1))
                if first:
                    pe.wait_ge(S["w_cut"], 8)
                if later(s):
                    pe.wait_ge(*at("y_added", s - 1))
                product(pe, bank[4][:], [((gTp[0][:, e, :], gTp[1][:, e, :]), (uep[0][:, e, :], uep[1][:, e, :]))
                                         for e in range(KE)]).then_inc(S["y_made"], 1)

            def step(s, first=False, last=False):
                if not last:
                    route(s + 1)
                turn_g(s)
                if not last:
                    downs(s + 1)
                ups(s, first)

            pe.wait_ge(S["c_loaded"], 48)
            route(0)
            downs(0, True)
            step(0, first=True)
            with pe.Fori(1, NB - 1) as s:
                step(s)
            step(NB - 1, last=True)

        @block.scalar
        def _(act):
            def exps(s):
                act.wait_ge(*at("shift_ready", s))
                for i in range(2):
                    act.activation(e_all[:, i, :], r[:, i, :], ACT.Exp, bias=small[:, 7, i:i + 1])
                    a = act.activation(e_top[:, i, :], top[:, i, :], ACT.Exp, bias=small[:, 7, i:i + 1])
                a.then_inc(S["exps_ready"], 1)

            def silus(s):
                act.wait_ge(*at("ew_made", s))
                if later(s):
                    act.wait_ge(*at("g_turned", s - 1))
                for b in range(2):
                    act.activation(g[:, 512 * b:512 * (b + 1)], bank[b][:], ACT.Silu).then_inc(S["silu_ready"], 1)

            def split_g(s):
                act.wait_ge(*at("g_turned", s))
                if later(s):
                    act.wait_ge(*at("y_made", s - 1))
                for b in range(2):
                    act.activation(gTp[0][:, 4 * b:4 * b + 4, :].rearrange("p e t -> p (e t)"), bank[2 + b][:], ACT.Copy
                                   ).then_inc(S["gT_hi"], 1)

            def step(s, last=False):
                split_g(s)
                if not last:
                    silus(s + 1)
                    exps(s + 1)

            silus(0)
            exps(0)
            with act.Fori(0, NB - 1) as s:
                step(s)
            step(NB - 1, last=True)

        @block.vector
        def _(dve):
            chain = [0]

            def then(ins):
                chain[0] = chain[0] + 1
                ins.then_inc(S["s_turn"], 1)
                dve.wait_ge(S["s_turn"], chain[0])

            def interleave(s):
                if later(s):
                    dve.wait_ge(*at("routed", s - 1))
                for i in range(2):
                    for e in range(2):
                        rows = slice(K * e, K * (e + 1))
                        last = dve.tensor_scalar(z[rows, i, :, e], hqT[rows, bass.ds(s * K + i * (T // 2), K)], 1.0, None,
                                                 ALU.mult)
                last.then_inc(S["z_ready"], 1)

            def route(s):
                sx, sy = top[:, 0, :], top[:, 1, :]
                sums, rest, chosen, wts = (pairs[:, n] for n in range(4))
                flat = lambda x: x.rearrange("p a b -> p (a b)")
                dve.wait_ge(*at("routed", s))
                if later(s):
                    dve.wait_ge(*at("exps_ready", s - 1))
                then(dve.tensor_copy(r[:], bank[5][:, 0:2 * K].rearrange("p (i k) -> p i k", i=2)))
                for i in range(2):
                    m = dve.max(top[:, i, :], r[:, i, :])
                then(m)
                for i in range(2):
                    dve.max_index(idx[:, i, :], top[:, i, :], r[:, i, :])
                dve.tensor_scalar(small[:, 7, 0:2], top[:, :, 0], -1.0, None, ALU.mult).then_inc(S["shift_ready"], 1)
                then(dve.tensor_tensor(sums, sx.unsqueeze(2).to_broadcast([P, TOP, TOP]),
                                       sy.unsqueeze(1).to_broadcast([P, TOP, TOP]), ALU.add))
                dve.tensor_copy(idf[:], idx[:])
                then(dve.max(best[:], flat(sums)))
                then(dve.match_replace(flat(rest), best[:], flat(sums), LOWEST))
                then(dve.tensor_tensor(flat(chosen), flat(rest), flat(sums), ALU.not_equal))
                dve.tensor_tensor(hoty[:], iota_sb[:].unsqueeze(2).to_broadcast([P, K, TOP]),
                                  idf[:, 1, :].unsqueeze(1).to_broadcast([P, K, TOP]), ALU.is_equal)
                then(dve.tensor_tensor(hotx[:], iota_sb[:, 0:NX].unsqueeze(2).to_broadcast([P, NX, TOP]),
                                       idf[:, 0, :].unsqueeze(1).to_broadcast([P, NX, TOP]), ALU.is_equal))
                dve.tensor_tensor(hoty[:], hoty[:], left_sb[:].unsqueeze(1).to_broadcast([P, K, TOP]), ALU.mult)
                then(dve.tensor_reduce(small[:, 0, :], chosen, AX.X, ALU.add))
                then(dve.tensor_tensor(hotx[:], hotx[:], small[:, 0, :].unsqueeze(1).to_broadcast([P, NX, TOP]), ALU.mult))
                dve.tensor_reduce(rank[:], hoty[:], AX.X, ALU.add)
                then(dve.tensor_reduce(least[:], hotx[:], AX.X, ALU.add))
                then(dve.tensor_scalar(least[:], least[:], -1.0, float(TOP), ALU.mult, ALU.add))
                dve.wait_ge(*at("exps_ready", s))
                dve.tensor_tensor(wts, e_top[:, 0, :].unsqueeze(2).to_broadcast([P, TOP, TOP]),
                                  e_top[:, 1, :].unsqueeze(1).to_broadcast([P, TOP, TOP]), ALU.mult)
                then(dve.tensor_tensor(w[:], rank[:].unsqueeze(1).to_broadcast([P, NX, K]),
                                       least[:].unsqueeze(2).to_broadcast([P, NX, K]), ALU.is_gt))
                then(dve.tensor_tensor(wts, wts, chosen, ALU.mult))
                then(dve.tensor_reduce(small[:, 1, :], wts, AX.X, ALU.add))
                dve.tensor_reduce(small[:, 2, 0:1], small[:, 1, :], AX.X, ALU.add)
                then(dve.scalar_tensor_tensor(small[:, 3, :], idf[:, 0, :], float(NX), small[:, 1, :], ALU.is_ge, ALU.mult))
                dve.tensor_reduce(small[:, 2, 1:2], small[:, 3, :], AX.X, ALU.add)
                then(dve.reciprocal(small[:, 2, 2:3], small[:, 2, 0:1]))
                dve.tensor_tensor(w[:], w[:], e_all[:, 1, :].unsqueeze(1).to_broadcast([P, NX, K]), ALU.mult)
                then(dve.tensor_scalar(ex[:], e_all[:, 0, 0:NX], small[:, 2, 2:3], None, ALU.mult))
                then(dve.tensor_tensor(w[:], w[:], ex[:].unsqueeze(2).to_broadcast([P, NX, K]), ALU.mult))
                last = w[:].rearrange("p a b -> p (a b)")[:, NE - 1:NE]
                dve.scalar_tensor_tensor(last, small[:, 2, 1:2], small[:, 2, 2:3], last, ALU.mult, ALU.add
                                         ).then_inc(S["w_ready"], 1)

            def weight(s):
                dve.wait_ge(S["silu_ready"], 2 * (s + 1))
                dve.wait_ge(*at("w_ready", s))
                dve.tensor_tensor(g[:], g[:], w[:].rearrange("p a b -> p (a b)"), ALU.mult).then_inc(S["g_ready"], 1)

            def split_g(s):
                for b in range(2):
                    dve.wait_ge(S["gT_hi"], 2 * s + b + 1)
                    hi, lo = (x[:, 4 * b:4 * b + 4, :].rearrange("p e t -> p (e t)") for x in gTp)
                    dve.tensor_tensor(lo, bank[2 + b][:], hi, ALU.subtract).then_inc(S["gT_lo"], 1)

            def add_y(s):
                dve.wait_ge(*at("y_made", s))
                row = y[:].rearrange("p b d -> p (b d)")[:, bass.ds(s * DM, DM)]
                dve.tensor_tensor(row, row, bank[4][:], ALU.add).then_inc(S["y_added"], 1)

            def step(s, last=False):
                dve.sem_clear(S["s_turn"])
                chain[0] = 0
                if not last:
                    interleave(s + 1)
                weight(s)
                split_g(s)
                if not last:
                    route(s + 1)
                add_y(s)

            dve.wait_ge(S["z_zero"], 1)
            dve.wait_ge(S["c_loaded"], 48)
            interleave(0)
            route(0)
            with dve.Fori(0, NB - 1) as s:
                step(s)
            step(NB - 1, last=True)


def l1_mlp(nc, sb, sem, bank, gate, up, down, xT_all, y, out):
    INTER = 2048
    J, CH = 2, 512
    PAIRS, NC, TPC = INTER // (J * P), T // CH, CH // P
    W = J * P

    def parts(name, shape):
        return sb("m_" + name + "_hi", shape, F32R), sb("m_" + name + "_lo", shape, F32R)

    NG, ND = KD * W, J * DM
    wp = [parts(f"w{i}", [P, 2 * NG + ND]) for i in range(2)]
    stage = sb("m_stage", [P, 2 * NG + ND], F32)
    gated = [sb(f"m_gated{j}", [P, CH], F32) for j in range(J)]
    prod = [sb(f"m_prod{j}", [P, CH], F32) for j in range(J)]
    prodp = [parts(f"prod{j}", [P, CH]) for j in range(J)]

    names = """w_staged w_hi w_cut gate_made up_made silu_ready prod_ready prod_hi prod_lo y_made y_added stored""".split()
    S = {n: sem("m_" + n) for n in names}

    def gate_of(slot, part, k, j):
        return wp[slot][part][:, k * W + j * P:k * W + (j + 1) * P]

    def up_of(slot, part, k, j):
        return wp[slot][part][:, NG + k * W + j * P:NG + k * W + (j + 1) * P]

    def down_of(slot, part, j):
        return wp[slot][part][:, 2 * NG + j * DM:2 * NG + (j + 1) * DM]

    def turns(eng, step):
        with eng.Fori(0, PAIRS // 2) as o:
            for slot in range(2):
                with eng.Fori(0, NC) as c:
                    step((2 * o + slot) * NC + c, c, slot, 2 * o + slot)

    def before(n, each, i):
        return each * n + i + 1

    def now(n, each, i):
        return each * (n + 1) + i + 1

    block = nc.Block()
    with block:
        @block.sync
        def _(sp):
            g3, u3 = (w.rearrange("(k p) f -> p k f", p=P) for w in (gate, up))
            d3 = down.rearrange("(f p) d -> p f d", p=P)

            def load(pair):
                col, row = sp.snap(pair * W), sp.snap(pair * J)
                if not isinstance(pair, int) or pair > 0:
                    sp.wait_ge(S["w_cut"], pair)
                sp.dma_start(stage[:, 0:NG].rearrange("p (k f) -> p k f", k=KD), g3[:, :, bass.ds(col, W)]).then_inc(S["w_staged"], 16)
                sp.dma_start(stage[:, NG:2 * NG].rearrange("p (k f) -> p k f", k=KD), u3[:, :, bass.ds(col, W)]).then_inc(S["w_staged"], 16)
                sp.dma_start(stage[:, 2 * NG:].rearrange("p (j d) -> p j d", j=J), d3[:, bass.ds(row, J), :]).then_inc(S["w_staged"], 16)

            load(0)
            with sp.Fori(1, PAIRS) as pair:
                load(pair)
            for c in range(NC):
                sp.wait_ge(S["y_added"], now((PAIRS - 1) * NC + c, TPC, TPC - 1))
                sp.dma_start(out[c * CH:(c + 1) * CH, :].rearrange("(b p) d -> p b d", p=P), y[:, TPC * c:TPC * (c + 1), :]
                             ).then_inc(S["stored"], 16)
            sp.wait_ge(S["stored"], 16 * NC)

        @block.tensor
        def _(pe):
            def step(n, c, slot, pair):
                col = pe.snap(c * CH)
                xs = [[xT_all[part][:, k, bass.ds(col, CH)] for part in range(2)] for k in range(KD)]
                pe.wait_ge(S["w_cut"], pair + 1)
                for j in range(J):
                    pe.wait_ge(S["prod_ready"], before(n, J, j))
                    product(pe, bank[2 * j][:], [([gate_of(slot, q, k, j) for q in range(2)], xs[k]) for k in range(KD)]
                            ).then_inc(S["gate_made"], 1)
                    product(pe, bank[2 * j + 1][:], [([up_of(slot, q, k, j) for q in range(2)], xs[k]) for k in range(KD)]
                            ).then_inc(S["up_made"], 1)
                for j in range(J):
                    pe.wait_ge(S["prod_lo"], J * n + j + 1)
                    for b in range(TPC):
                        if j == 0:
                            pe.wait_ge(S["y_added"], before(n, TPC, b))
                        rows = slice(b * P, (b + 1) * P)
                        mm = product(pe, bank[4 + b][:], [([prodp[j][q][:, rows] for q in range(2)],
                                                           [down_of(slot, q, j) for q in range(2)])],
                                     first=j == 0, last=j == J - 1)
                        if j == J - 1:
                            mm.then_inc(S["y_made"], 1)

            turns(pe, step)

        @block.scalar
        def _(act):
            def cut(pair, slot):
                act.wait_ge(S["w_staged"], 48 * (pair + 1))
                act.activation(wp[slot][0][:], stage[:], ACT.Copy).then_inc(S["w_hi"], 1)

            def step(n, c, slot, pair):
                for j in range(J):
                    act.wait_ge(S["gate_made"], J * n + j + 1)
                    act.activation(gated[j][:], bank[2 * j][:], ACT.Silu).then_inc(S["silu_ready"], 1)
                    act.wait_ge(S["prod_ready"], now(n, J, j))
                    act.activation(prodp[j][0][:], prod[j][:], ACT.Copy).then_inc(S["prod_hi"], 1)

            def pair_steps(o, slot, last=False):
                pair = 2 * o + slot
                if not last:
                    act.wait_ge(S["y_added"], before(pair * NC, TPC, TPC - 1))
                    cut(pair + 1, 1 - slot)
                with act.Fori(0, NC) as c:
                    step(pair * NC + c, c, slot, pair)

            cut(0, 0)
            with act.Fori(0, PAIRS // 2 - 1) as o:
                pair_steps(o, 0)
                pair_steps(o, 1)
            pair_steps(PAIRS // 2 - 1, 0)
            pair_steps(PAIRS // 2 - 1, 1, last=True)

        @block.gpsimd
        def _(pool):
            with pool.Fori(0, PAIRS // 2) as o:
                for slot in range(2):
                    pool.wait_ge(S["w_hi"], 2 * o + slot + 1)
                    pool.tensor_tensor(wp[slot][1][:], stage[:], wp[slot][0][:], ALU.subtract).then_inc(S["w_cut"], 1)

        @block.vector
        def _(dve):
            def step(n, c, slot, pair):
                for j in range(J):
                    dve.wait_ge(S["silu_ready"], J * n + j + 1)
                    dve.wait_ge(S["up_made"], J * n + j + 1)
                    dve.tensor_tensor(prod[j][:], gated[j][:], bank[2 * j + 1][:], ALU.mult).then_inc(S["prod_ready"], 1)
                    dve.wait_ge(S["prod_hi"], J * n + j + 1)
                    dve.tensor_tensor(prodp[j][1][:], prod[j][:], prodp[j][0][:], ALU.subtract).then_inc(S["prod_lo"], 1)
                for b in range(TPC):
                    dve.wait_ge(S["y_made"], TPC * n + b + 1)
                    row = y[:].rearrange("p b d -> p (b d)")[:, bass.ds((c * TPC + b) * DM, DM)]
                    dve.tensor_tensor(row, row, bank[4 + b][:], ALU.add).then_inc(S["y_added"], 1)

            dve.sem_inc(S["prod_ready"], J)
            dve.sem_inc(S["y_added"], TPC)
            turns(dve, step)


def build(nc, a, out):
    x1 = nc.dram_tensor("x1", (T, DM), F32).ap()
    x2 = nc.dram_tensor("x2", (T, DM), F32).ap()
    x3 = nc.dram_tensor("x3", (T, DM), F32).ap()
    with ExitStack() as top:
        stage_sems = []

        def sem(name):
            stage_sems.append(nc.alloc_semaphore(name=name))
            return stage_sems[-1]

        def stage_ends():
            nc.clear_and_free_semaphores(stage_sems)
            nc.all_engine_barrier()
            stage_sems.clear()

        def holds(ctx):
            return lambda name, shape, dtype: ctx.enter_context(nc.sbuf_tensor(name, shape, dtype))

        bank = [top.enter_context(nc.psum_tensor(f"bank{i}", [P, 512], F32)) for i in range(8)]
        ident = top.enter_context(nc.sbuf_tensor("ident", [P, P], F32))
        ident_loaded = sem("ident_loaded")
        with nc.Block() as block:
            @block.sync
            def _(sp):
                sp.dma_start(ident[:], a["ident"]).then_inc(ident_loaded, 16)
                sp.wait_ge(ident_loaded, 16)
        with ExitStack() as c:
            l0_attention(nc, holds(c), sem, bank, ident, a["x"], a["ctxT"], a["wq0"], a["wk0"], a["wv0"], a["wo0"],
                         a["gq"], a["gk"], x1)
        stage_ends()
        with ExitStack() as c:
            l0_ffn(nc, holds(c), sem, bank, ident, x1, a["w1"], a["b1"], a["w2"], a["b2"], a["w3"], a["b3"], x2)
        stage_ends()
        with ExitStack() as c:
            l1_attention(nc, holds(c), sem, bank, ident, x2, a["ctxT"], a["pos"], a["wq1"], a["wkv"], a["wo1"], a["bo"], x3)
        stage_ends()
        with ExitStack() as kept:
            xT_all = [holds(kept)(f"xT_all{i}", [P, KD, T], F32R) for i in range(2)]
            y = holds(kept)("y_all", [P, NB, DM], F32)
            with ExitStack() as routing:
                hqT = holds(routing)("hqT", [P, T], F32)
                with ExitStack() as c:
                    l1_ffn_front(nc, holds(c), sem, bank, ident, x3, a["wr"], xT_all, hqT, y)
                with ExitStack() as c:
                    l1_experts(nc, holds(c), sem, bank, ident, a["keys"], a["iota"], a["left"], a["deT"], a["ue"],
                               xT_all, hqT, y)
            with ExitStack() as c:
                l1_mlp(nc, holds(c), sem, bank, a["gate"], a["up"], a["down"], xT_all, y, out)


def kernel(x, ctx_1024, fside_BxSx2_0, L0_xattn_Wq, L0_xattn_Wk, L0_xattn_Wv, L0_xattn_Wo, L0_xattn_gq, L0_xattn_gk,
           L0_ffn_W1, L0_ffn_b1, L0_ffn_W2, L0_ffn_b2, L0_ffn_W3, L0_ffn_b3, L1_xattn_Wq, L1_xattn_Wkv, L1_xattn_Wout,
           L1_xattn_bout, L1_ffn_W_q, L1_ffn_keys, L1_ffn_down_embed, L1_ffn_up_embed, L1_ffn_gate_w, L1_ffn_up_w,
           L1_ffn_down_w):
    import numpy as np
    import concourse.bacc as _bacc
    from concourse.bass_utils import run_bass_kernel_spmd as _run
    nc = _bacc.Bacc("TRN2", target_bir_lowering=False, num_devices=1)

    def halves(w):
        w = np.asarray(w)
        return w.reshape(w.shape[0], 2, 1024).transpose(1, 0, 2)

    def on_rows(b):
        return np.broadcast_to(b, (P, len(b)))

    laid_out = {
        "ident": np.eye(P, dtype=np.float32),
        "x": np.asarray(x).reshape(T, DM),
        "ctxT": np.asarray(ctx_1024).reshape(T, KC, P).transpose(2, 1, 0),
        "wq0": halves(L0_xattn_Wq), "wk0": halves(L0_xattn_Wk), "wv0": halves(L0_xattn_Wv),
        "wo0": np.asarray(L0_xattn_Wo).reshape(2, 1024, DM),
        "gq": np.asarray(L0_xattn_gq).reshape(P, 1), "gk": np.asarray(L0_xattn_gk).reshape(P, 1),
        "w1": np.asarray(L0_ffn_W1).T, "w2": np.asarray(L0_ffn_W2).T, "w3": np.asarray(L0_ffn_W3).T,
        "b1": np.asarray(L0_ffn_b1).reshape(8, P).T, "b2": np.asarray(L0_ffn_b2).reshape(8, P).T,
        "b3": on_rows(np.asarray(L0_ffn_b3)),
        "pos": np.asarray(fside_BxSx2_0).reshape(T, 2),
        "wq1": np.asarray(L1_xattn_Wq), "wkv": np.asarray(L1_xattn_Wkv), "wo1": np.asarray(L1_xattn_Wout),
        "bo": on_rows(np.asarray(L1_xattn_bout)),
        "wr": np.asarray(L1_ffn_W_q),
        "keys": np.concatenate([np.asarray(L1_ffn_keys)] * 2, 1).transpose(1, 0, 2),
        "iota": on_rows(np.arange(64, dtype=np.float32)), "left": on_rows(np.arange(8, 0, -1).astype(np.float32)),
        "deT": np.asarray(L1_ffn_down_embed).T, "ue": np.asarray(L1_ffn_up_embed),
        "gate": np.asarray(L1_ffn_gate_w), "up": np.asarray(L1_ffn_up_w), "down": np.asarray(L1_ffn_down_w),
    }
    arrays = {"in_" + name: np.ascontiguousarray(v) for name, v in laid_out.items()}
    given = {name[3:]: nc.dram_tensor(name, v.shape, mybir.dt.from_np(v.dtype), kind="ExternalInput").ap()
             for name, v in arrays.items()}
    build(nc, given, nc.dram_tensor("out_0", (T, DM), F32, kind="ExternalOutput").ap())
    return _run(nc, [arrays], core_ids=[0]).results[0]["out_0"].reshape(16, 128, 512)
```

```python
from contextlib import ExitStack

import concourse.bass as bass
from concourse import mybir

ALU = mybir.AluOpType
ACT = mybir.ActivationFunctionType
AX = mybir.AxisListType
F32 = mybir.dt.float32
F32R = mybir.dt.float32r
I32 = mybir.dt.int32
U32 = mybir.dt.uint32

P = 128
T = 2048
NB = 16
DM = 512
KD = DM // P
CD = 256
KC = CD // P
EPS = 1e-5
RSQRT_MAGIC = 0x5F3759DF
AHEAD = (slice(0, 2), slice(2, NB))


def part_products(parts_a, parts_b):
    (ah, al), (bh, bl) = parts_a, parts_b
    return ((ah, bh), (ah, bl), (al, bh))


def product(pe, out, pairs, first=True, last=True):
    terms = [t for a, b in pairs for t in part_products(a, b)]
    for n, (st, mv) in enumerate(terms):
        mm = pe.matmul(out, st, mv, start=first and n == 0, stop=last and n == len(terms) - 1)
    return mm


def rsqrt_steps(dve, then, out, v, t_a):
    then(dve.tensor_scalar(out.bitcast(I32), v.bitcast(I32), -0.5, float(RSQRT_MAGIC), ALU.mult, ALU.add))
    for n in range(3):
        then(dve.tensor_tensor(t_a, out, out, ALU.mult))
        then(dve.scalar_tensor_tensor(t_a, t_a, -0.5, v, ALU.mult, ALU.mult))
        last = dve.scalar_tensor_tensor(out, t_a, 1.5, out, ALU.add, ALU.mult)
        if n < 2:
            then(last)
    return last


def norm_statistics(dve, then, tiles, x, bn, mv, ln, ln_t):
    for b in range(tiles.start, tiles.stop):
        stats = dve.bn_stats(bn[:, b, :], x[:, b, :])
    then(stats)
    for b in range(tiles.start, tiles.stop):
        stats = dve.bn_aggr(mv[:, b, :], bn[:, b, :])
    then(stats)
    dve.tensor_copy(ln[:, tiles, 0], mv[:, tiles, 0])
    then(dve.tensor_scalar(ln_t[:, 0, tiles], mv[:, tiles, 1], EPS, None, ALU.add))
    then(rsqrt_steps(dve, then, ln[:, tiles, 1], ln_t[:, 0, tiles], ln_t[:, 1, tiles]))


def l0_attention(nc, sb, sem, bank, ident, x, ctxT, wq, wk, wv, wo, gq, gk, x1):
    H, D, HALF, G = 16, 128, 8, 4
    W = HALF * D
    STEPS = 2 * NB

    def parts(name, shape):
        return sb(name + "_hi", shape, F32R), sb(name + "_lo", shape, F32R)

    wqp, wkp, wvp, wop = parts("wq", [P, KD, W]), parts("wk", [P, KC, W]), parts("wv", [P, KC, W]), parts("wo", [P, HALF, DM])
    stage = [sb(f"stage{i}", [P, 2048], F32) for i in range(2)]
    xres = sb("xres", [P, NB, DM], F32)
    x_in = sb("x_in", [P, DM], F32)
    xn = sb("xn", [P, DM], F32)
    xTp = parts("xT", [P, KD, P])
    ctx_in = sb("ctx_in", [P, KC, P], F32)
    ctxp = parts("ctx", [P, KC, P])
    q_sb = [sb(f"q_sb{g}", [P, G * D], F32) for g in range(2)]
    k_sb = [sb(f"k_sb{g}", [P, G * D], F32) for g in range(2)]
    v_sb = [sb(f"v_sb{g}", [P, G * D], F32) for g in range(2)]
    qT_sb = sb("qT_sb", [P, G * P], F32)
    kT_sb = sb("kT_sb", [P, G * P], F32)
    junk = sb("junk", [P, 2 * G, P], mybir.dt.bfloat16)
    prob = [sb(f"prob{g}", [P, G, P], F32) for g in range(2)]
    pT_sb = sb("pT_sb", [P, G * P], F32)
    oTp = [parts(f"oT{g}", [P, G, P]) for g in range(2)]
    bn = sb("bn", [P, NB, 6], F32)
    mv = sb("mv", [P, NB, 2], F32)
    ln = sb("ln", [P, NB, 2], F32)
    ln_t = sb("ln_t", [P, 2, NB], F32)
    ln_now = sb("ln_now", [P, 2], F32)
    gqk = sb("gqk", [P, 3], F32)
    ssq = [sb(f"ssq{g}", [P, 2, G], F32) for g in range(2)]
    rms = [sb(f"rms{g}", [P, 3, 2 * G], F32) for g in range(2)]
    mx = [sb(f"mx{g}", [P, 2, G], F32) for g in range(2)]
    den = [sb(f"den{g}", [P, 2, G], F32) for g in range(2)]

    names = """x_loaded ctx_loaded xres_loaded0 xres_loaded1 g_loaded xn_ready xT_turned xT_hi xT_lo ctx_hi ctx_split
        w_hi w_staged0 w_staged1 w_cut stored s_turn y_ready y_added""".split()
    names += [f"{n}{g}" for g in range(2) for n in """q_made k_made v_made q_copied k_copied v_copied squared
        rms_ready k_normed q_turned k_turned qT_copied kT_copied scored bias_ready exped normed p_turned pT_copied
        mixed oT_hi oT_lo""".split()]
    S = {n: sem("a_" + n) for n in names}

    def at(n, s):
        return S[n], s + 1

    def later(s):
        return not isinstance(s, int) or s > 0

    CUT = 2048
    QKV, PIECES = 4, 6
    SCORES = (6, 4)

    def parts_of_piece(n):
        wp, c = ((wqp, 0), (wqp, 1), (wkp, 0), (wvp, 0), (wop, 0), (wop, 1))[n]
        return [w[:].rearrange("p k w -> p (k w)")[:, c * CUT:(c + 1) * CUT] for w in wp]

    def new_weights(pe, s, half_pieces):
        if isinstance(s, int) and s % NB == 0:
            pe.wait_ge(S["w_cut"], PIECES * (s // NB) + half_pieces)

    block = nc.Block()
    with block:
        @block.sync
        def _(sp):
            def load_x(s):
                row = sp.snap((s % NB) * P)
                if later(s):
                    sp.wait_ge(*at("xn_ready", s - 1))
                sp.dma_start(x_in[:], x[bass.ds(row, P), :]).then_inc(S["x_loaded"], 16)

            def load_ctx(s):
                row = sp.snap((s % NB) * P)
                if later(s):
                    sp.wait_ge(*at("ctx_split", s - 1))
                sp.dma_start(ctx_in[:], ctxT[:, :, bass.ds(row, P)]).then_inc(S["ctx_loaded"], 16)

            load_x(0)
            load_ctx(0)
            sp.dma_start(gqk[:, 0:1], gq).then_inc(S["g_loaded"], 16)
            sp.dma_start(gqk[:, 1:2], gk).then_inc(S["g_loaded"], 16)
            for i, tiles in enumerate(AHEAD):
                sp.dma_start(xres[:, tiles, :], x.rearrange("(b p) d -> p b d", p=P)[:, tiles, :]).then_inc(S[f"xres_loaded{i}"], 16)
            load_x(1)

            def step(s, to_load=2, final=False):
                if to_load > 1:
                    load_x(s + 2)
                if to_load > 0:
                    load_ctx(s + 1)
                if final:
                    row, col = sp.snap((s - NB) * P), sp.snap((s - NB) * DM)
                    sp.wait_ge(S["y_added"], s + 1)
                    sp.dma_start(x1[bass.ds(row, P), :], xres[:].rearrange("p b d -> p (b d)")[:, bass.ds(col, DM)]).then_inc(S["stored"], 16)

            with sp.Fori(0, NB) as s:
                step(s)
            with sp.Fori(NB, STEPS - 2) as s:
                step(s, final=True)
            step(STEPS - 2, to_load=1, final=True)
            step(STEPS - 1, to_load=0, final=True)
            sp.wait_ge(S["stored"], 16 * NB)

        @block.gpsimd
        def _(pool):
            def fetch(h, n):
                q, k, v, o = (w[h].rearrange("(k p) w -> p k w", p=P) for w in (wq, wk, wv, wo))
                src = (q[:, 0:2], q[:, 2:4], k, v, o[:, 0:4], o[:, 4:8])[n]
                if h or n >= 2:
                    pool.wait_ge(S["w_cut"], PIECES * h + n - 1)
                pool.dma_start(stage[n % 2][:], src).then_inc(S[f"w_staged{n % 2}"], 16)

            def split_ctx(s):
                pool.wait_ge(*at("ctx_hi", s))
                pool.tensor_tensor(ctxp[1][:], ctx_in[:], ctxp[0][:], ALU.subtract).then_inc(S["ctx_split"], 1)

            def norm_k(s, g):
                pool.wait_ge(*at(f"rms_ready{g}", s))
                k3 = k_sb[g][:].rearrange("p (h d) -> p h d", h=G)
                pool.tensor_tensor(k3, k3, rms[g][:, 0, G:2 * G].unsqueeze(2).to_broadcast([P, G, D]),
                                   ALU.mult).then_inc(S[f"k_normed{g}"], 1)

            def step(s, last=False):
                norm_k(s, 0)
                norm_k(s, 1)
                if not last:
                    split_ctx(s + 1)

            for n in range(PIECES):
                fetch(0, n)
                if n == 1:
                    split_ctx(0)
            fetch(1, 0)
            fetch(1, 1)
            with pool.Fori(0, NB - 1) as s:
                step(s)
            norm_k(NB - 1, 0)
            norm_k(NB - 1, 1)
            split_ctx(NB)
            for n in range(2, PIECES):
                fetch(1, n)
            with pool.Fori(NB, STEPS - 1) as s:
                step(s)
            step(STEPS - 1, last=True)

        @block.tensor
        def _(pe):
            def turn(out_bank, src, what):
                for j in range(4):
                    t = pe.transpose(bank[out_bank][:, j * P:(j + 1) * P], src[:, j * P:(j + 1) * P], ident[:])
                t.then_inc(S[what], 1)

            def turn_x(s, first=False):
                pe.wait_ge(*at("xn_ready", s))
                if not first:
                    pe.wait_ge(*at("q_copied1", s - 1))
                turn(0, xn, "xT_turned")

            def project(s, g, what, b, act, kt, wp):
                cols = slice(g * G * D, (g + 1) * G * D)
                pairs = [((act[0][:, k, :], act[1][:, k, :]), (wp[0][:, k, cols], wp[1][:, k, cols])) for k in range(kt)]
                product(pe, bank[b][:], pairs).then_inc(S[f"{what}_made{g}"], 1)

            def queries(s, g, first=False):
                if g == 0:
                    pe.wait_ge(*at("xT_lo", s))
                    new_weights(pe, s, 2)
                else:
                    pe.wait_ge(*at("q_copied0", s))
                project(s, g, "q", 0, xTp, KD, wqp)

            def keys(s, g, first=False):
                if g == 0:
                    pe.wait_ge(*at("ctx_split", s))
                    new_weights(pe, s, 3)
                    if not first:
                        pe.wait_ge(*at("kT_copied1", s - 1))
                else:
                    if not first:
                        pe.wait_ge(*at("oT_lo0", s - 1))
                project(s, g, "k", (3, 7)[g], ctxp, KC, wkp)

            def values(s, g, first=False):
                if g == 0:
                    pe.wait_ge(*at("ctx_split", s))
                    new_weights(pe, s, QKV)
                    if not first:
                        pe.wait_ge(*at("pT_copied0", s - 1))
                else:
                    if not first:
                        pe.wait_ge(*at("y_added", s - 1))
                project(s, g, "v", (5, 1)[g], ctxp, KC, wvp)

            def turn_q(s, g, first=False):
                pe.wait_ge(*at(f"q_copied{g}", s))
                if g == 0:
                    pe.wait_ge(*at("v_copied0", s))
                elif not first:
                    pe.wait_ge(*at("pT_copied1", s - 1))
                turn((5, 2)[g], q_sb[g], f"q_turned{g}")

            def turn_k(s, g):
                pe.wait_ge(*at(f"k_normed{g}", s))
                if g == 1:
                    pe.wait_ge(*at("k_copied0", s))
                elif later(s):
                    pe.wait_ge(*at("exped0", s - 1))
                turn((6, 3)[g], k_sb[g], f"k_turned{g}")

            def score(s, g):
                pe.wait_ge(*at(f"qT_copied{g}", s))
                pe.wait_ge(*at(f"kT_copied{g}", s))
                if g == 1 and later(s):
                    pe.wait_ge(*at("oT_lo1", s - 1))
                for j in range(G):
                    c = slice(j * P, (j + 1) * P)
                    mm = pe.matmul(bank[SCORES[g]][:, c], qT_sb[:, c], kT_sb[:, c], start=True, stop=True)
                mm.then_inc(S[f"scored{g}"], 1)

            def turn_p(s, g):
                pe.wait_ge(*at(f"normed{g}", s))
                pe.wait_ge(*at(("qT_copied0", "qT_copied1")[g], s))
                turn((5, 2)[g], prob[g][:].rearrange("p h k -> p (h k)"), f"p_turned{g}")

            def mix(s, g):
                pe.wait_ge(*at(f"pT_copied{g}", s))
                pe.wait_ge(*at(f"v_copied{g}", s))
                pe.wait_ge(*at(("k_copied1", "exped1")[g], s))
                for j in range(G):
                    c = slice(j * P, (j + 1) * P)
                    mm = pe.matmul(bank[(7, 4)[g]][:, c], v_sb[g][:, c], pT_sb[:, c], start=True, stop=True)
                mm.then_inc(S[f"mixed{g}"], 1)

            def output(s, g):
                pe.wait_ge(*at(f"oT_lo{g}", s))
                if g == 0:
                    new_weights(pe, s, PIECES)
                    pe.wait_ge(*at("v_copied1", s))
                pairs = [((oTp[g][0][:, j, :], oTp[g][1][:, j, :]), (wop[0][:, g * G + j, :], wop[1][:, g * G + j, :]))
                         for j in range(G)]
                mm = product(pe, bank[1][:], pairs, first=g == 0, last=g == 1)
                if g == 1:
                    mm.then_inc(S["y_ready"], 1)

            def step(s, first=False, last=False):
                if not last:
                    turn_x(s + 1)
                turn_q(s, 0)
                turn_k(s, 0)
                keys(s, 1, first)
                score(s, 0)
                values(s, 1, first)
                turn_q(s, 1, first)
                if not last:
                    queries(s + 1, 0)
                turn_k(s, 1)
                turn_p(s, 0)
                score(s, 1)
                mix(s, 0)
                if not last:
                    values(s + 1, 0)
                output(s, 0)
                turn_p(s, 1)
                if not last:
                    keys(s + 1, 0)
                mix(s, 1)
                if not last:
                    queries(s + 1, 1)
                output(s, 1)

            turn_x(0, True)
            queries(0, 0, True)
            keys(0, 0, True)
            values(0, 0, True)
            queries(0, 1, True)
            step(0, first=True)
            with pe.Fori(1, NB - 1) as s:
                step(s)
            step(NB - 1)
            step(NB)
            with pe.Fori(NB + 1, STEPS - 1) as s:
                step(s)
            step(STEPS - 1, last=True)

        @block.scalar
        def _(act):
            def split_xT(s):
                act.wait_ge(*at("xT_turned", s))
                if not isinstance(s, int) or s > 0:
                    act.wait_ge(*at("q_made1", s - 1))
                act.activation(xTp[0][:].rearrange("p k t -> p (k t)"), bank[0][:], ACT.Copy).then_inc(S["xT_hi"], 1)

            def split_ctx(s):
                act.wait_ge(S["ctx_loaded"], 16 * (s + 1))
                act.activation(ctxp[0][:], ctx_in[:], ACT.Copy).then_inc(S["ctx_hi"], 1)

            def square(s, g, kind):
                src = (q_sb, k_sb)[kind][g]
                act.wait_ge(*at(("q_copied", "k_copied")[kind] + str(g), s))
                if g == 0 and kind == 0 and (not isinstance(s, int) or s > 0):
                    act.wait_ge(*at("rms_ready1", s - 1))
                if g == 1 and kind == 0:
                    act.wait_ge(*at("rms_ready0", s))
                for j in range(G):
                    a = act.activation(junk[:, kind * G + j, :], src[:, j * D:(j + 1) * D], ACT.Square,
                                       accum_out=ssq[g][:, kind, j:j + 1])
                a.then_inc(S[f"squared{g}"], 1)

            def copy_v(s, g):
                act.wait_ge(*at(f"v_made{g}", s))
                if not isinstance(s, int) or s > 0:
                    act.wait_ge(*at(f"mixed{g}", s - 1))
                act.activation(v_sb[g][:], bank[(5, 1)[g]][:], ACT.Copy).then_inc(S[f"v_copied{g}"], 1)

            def copy_qT(s, g):
                act.wait_ge(*at(f"q_turned{g}", s))
                if g == 1:
                    act.wait_ge(*at("scored0", s))
                act.activation(qT_sb[:], bank[(5, 2)[g]][:], ACT.Copy).then_inc(S[f"qT_copied{g}"], 1)

            def exps(s, g):
                act.wait_ge(*at(f"bias_ready{g}", s))
                for j in range(G):
                    a = act.activation(prob[g][:, j, :], bank[SCORES[g]][:, j * P:(j + 1) * P], ACT.Exp,
                                       bias=mx[g][:, 1, j:j + 1], scale=rms[g][:, 0, j:j + 1],
                                       accum_out=den[g][:, 0, j:j + 1])
                a.then_inc(S[f"exped{g}"], 1)

            def split_o(s, g):
                act.wait_ge(*at(f"mixed{g}", s))
                if g == 0 and (not isinstance(s, int) or s > 0):
                    act.wait_ge(*at("y_ready", s - 1))
                act.activation(oTp[g][0][:].rearrange("p h q -> p (h q)"), bank[(7, 4)[g]][:], ACT.Copy
                               ).then_inc(S[f"oT_hi{g}"], 1)

            def cut_hi(h, pieces):
                for n in pieces:
                    act.wait_ge(S[f"w_staged{n % 2}"], 16 * (3 * h + n // 2 + 1))
                    if h and n == 0:
                        act.wait_ge(*at("v_made1", NB - 1))
                    if h and n == QKV:
                        act.wait_ge(*at("y_ready", NB - 1))
                    act.activation(parts_of_piece(n)[0], stage[n % 2][:], ACT.Copy).then_inc(S["w_hi"], 1)

            def step(s, last=False):
                if not last:
                    split_xT(s + 1)
                copy_qT(s, 0)
                square(s, 1, 0)
                square(s, 1, 1)
                exps(s, 0)
                copy_v(s, 1)
                if not last:
                    split_ctx(s + 1)
                if isinstance(s, int) and s == NB - 1:
                    cut_hi(1, range(QKV))
                copy_qT(s, 1)
                if not last:
                    square(s + 1, 0, 0)
                split_o(s, 0)
                exps(s, 1)
                if not last:
                    copy_v(s + 1, 0)
                    square(s + 1, 0, 1)
                split_o(s, 1)

            split_ctx(0)
            cut_hi(0, range(2))
            split_xT(0)
            cut_hi(0, range(2, QKV))
            square(0, 0, 0)
            square(0, 0, 1)
            copy_v(0, 0)
            cut_hi(0, range(QKV, PIECES))
            step(0)
            with act.Fori(1, NB - 1) as s:
                step(s)
            step(NB - 1)
            cut_hi(1, range(QKV, PIECES))
            step(NB)
            with act.Fori(NB + 1, STEPS - 1) as s:
                step(s)
            step(STEPS - 1, last=True)

        @block.vector
        def _(dve):
            chain = [0]

            def then(ins):
                chain[0] = chain[0] + 1
                ins.then_inc(S["s_turn"], 1)
                dve.wait_ge(S["s_turn"], chain[0])

            def chain_from_zero():
                dve.sem_clear(S["s_turn"])
                chain[0] = 0

            def statistics(i):
                dve.wait_ge(S[f"xres_loaded{i}"], 16)
                norm_statistics(dve, then, AHEAD[i], xres, bn, mv, ln, ln_t)

            def layer_norm(s):
                dve.wait_ge(S["x_loaded"], 16 * (s + 1))
                if later(s):
                    dve.wait_ge(*at("xT_turned", s - 1))
                then(dve.tensor_copy(ln_now[:], ln[:].rearrange("p b c -> p (b c)")[:, bass.ds((s % NB) * 2, 2)]))
                dve.tensor_scalar(xn[:], x_in[:], ln_now[:, 0:1], ln_now[:, 1:2], ALU.subtract, ALU.mult
                                  ).then_inc(S["xn_ready"], 1)

            def cut_lo(h, pieces):
                for n in pieces:
                    hi, lo = parts_of_piece(n)
                    dve.wait_ge(S["w_hi"], PIECES * h + n + 1)
                    dve.tensor_tensor(lo, stage[n % 2][:], hi, ALU.subtract).then_inc(S["w_cut"], 1)

            def split_xT(s):
                dve.wait_ge(*at("xT_hi", s))
                hi, lo = (p[:].rearrange("p k t -> p (k t)") for p in xTp)
                dve.tensor_tensor(lo, bank[0][:], hi, ALU.subtract).then_inc(S["xT_lo"], 1)

            def copy_q(s, g):
                dve.wait_ge(*at(f"q_made{g}", s))
                dve.tensor_copy(q_sb[g][:], bank[0][:]).then_inc(S[f"q_copied{g}"], 1)

            def copy_k(s, g):
                dve.wait_ge(*at(f"k_made{g}", s))
                dve.tensor_copy(k_sb[g][:], bank[(3, 7)[g]][:]).then_inc(S[f"k_copied{g}"], 1)

            def means(s, g):
                dve.wait_ge(S[f"squared{g}"], 2 * (s + 1))
                r = rms[g]
                both = ssq[g][:].rearrange("p a h -> p (a h)")
                then(dve.tensor_scalar(r[:, 2, :], both, D * EPS, None, ALU.add))
                rsqrt_steps(dve, then, r[:, 0, :], r[:, 2, :], r[:, 1, :]).then_inc(S[f"rms_ready{g}"], 1)

            def copy_kT(s, g):
                dve.wait_ge(*at(f"k_turned{g}", s))
                if g == 1:
                    dve.wait_ge(*at("scored0", s))
                dve.tensor_scalar(kT_sb[:], bank[(6, 3)[g]][:], gqk[:, 2:3], None, ALU.mult
                                  ).then_inc(S[f"kT_copied{g}"], 1)

            def maxima(s, g):
                dve.wait_ge(*at(f"scored{g}", s))
                then(dve.tensor_reduce(mx[g][:, 0, :], bank[SCORES[g]][:].rearrange("p (h k) -> p h k", h=G),
                                       AX.X, ALU.max))
                dve.scalar_tensor_tensor(mx[g][:, 1, :], mx[g][:, 0, :], -1.0, rms[g][:, 0, 0:G], ALU.mult, ALU.mult
                                         ).then_inc(S[f"bias_ready{g}"], 1)

            def normalise(s, g):
                dve.wait_ge(*at(f"exped{g}", s))
                then(dve.reciprocal(den[g][:, 1, :], den[g][:, 0, :]))
                dve.tensor_tensor(prob[g][:], prob[g][:], den[g][:, 1, :].unsqueeze(2).to_broadcast([P, G, P]),
                                  ALU.mult).then_inc(S[f"normed{g}"], 1)

            def copy_pT(s, g):
                dve.wait_ge(*at(f"p_turned{g}", s))
                if g == 1:
                    dve.wait_ge(*at("mixed0", s))
                dve.tensor_copy(pT_sb[:], bank[(5, 2)[g]][:]).then_inc(S[f"pT_copied{g}"], 1)

            def split_o(s, g):
                dve.wait_ge(*at(f"oT_hi{g}", s))
                hi, lo = (p[:].rearrange("p h q -> p (h q)") for p in oTp[g])
                dve.tensor_tensor(lo, bank[(7, 4)[g]][:], hi, ALU.subtract).then_inc(S[f"oT_lo{g}"], 1)

            def add_y(s):
                dve.wait_ge(*at("y_ready", s))
                r = xres[:].rearrange("p b d -> p (b d)")[:, bass.ds((s % NB) * DM, DM)]
                dve.tensor_tensor(r, r, bank[1][:], ALU.add).then_inc(S["y_added"], 1)

            def step(s, last=False):
                chain_from_zero()
                if not last:
                    split_xT(s + 1)
                copy_kT(s, 0)
                copy_k(s, 1)
                maxima(s, 0)
                means(s, 1)
                normalise(s, 0)
                if isinstance(s, int) and s == NB - 1:
                    cut_lo(1, range(QKV))
                if not last:
                    copy_q(s + 1, 0)
                copy_kT(s, 1)
                copy_pT(s, 0)
                maxima(s, 1)
                split_o(s, 0)
                normalise(s, 1)
                copy_pT(s, 1)
                if not last:
                    copy_k(s + 1, 0)
                if not isinstance(s, int) or s < STEPS - 2:
                    layer_norm(s + 2)
                split_o(s, 1)
                if not last:
                    copy_q(s + 1, 1)
                    means(s + 1, 0)
                add_y(s)

            dve.wait_ge(S["g_loaded"], 32)
            then(dve.scalar_tensor_tensor(gqk[:, 2:3], gqk[:, 0:1], float(D) ** 0.5, gqk[:, 1:2], ALU.mult, ALU.mult))
            statistics(0)
            layer_norm(0)
            cut_lo(0, range(2))
            split_xT(0)
            layer_norm(1)
            cut_lo(0, range(2, QKV))
            copy_q(0, 0)
            copy_k(0, 0)
            means(0, 0)
            copy_q(0, 1)
            cut_lo(0, range(QKV, PIECES))
            statistics(1)
            step(0)
            with dve.Fori(1, NB - 1) as s:
                step(s)
            step(NB - 1)
            cut_lo(1, range(QKV, PIECES))
            step(NB)
            with dve.Fori(NB + 1, STEPS - 2) as s:
                step(s)
            step(STEPS - 2)
            step(STEPS - 1, last=True)


def l0_ffn(nc, sb, sem, bank, ident, x1, w1, b1, w2, b2, w3, b3, x2):
    HID = 1024
    KH = HID // P
    CH = 512
    NC, TPC = T // CH, CH // P

    def parts(name, shape):
        return sb("f_" + name + "_hi", shape, F32R), sb("f_" + name + "_lo", shape, F32R)

    w1p, w2p, w3p = parts("w1", [P, KD, HID]), parts("w2", [P, KH, HID]), parts("w3", [P, KH, DM])
    PIECE = 1024
    stage = [sb(f"f_stage{i}", [P, PIECE], F32) for i in range(2)]
    x_in = [sb(f"f_x_in{i}", [P, DM], F32) for i in range(2)]
    res = [sb(f"f_res{i}", [P, DM], F32) for i in range(2)]
    xTp = parts("xT", [P, KD, CH])
    h1p = parts("h1", [P, KH, CH])
    h2p = [parts(f"h2{i}", [P, CH]) for i in range(2)]
    relu = [sb(f"f_relu{i}", [P, CH], F32) for i in range(2)]
    b12 = sb("f_b12", [P, 2, KH], F32)
    b3r = sb("f_b3", [P, DM], F32)
    bn = sb("f_bn", [P, 6], F32)
    mv = sb("f_mv", [P, 2], F32)
    rs = sb("f_rs", [P, 3], F32)

    names = """x_loaded0 x_loaded1 res_loaded0 res_loaded1 b_loaded w_staged0 w_staged1 w_hi w_cut xn_ready
        xT_turned xT_hi xT_lo h_made h_hi relu_ready h_lo y_made bias_added y_added stored0 stored1 s_turn""".split()
    S = {n: sem("f_" + n) for n in names}
    NP1, NP2, NP3 = KD * HID // PIECE, KH * HID // PIECE, KH * DM // PIECE
    HB = (4, 5, 6)

    def tile_of(c, j):
        return TPC * c + j + 1

    def hid(c, layer, m):
        return 2 * KH * c + layer * KH + m + 1

    pieces = [(w1.rearrange("(k p) h -> p k h", p=P)[:, :, 256 * n:256 * (n + 1)],
               [w[:, :, 256 * n:256 * (n + 1)] for w in w1p], KD) for n in range(NP1)]
    pieces += [(w2.rearrange("(k p) h -> p k h", p=P)[:, :, P * n:P * (n + 1)],
                [w[:, :, P * n:P * (n + 1)] for w in w2p], KH) for n in range(NP2)]
    pieces += [(w3.rearrange("(k p) h -> p k h", p=P)[:, 2 * n:2 * n + 2, :],
                [w[:, 2 * n:2 * n + 2, :] for w in w3p], 2) for n in range(NP3)]

    block = nc.Block()
    with block:
        @block.sync
        def _(sp):
            def load_x(c, j):
                row = sp.snap((c * TPC + j) * P)
                if not (isinstance(c, int) and c == 0 and j < 2):
                    sp.wait_ge(S["xT_turned"], tile_of(c, j) - 2)
                sp.dma_start(x_in[j % 2][:], x1[bass.ds(row, P), :]).then_inc(S[f"x_loaded{j % 2}"], 16)

            def load_res(c, j, first):
                row = sp.snap((c * TPC + j) * P)
                if not (first and j < 2):
                    sp.wait_ge(S[f"stored{j % 2}"], 16 * (2 * c + j // 2))
                sp.dma_start(res[j % 2][:], x1[bass.ds(row, P), :]).then_inc(S[f"res_loaded{j % 2}"], 16)

            def store(c, j):
                row = sp.snap((c * TPC + j) * P)
                sp.wait_ge(S["y_added"], tile_of(c, j))
                sp.dma_start(x2[bass.ds(row, P), :], res[j % 2][:]).then_inc(S[f"stored{j % 2}"], 16)

            def finish(c, first=False):
                for j in range(TPC):
                    store(c, j)
                    if j + 2 < TPC:
                        load_res(c, j + 2, first)

            def step(c, last=False):
                if not last:
                    for j in range(TPC):
                        load_x(c + 1, j)

            def first_res(c, first=False):
                load_res(c, 0, first)
                load_res(c, 1, first)

            load_x(0, 0)
            load_x(0, 1)
            sp.dma_start(b12[:, 0, :], b1).then_inc(S["b_loaded"], 16)
            sp.dma_start(b12[:, 1, :], b2).then_inc(S["b_loaded"], 16)
            sp.dma_start(b3r[:], b3).then_inc(S["b_loaded"], 16)
            load_x(0, 2)
            load_x(0, 3)
            first_res(0, first=True)
            step(0)
            finish(0, first=True)
            with sp.Fori(1, NC - 1) as c:
                first_res(c)
                step(c)
                finish(c)
            first_res(NC - 1)
            finish(NC - 1)
            for i in range(2):
                sp.wait_ge(S[f"stored{i}"], 16 * 2 * NC)

        @block.gpsimd
        def _(pool):
            def fetch(n):
                if n >= 2:
                    pool.wait_ge(S["w_cut"], n - 1)
                pool.dma_start(stage[n % 2][:].rearrange("p (k c) -> p k c", k=pieces[n][2]), pieces[n][0]
                               ).then_inc(S[f"w_staged{n % 2}"], 16)

            fetch(0)
            for n in range(len(pieces)):
                if n + 1 < len(pieces):
                    fetch(n + 1)
                _, (hi, lo), k = pieces[n]
                raw = stage[n % 2][:].rearrange("p (k c) -> p k c", k=k)
                pool.wait_ge(S["w_hi"], n + 1)
                pool.tensor_tensor(lo, raw, hi, ALU.subtract).then_inc(S["w_cut"], 1)

            def add_bias(c, j):
                pool.wait_ge(S[f"res_loaded{j % 2}"], 16 * (2 * c + j // 2 + 1))
                pool.tensor_tensor(res[j % 2][:], res[j % 2][:], b3r[:], ALU.add).then_inc(S["bias_added"], 1)

            pool.wait_ge(S["b_loaded"], 48)
            with pool.Fori(0, NC) as c:
                for j in range(TPC):
                    add_bias(c, j)

        @block.tensor
        def _(pe):
            def turn_x(c, j):
                pe.wait_ge(S["xn_ready"], tile_of(c, j))
                if not (isinstance(c, int) and c == 0 and j == 0):
                    pe.wait_ge(S["xT_lo"], tile_of(c, j) - 1)
                for k in range(KD):
                    t = pe.transpose(bank[7][:, k * P:(k + 1) * P], x_in[j % 2][:, k * P:(k + 1) * P], ident[:])
                t.then_inc(S["xT_turned"], 1)

            def hidden1(c, m, first):
                pe.wait_ge(S["w_cut"], m // 2 + 1)
                if m == 0:
                    pe.wait_ge(S["xT_lo"], tile_of(c, TPC - 1))
                if not (first and m < 3):
                    pe.wait_ge(S["relu_ready"], hid(c, 0, m) - 3)
                cols = slice(m * P, (m + 1) * P)
                pairs = [((w1p[0][:, k, cols], w1p[1][:, k, cols]), (xTp[0][:, k, :], xTp[1][:, k, :])) for k in range(KD)]
                product(pe, bank[HB[m % 3]][:], pairs).then_inc(S["h_made"], 1)

            def hidden2(c, m):
                pe.wait_ge(S["w_cut"], NP1 + m + 1)
                if m == 0:
                    pe.wait_ge(S["h_lo"], hid(c, 0, KH - 1))
                pe.wait_ge(S["relu_ready"], hid(c, 1, m) - 3)
                cols = slice(m * P, (m + 1) * P)
                pairs = [((w2p[0][:, k, cols], w2p[1][:, k, cols]), (h1p[0][:, k, :], h1p[1][:, k, :])) for k in range(KH)]
                product(pe, bank[HB[(KH + m) % 3]][:], pairs).then_inc(S["h_made"], 1)

            def output(c, m, first):
                pe.wait_ge(S["w_cut"], NP1 + NP2 + m // 2 + 1)
                pe.wait_ge(S["h_lo"], hid(c, 1, m))
                if m == 0 and not first:
                    pe.wait_ge(S["y_added"], tile_of(c, 0) - 1)
                for j in range(TPC):
                    rows = slice(j * P, (j + 1) * P)
                    mm = product(pe, bank[j][:], [((h2p[m % 2][0][:, rows], h2p[m % 2][1][:, rows]),
                                                   (w3p[0][:, m, :], w3p[1][:, m, :]))], first=m == 0, last=m == KH - 1)
                mm.then_inc(S["y_made"], 1)

            def step(c, first=False, last=False):
                for m in range(KH):
                    hidden1(c, m, first)
                for m in range(KH):
                    hidden2(c, m)
                    if m > 0:
                        output(c, m - 1, first)
                    if not last and 1 <= m <= TPC:
                        turn_x(c + 1, m - 1)
                output(c, KH - 1, first)

            for j in range(TPC):
                turn_x(0, j)
            step(0, first=True)
            with pe.Fori(1, NC - 1) as c:
                step(c)
            step(NC - 1, last=True)

        @block.scalar
        def _(act):
            def split_x(c, j):
                act.wait_ge(S["xT_turned"], tile_of(c, j))
                out = xTp[0][:, :, j * P:(j + 1) * P]
                act.activation(out, bank[7][:].rearrange("p (k t) -> p k t", k=KD), ACT.Copy).then_inc(S["xT_hi"], 1)

            def hidden(c, layer, m):
                act.wait_ge(S["h_made"], hid(c, layer, m))
                if layer == 1 and m >= 2:
                    act.wait_ge(S["y_made"], KH * c + m - 1)
                out = h1p[0][:, m, :] if layer == 0 else h2p[m % 2][0][:]
                act.activation(out, bank[HB[(layer * KH + m) % 3]][:], ACT.Relu, bias=b12[:, layer, m:m + 1]
                               ).then_inc(S["h_hi"], 1)

            def cut_hi(n):
                _, (hi, _), k = pieces[n]
                act.wait_ge(S[f"w_staged{n % 2}"], 16 * (n // 2 + 1))
                act.activation(hi, stage[n % 2][:].rearrange("p (k c) -> p k c", k=k), ACT.Copy).then_inc(S["w_hi"], 1)

            def step(c, last=False, first=False):
                for m in range(KH):
                    if first:
                        cut_hi(NP1 + m)
                    hidden(c, 0, m)
                for m in range(KH):
                    if first and m < NP3:
                        cut_hi(NP1 + NP2 + m)
                    hidden(c, 1, m)
                    if not last and 1 <= m <= TPC:
                        split_x(c + 1, m - 1)

            act.wait_ge(S["b_loaded"], 48)
            for n in range(NP1):
                cut_hi(n)
                split_x(0, n)
            step(0, first=True)
            with act.Fori(1, NC - 1) as c:
                step(c)
            step(NC - 1, last=True)

        @block.vector
        def _(dve):
            chain = [0]

            def then(ins):
                chain[0] = chain[0] + 1
                ins.then_inc(S["s_turn"], 1)
                dve.wait_ge(S["s_turn"], chain[0])

            def layer_norm(c, j):
                x = x_in[j % 2]
                dve.wait_ge(S[f"x_loaded{j % 2}"], 16 * (2 * c + j // 2 + 1))
                then(dve.bn_stats(bn[:], x[:]))
                then(dve.bn_aggr(mv[:], bn[:]))
                then(dve.tensor_scalar(rs[:, 2:3], mv[:, 1:2], EPS, None, ALU.add))
                then(rsqrt_steps(dve, then, rs[:, 0:1], rs[:, 2:3], rs[:, 1:2]))
                dve.tensor_scalar(x[:], x[:], mv[:, 0:1], rs[:, 0:1], ALU.subtract, ALU.mult).then_inc(S["xn_ready"], 1)

            def split_x(c, j):
                dve.wait_ge(S["xT_hi"], tile_of(c, j))
                hi, lo = (p[:, :, j * P:(j + 1) * P] for p in xTp)
                dve.tensor_tensor(lo, bank[7][:].rearrange("p (k t) -> p k t", k=KD), hi, ALU.subtract
                                  ).then_inc(S["xT_lo"], 1)

            def hidden(c, layer, m, first=False):
                if not (first and layer == 0 and m < 2):
                    dve.wait_ge(S["h_lo"], hid(c, layer, m) - 2)
                hi, lo = (p[:, m, :] if layer == 0 else p[:] for p in (h1p if layer == 0 else h2p[m % 2]))
                dve.wait_ge(S["h_hi"], hid(c, layer, m))
                dve.tensor_scalar(relu[m % 2][:], bank[HB[(layer * KH + m) % 3]][:], b12[:, layer, m:m + 1], 0.0, ALU.add, ALU.max
                                  ).then_inc(S["relu_ready"], 1)
                dve.wait_ge(S["relu_ready"], hid(c, layer, m))
                dve.tensor_tensor(lo, relu[m % 2][:], hi, ALU.subtract).then_inc(S["h_lo"], 1)

            def add_y(c, j):
                dve.wait_ge(S["bias_added"], tile_of(c, j))
                dve.wait_ge(S["y_made"], KH * (c + 1))
                dve.tensor_tensor(res[j % 2][:], res[j % 2][:], bank[j][:], ALU.add).then_inc(S["y_added"], 1)

            def step(c, first=False, last=False):
                dve.sem_clear(S["s_turn"])
                chain[0] = 0
                for m in range(KH):
                    hidden(c, 0, m, first)
                    if not first and 2 <= m < 2 + TPC:
                        add_y(c - 1, m - 2)
                for m in range(KH):
                    if not last and m < 2:
                        layer_norm(c + 1, m)
                    hidden(c, 1, m)
                    if not last and 1 <= m <= TPC:
                        split_x(c + 1, m - 1)
                        if m + 1 < TPC:
                            layer_norm(c + 1, m + 1)

            for j in range(2):
                layer_norm(0, j)
            for j in range(TPC):
                split_x(0, j)
                if j + 2 < TPC:
                    layer_norm(0, j + 2)
            dve.wait_ge(S["b_loaded"], 48)
            step(0, first=True)
            with dve.Fori(1, NC - 1) as c:
                step(c)
            step(NC - 1, last=True)
            for j in range(TPC):
                add_y(NC - 1, j)


def l1_attention(nc, sb, sem, bank, ident, x2, ctxT, pos, wq, wkv, wo, bo, x3):
    H, D, PAD = 32, 16, 32
    NG, G = 8, 4
    RING = 3
    HERE = 4
    ROT = D // 2
    BASE = 10000.0
    TWO_PI = (6.28125, 0.0019350051879882812, 3.0199158198e-07)
    ROUND = 1.5 * 2.0 ** 23

    def parts(name, shape):
        return sb("l_" + name + "_hi", shape, F32R), sb("l_" + name + "_lo", shape, F32R)

    wqp, wkvp, wop = parts("wq", [P, KD, DM]), parts("wkv", [P, KC, 2 * DM]), parts("wo", [P, KD, DM])
    stage = [sb(f"l_stage{i}", [P, 2048], F32) for i in range(3)]
    xn, res, bor = (sb("l_" + n, [P, DM], F32) for n in ("xn", "res", "bo"))
    x_all = sb("l_x_all", [P, NB, DM], F32)
    xTp = parts("xT", [P, KD, P])
    ctx_in = sb("l_ctx_in", [P, KC, P], F32)
    ctxp = parts("ctx", [P, KC, P])
    pos_sb = sb("l_pos", [P, NB, 2], F32)
    ang = sb("l_ang", [P, 4, NB * ROT], F32)
    cos2 = sb("l_cos2", [P, NB, D], F32)
    sin2 = sb("l_sin2", [P, NB, D], F32)
    cos_now = sb("l_cos_now", [P, D], F32)
    qk = [sb(f"l_qk{i}", [P, H, D], F32) for i in range(2)]
    rotA = [sb(f"l_rotA{i}", [P, H, D], F32) for i in range(2)]
    rotB = [sb(f"l_rotB{i}", [P, H, D], F32) for i in range(2)]
    roped = [sb(f"l_roped{i}", [P, H * PAD], F32) for i in range(2)]
    qkT = [sb(f"l_qkT{i}", [P, 8, P], F32) for i in range(2)]
    v_sb = sb("l_v", [P, DM], F32)
    prob = [sb(f"l_prob{i}", [P, G, P], F32) for i in range(HERE)]
    pT = [sb(f"l_pT{i}", [P, 4, P], F32) for i in range(2)]
    mx = sb("l_mx", [P, NG, 2, G], F32)
    den = sb("l_den", [P, 2, H], F32)
    o_sb = sb("l_o", [P, DM], F32)
    oTp = parts("oT", [P, KD, P])
    bn, mv = sb("l_bn", [P, NB, 6], F32), sb("l_mv", [P, NB, 2], F32)
    ln = sb("l_ln", [P, NB, 2], F32)
    ln_t = sb("l_ln_t", [P, 2, NB], F32)
    ln_now = sb("l_ln_now", [P, 2], F32)

    names = """x_loaded0 x_loaded1 ctx_loaded b_loaded w_staged0 w_staged1 w_staged2 w_hi w_cut pad_zero
        xn_ready xT_turned xT_hi xT_lo ctx_hi ctx_lo q_made k_made v_made q_copied k_copied v_copied rotA0 rotA1 rotB0
        rotB1 roped0 roped1 q0_turned q1_turned k0_turned k1_turned q0_in k0_in q1_in k1_in scored bias exped
        p_turned pT_in mixed o_ready oT_turned oT_hi oT_lo y_made y_added bo_added stored s_turn a_turn cos_here""".split()
    S = {n: sem("l_" + n) for n in names}

    def at(n, s):
        return S[n], s + 1

    def later(s):
        return not isinstance(s, int) or s > 0

    def group(s, g):
        return NG * s + g + 1

    def head(g, t):
        return NG // 2 * G * (g // 4) + 4 * t + g % 4

    block = nc.Block()
    with block:
        @block.sync
        def _(sp):
            def load_ctx(s):
                row = sp.snap(s * P)
                if later(s):
                    sp.wait_ge(*at("ctx_lo", s - 1))
                sp.dma_start(ctx_in[:], ctxT[:, :, bass.ds(row, P)]).then_inc(S["ctx_loaded"], 16)

            def store(s):
                row = sp.snap(s * P)
                sp.wait_ge(*at("bo_added", s))
                sp.dma_start(x3[bass.ds(row, P), :], res[:]).then_inc(S["stored"], 16)

            sp.dma_start(pos_sb[:], pos.rearrange("(b p) c -> p b c", p=P)).then_inc(S["b_loaded"], 16)
            sp.dma_start(bor[:], bo).then_inc(S["b_loaded"], 16)
            load_ctx(0)
            for i, tiles in enumerate(AHEAD):
                sp.dma_start(x_all[:, tiles, :], x2.rearrange("(b p) d -> p b d", p=P)[:, tiles, :]).then_inc(S[f"x_loaded{i}"], 16)
            load_ctx(1)
            with sp.Fori(1, NB - 1) as s:
                load_ctx(s + 1)
                store(s - 1)
            store(NB - 2)
            store(NB - 1)
            sp.wait_ge(S["stored"], 16 * NB)

        @block.gpsimd
        def _(pool):
            weights = [(wq.rearrange("(k p) w -> p k w", p=P), wqp), (wkv.rearrange("(k p) w -> p k w", p=P), wkvp),
                       (wo.rearrange("(k p) w -> p k w", p=P), wop)]
            for n, (src, _) in enumerate(weights):
                pool.dma_start(stage[n][:], src).then_inc(S[f"w_staged{n}"], 16)
            for i in range(2):
                pool.memset(roped[i][:], 0.0).then_inc(S["pad_zero"], 1)

            def cut_lo(n):
                hi, lo = (w[:].rearrange("p k w -> p (k w)") for w in weights[n][1])
                pool.wait_ge(S["w_hi"], n + 1)
                pool.tensor_tensor(lo, stage[n][:], hi, ALU.subtract).then_inc(S["w_cut"], 1)

            def split_ctx(s):
                pool.wait_ge(*at("ctx_hi", s))
                pool.tensor_tensor(ctxp[1][:], ctx_in[:], ctxp[0][:], ALU.subtract).then_inc(S["ctx_lo"], 1)

            def by_cosine(s, i):
                pool.wait_ge(*at(("q_copied", "k_copied")[i], s))
                if later(s):
                    pool.wait_ge(*at(f"roped{i}", s - 1))
                pool.wait_ge(*at("cos_here", s))
                pool.tensor_tensor(rotA[i][:], qk[i][:], cos_now[:].unsqueeze(1).to_broadcast([P, H, D]), ALU.mult).then_inc(S[f"rotA{i}"], 1)

            def add_bias(s):
                pool.wait_ge(*at("y_added", s))
                pool.tensor_tensor(res[:], res[:], bor[:], ALU.add).then_inc(S["bo_added"], 1)

            cut_lo(0)
            cut_lo(1)
            split_ctx(0)
            by_cosine(0, 0)
            by_cosine(0, 1)
            cut_lo(2)
            pool.wait_ge(S["b_loaded"], 32)
            split_ctx(1)
            by_cosine(1, 0)
            by_cosine(1, 1)
            with pool.Fori(1, NB - 1) as s:
                split_ctx(s + 1)
                by_cosine(s + 1, 0)
                by_cosine(s + 1, 1)
                add_bias(s - 1)
            add_bias(NB - 2)
            add_bias(NB - 1)

        @block.tensor
        def _(pe):
            def turn(b, src, what):
                for k in range(4):
                    t = pe.transpose(bank[b][:, k * P:(k + 1) * P], src[:, k * P:(k + 1) * P], ident[:])
                t.then_inc(S[what], 1)

            def turn_x(s):
                pe.wait_ge(*at("xn_ready", s))
                if later(s):
                    pe.wait_ge(*at("k1_in", s - 1))
                turn(7, xn[:], "xT_turned")

            def project(b, act, kt, wp, cols, what):
                pairs = [((act[0][:, k, :], act[1][:, k, :]), (wp[0][:, k, cols], wp[1][:, k, cols])) for k in range(kt)]
                product(pe, bank[b][:], pairs).then_inc(S[what], 1)

            def queries(s):
                pe.wait_ge(*at("xT_lo", s))
                if not later(s):
                    pe.wait_ge(S["w_cut"], 1)
                project(7, xTp, KD, wqp, slice(0, DM), "q_made")

            def keys(s):
                pe.wait_ge(*at("ctx_lo", s))
                if not later(s):
                    pe.wait_ge(S["w_cut"], 2)
                pe.wait_ge(*at("q_copied", s))
                project(7, ctxp, KC, wkvp, slice(0, DM), "k_made")

            def values(s):
                pe.wait_ge(*at("q1_in", s))
                project(3, ctxp, KC, wkvp, slice(DM, 2 * DM), "v_made")

            def turn_q(s, half):
                pe.wait_ge(*at("roped0", s))
                if half:
                    pe.wait_ge(*at("q0_in", s))
                elif later(s - 1):
                    pe.wait_ge(*at("y_added", s - 2))
                turn(3, roped[0][:, 4 * P * half:4 * P * (half + 1)], f"q{half}_turned")

            def turn_k(s, half):
                pe.wait_ge(*at("roped1", s))
                pe.wait_ge(*at(("k_copied", "k0_in")[half], s))
                turn(7, roped[1][:, 4 * P * half:4 * P * (half + 1)], f"k{half}_turned")

            def score(s, g):
                half, rows = g // 4, slice(PAD * (g % 4), PAD * (g % 4) + D)
                if g % 4 == 0:
                    pe.wait_ge(*at(f"q{half}_in", s))
                    pe.wait_ge(*at(f"k{half}_in", s))
                if g >= RING:
                    pe.wait_ge(S["exped"], group(s, g - RING))
                elif later(s):
                    pe.wait_ge(S["exped"], group(s - 1, (6, 7, 5)[g]))
                for t in range(G):
                    mm = pe.matmul(bank[g % RING][:, t * P:(t + 1) * P], qkT[0][rows, 4 * half + t, :],
                                   qkT[1][rows, 4 * half + t, :], start=True, stop=True)
                mm.then_inc(S["scored"], 1)

            def turn_p(s, g):
                pe.wait_ge(S["exped"], group(s, g))
                if g >= 2 or later(s):
                    pe.wait_ge(S["pT_in"], group(s, g - 2))
                turn(4 + g % 2, prob[g % HERE][:].rearrange("p h k -> p (h k)"), "p_turned")

            def mix(s, g):
                pe.wait_ge(S["pT_in"], group(s, g))
                if g == 0:
                    pe.wait_ge(*at("v_copied", s))
                    if later(s):
                        pe.wait_ge(*at("o_ready", s - 1))
                for t in range(G):
                    c = slice(head(g, t) * D, (head(g, t) + 1) * D)
                    mm = pe.matmul(bank[6][:, c], pT[g % 2][:, t, :], v_sb[:, c], start=True, stop=True)
                mm.then_inc(S["mixed"], 1)

            def turn_o(s):
                pe.wait_ge(*at("o_ready", s))
                pe.wait_ge(*at("v_copied", s if isinstance(s, int) and s == NB - 1 else s + 1))
                turn(3, o_sb[:], "oT_turned")

            def output(s):
                pe.wait_ge(*at("oT_lo", s))
                if not later(s):
                    pe.wait_ge(S["w_cut"], 3)
                project(3, oTp, KD, wop, slice(0, DM), "y_made")

            def step(s, last=False):
                score(s, 0)
                if not last:
                    turn_x(s + 1)
                score(s, 1)
                if later(s):
                    turn_o(s - 1)
                score(s, 2)
                turn_p(s, 0)
                score(s, 3)
                turn_p(s, 1)
                mix(s, 0)
                if not last:
                    queries(s + 1)
                score(s, 4)
                turn_p(s, 2)
                mix(s, 1)
                if later(s):
                    output(s - 1)
                score(s, 5)
                turn_p(s, 3)
                mix(s, 2)
                if not last:
                    keys(s + 1)
                score(s, 6)
                turn_p(s, 4)
                mix(s, 3)
                if not last:
                    turn_q(s + 1, 0)
                score(s, 7)
                turn_p(s, 5)
                mix(s, 4)
                if not last:
                    turn_k(s + 1, 0)
                turn_p(s, 6)
                mix(s, 5)
                if not last:
                    turn_q(s + 1, 1)
                turn_p(s, 7)
                mix(s, 6)
                if not last:
                    turn_k(s + 1, 1)
                    values(s + 1)
                mix(s, 7)

            turn_x(0)
            queries(0)
            keys(0)
            for half in range(2):
                turn_q(0, half)
                turn_k(0, half)
            values(0)
            step(0)
            with pe.Fori(1, NB - 1) as s:
                step(s)
            step(NB - 1, last=True)
            turn_o(NB - 1)
            output(NB - 1)

        @block.scalar
        def _(act):
            def split_ctx(s):
                act.wait_ge(S["ctx_loaded"], 16 * (s + 1))
                if later(s):
                    act.wait_ge(*at("v_made", s - 1))
                act.activation(ctxp[0][:], ctx_in[:], ACT.Copy).then_inc(S["ctx_hi"], 1)

            def split_x(s):
                act.wait_ge(*at("xT_turned", s))
                act.activation(xTp[0][:].rearrange("p k t -> p (k t)"), bank[7][:], ACT.Copy).then_inc(S["xT_hi"], 1)

            def copy_qk(s, i):
                act.wait_ge(*at(("q_made", "k_made")[i], s))
                if later(s):
                    act.wait_ge(*at(f"roped{i}", s - 1))
                act.activation(qk[i][:].rearrange("p h d -> p (h d)"), bank[7][:], ACT.Copy
                               ).then_inc(S[("q_copied", "k_copied")[i]], 1)

            def copy_v(s):
                act.wait_ge(*at("v_made", s))
                if later(s):
                    act.wait_ge(S["mixed"], 8 * s)
                act.activation(v_sb[:], bank[3][:], ACT.Copy).then_inc(S["v_copied"], 1)

            def queries_in(s, half):
                act.wait_ge(*at(f"q{half}_turned", s))
                act.activation(qkT[0][:, 4 * half:4 * half + 4, :].rearrange("p k t -> p (k t)"), bank[3][:],
                               ACT.Copy).then_inc(S[f"q{half}_in"], 1)

            def exps(s, g):
                act.wait_ge(S["bias"], group(s, g))
                if g >= HERE or later(s):
                    act.wait_ge(S["p_turned"], group(s, g - HERE))
                for t in range(G):
                    h = head(g, t)
                    a = act.activation(prob[g % HERE][:, t, :], bank[g % RING][:, t * P:(t + 1) * P], ACT.Exp,
                                       bias=mx[:, g, 1, t:t + 1], scale=D ** -0.5, accum_out=den[:, 0, h:h + 1])
                a.then_inc(S["exped"], 1)

            def split_o(s):
                act.wait_ge(*at("oT_turned", s))
                act.activation(oTp[0][:].rearrange("p k t -> p (k t)"), bank[3][:], ACT.Copy).then_inc(S["oT_hi"], 1)

            def step(s, last=False):
                if not last:
                    split_ctx(s + 1)
                    split_x(s + 1)
                exps(s, 0)
                if later(s):
                    split_o(s - 1)
                exps(s, 1)
                exps(s, 2)
                if not last:
                    copy_qk(s + 1, 0)
                exps(s, 3)
                exps(s, 4)
                if not last:
                    copy_qk(s + 1, 1)
                exps(s, 5)
                if not last:
                    queries_in(s + 1, 0)
                exps(s, 6)
                exps(s, 7)
                if not last:
                    queries_in(s + 1, 1)
                    copy_v(s + 1)

            def cut_hi(n):
                hi = (wqp, wkvp, wop)[n][0]
                act.wait_ge(S[f"w_staged{n}"], 16)
                act.activation(hi[:].rearrange("p k w -> p (k w)"), stage[n][:], ACT.Copy).then_inc(S["w_hi"], 1)

            cut_hi(0)
            cut_hi(1)
            split_ctx(0)
            split_x(0)
            act.wait_ge(S["a_turn"], 1)
            act.activation(ang[:, 2, :], ang[:, 0, :], ACT.Sin).then_inc(S["a_turn"], 1)
            act.activation(ang[:, 3, :], ang[:, 1, :], ACT.Sin).then_inc(S["a_turn"], 1)
            copy_qk(0, 0)
            copy_qk(0, 1)
            queries_in(0, 0)
            queries_in(0, 1)
            copy_v(0)
            cut_hi(2)
            step(0)
            with act.Fori(1, NB - 1) as s:
                step(s)
            step(NB - 1, last=True)
            split_o(NB - 1)

        @block.vector
        def _(dve):
            chain = [0]

            def then(ins):
                chain[0] = chain[0] + 1
                ins.then_inc(S["s_turn"], 1)
                dve.wait_ge(S["s_turn"], chain[0])

            def tables():
                a = ang[:, 0, :].rearrange("p (b c j) -> p b c j", b=NB, c=2)
                dve.wait_ge(S["b_loaded"], 32)
                for j in range(ROT // 2):
                    last = dve.tensor_scalar(a[:, :, :, j], pos_sb[:], BASE ** (-j / (ROT // 2)), None, ALU.mult)
                    then(last)
                turns, t = ang[:, 1, :], ang[:, 0, :]
                then(dve.tensor_scalar(turns, t, 1.0 / 6.283185307179586, ROUND, ALU.mult, ALU.add))
                then(dve.tensor_scalar(turns, turns, -ROUND, None, ALU.add))
                for part in TWO_PI:
                    then(dve.scalar_tensor_tensor(t, turns, -part, t, ALU.mult, ALU.add))
                then(dve.tensor_scalar(t, t, 3.1415925, -3.1415925, ALU.min, ALU.max))
                then(dve.scalar_tensor_tensor(turns, t, -1.0, t, ALU.mult, ALU.max))
                dve.tensor_scalar(turns, turns, -1.0, 1.5707963267948966, ALU.mult, ALU.add).then_inc(S["a_turn"], 1)
                dve.wait_ge(S["a_turn"], 3)
                for k in range(2):
                    pair = lambda x: x[:].rearrange("p b (r k) -> p (b r) k", k=2)[:, :, k]
                    then(dve.tensor_copy(pair(cos2), ang[:, 3, :]))
                    then(dve.tensor_scalar(pair(sin2), ang[:, 2, :], (-1.0, 1.0)[k], None, ALU.mult))

            def statistics(i):
                dve.wait_ge(S[f"x_loaded{i}"], 16)
                norm_statistics(dve, then, AHEAD[i], x_all, bn, mv, ln, ln_t)

            def layer_norm(s):
                if later(s):
                    dve.wait_ge(*at("xT_turned", s - 1))
                then(dve.tensor_copy(ln_now[:], ln[:].rearrange("p b c -> p (b c)")[:, bass.ds(s * 2, 2)]))
                dve.tensor_scalar(xn[:], x_all[:].rearrange("p b d -> p (b d)")[:, bass.ds(s * DM, DM)],
                                  ln_now[:, 0:1], ln_now[:, 1:2], ALU.subtract, ALU.mult).then_inc(S["xn_ready"], 1)

            def copy_cosines(s):
                if later(s):
                    dve.wait_ge(*at("rotA1", s - 1))
                dve.tensor_copy(cos_now[:], cos2[:].rearrange("p b d -> p (b d)")[:, bass.ds(s * D, D)]
                                ).then_inc(S["cos_here"], 1)

            def split_x(s):
                dve.wait_ge(*at("xT_hi", s))
                hi, lo = (p[:].rearrange("p k t -> p (k t)") for p in xTp)
                dve.tensor_tensor(lo, bank[7][:], hi, ALU.subtract).then_inc(S["xT_lo"], 1)

            def by_sine(s, i):
                dve.wait_ge(*at(("q_copied", "k_copied")[i], s))
                t = sin2[:].rearrange("p b d -> p (b d)")[:, bass.ds(s * D, D)].rearrange("p (r k) -> p r k", k=2)
                for k in range(2):
                    out = rotB[i][:].rearrange("p h (r k) -> p h r k", k=2)[:, :, :, k]
                    src = qk[i][:].rearrange("p h (r k) -> p h r k", k=2)[:, :, :, 1 - k]
                    dve.tensor_tensor(out, src, t[:, :, k].unsqueeze(1).to_broadcast([P, H, ROT]), ALU.mult
                                      ).then_inc(S[f"rotB{i}"], 1)
                if later(s):
                    dve.wait_ge(*at(("q1_turned", "k1_turned")[i], s - 1))
                dve.wait_ge(S[f"rotB{i}"], 2 * (s + 1))
                dve.wait_ge(*at(f"rotA{i}", s))
                out = roped[i][:].rearrange("p (h w) -> p h w", w=PAD)[:, :, 0:D]
                dve.tensor_tensor(out, rotA[i][:], rotB[i][:], ALU.add).then_inc(S[f"roped{i}"], 1)

            def keys_in(s, half):
                dve.wait_ge(*at(f"k{half}_turned", s))
                dve.tensor_copy(qkT[1][:, 4 * half:4 * half + 4, :].rearrange("p k t -> p (k t)"), bank[7][:]
                                ).then_inc(S[f"k{half}_in"], 1)

            def maxima(s, g):
                dve.wait_ge(S["scored"], group(s, g))
                then(dve.tensor_reduce(mx[:, g, 0, :], bank[g % RING][:].rearrange("p (t k) -> p t k", t=G), AX.X, ALU.max))
                dve.tensor_scalar(mx[:, g, 1, :], mx[:, g, 0, :], -(D ** -0.5), None, ALU.mult).then_inc(S["bias"], 1)

            def probs_in(s, g):
                dve.wait_ge(S["p_turned"], group(s, g))
                if g >= 2 or later(s):
                    dve.wait_ge(S["mixed"], group(s, g - 2))
                dve.tensor_copy(pT[g % 2][:].rearrange("p h k -> p (h k)"), bank[4 + g % 2][:]).then_inc(S["pT_in"], 1)

            def normalise(s):
                dve.wait_ge(S["mixed"], 8 * (s + 1))
                then(dve.reciprocal(den[:, 1, :], den[:, 0, :]))
                dve.tensor_tensor(o_sb[:].rearrange("p (h d) -> p h d", h=H), bank[6][:].rearrange("p (h d) -> p h d", h=H),
                                  den[:, 1, :].unsqueeze(2).to_broadcast([P, H, D]), ALU.mult).then_inc(S["o_ready"], 1)

            def split_o(s):
                dve.wait_ge(*at("oT_hi", s))
                hi, lo = (p[:].rearrange("p k t -> p (k t)") for p in oTp)
                dve.tensor_tensor(lo, bank[3][:], hi, ALU.subtract).then_inc(S["oT_lo"], 1)

            def add_y(s):
                dve.wait_ge(*at("y_made", s))
                if later(s):
                    dve.wait_ge(S["stored"], 16 * s)
                dve.tensor_tensor(res[:], x_all[:].rearrange("p b d -> p (b d)")[:, bass.ds(s * DM, DM)], bank[3][:], ALU.add
                                  ).then_inc(S["y_added"], 1)

            def step(s, last=False):
                dve.sem_clear(S["s_turn"])
                chain[0] = 0
                maxima(s, 0)
                if not last:
                    split_x(s + 1)
                maxima(s, 1)
                if later(s):
                    split_o(s - 1)
                maxima(s, 2)
                probs_in(s, 0)
                maxima(s, 3)
                probs_in(s, 1)
                if not last:
                    copy_cosines(s + 1)
                maxima(s, 4)
                probs_in(s, 2)
                if later(s):
                    add_y(s - 1)
                if not last:
                    by_sine(s + 1, 0)
                maxima(s, 5)
                probs_in(s, 3)
                maxima(s, 6)
                probs_in(s, 4)
                if not last:
                    by_sine(s + 1, 1)
                maxima(s, 7)
                probs_in(s, 5)
                if not last:
                    keys_in(s + 1, 0)
                probs_in(s, 6)
                if not isinstance(s, int) or s < NB - 2:
                    layer_norm(s + 2)
                probs_in(s, 7)
                if not last:
                    keys_in(s + 1, 1)
                normalise(s)

            statistics(0)
            layer_norm(0)
            split_x(0)
            layer_norm(1)
            tables()
            copy_cosines(0)
            dve.wait_ge(S["pad_zero"], 2)
            by_sine(0, 0)
            by_sine(0, 1)
            statistics(1)
            keys_in(0, 0)
            keys_in(0, 1)
            step(0)
            with dve.Fori(1, NB - 2) as s:
                step(s)
            step(NB - 2)
            step(NB - 1, last=True)
            split_o(NB - 1)
            add_y(NB - 1)


def expert_weights(sb):
    return [[sb(f"e_{n}_{part}", shape, F32R) for part in ("hi", "lo")]
            for n, shape in (("de", [P, KD, 1024]), ("ue", [P, 1024 // P, DM]))]


def l1_ffn_front(nc, sb, sem, bank, ident, x3, wq, deT, ue, xT_all, hqT, y, dep, uep):
    def parts(name, shape):
        return sb("r_" + name + "_hi", shape, F32R), sb("r_" + name + "_lo", shape, F32R)

    R = 4
    wqp = parts("wq", [P, KD, P])
    stage = sb("r_stage", [P, KD, P], F32)
    e_stage = [sb(f"r_e_stage{i}", [P, 1024], F32) for i in range(2)]
    xn = [sb(f"r_xn{i}", [P, DM], F32) for i in range(2)]
    xTp = [parts(f"xT{i}", [P, KD, P]) for i in range(R)]
    bn, mv = sb("r_bn", [P, NB, 6], F32), sb("r_mv", [P, NB, 2], F32)
    ln = sb("r_ln", [P, NB, 2], F32)
    ln_t = sb("r_ln_t", [P, 2, NB], F32)
    ln_now = [sb(f"r_ln_now{i}", [P, 2], F32) for i in range(2)]
    names = """y_loaded0 y_loaded1 w_staged w_hi w_cut e_staged0 e_staged1 e_hi e_cut xn_ready xT_turned xT_hi xT_lo kept0 kept1 kept2 kept3 q_made q_kept s_turn""".split()
    S = {n: sem("r_" + n) for n in names}

    def nth(t, i):
        return R * t + i + 1

    src_de = deT.rearrange("(k p) e -> p k e", p=P)
    src_ue = ue.rearrange("(k p) d -> p k d", p=P)
    pieces = [(src_de[:, :, 256 * n:256 * (n + 1)], [x[:, :, 256 * n:256 * (n + 1)] for x in dep], KD) for n in range(4)]
    pieces += [(src_ue[:, 2 * n:2 * n + 2, :], [x[:, 2 * n:2 * n + 2, :] for x in uep], 2) for n in range(4)]

    CH = 512

    block = nc.Block()
    with block:
        @block.sync
        def _(sp):
            for i, tiles in enumerate(AHEAD):
                sp.dma_start(y[:, tiles, :], x3.rearrange("(b p) d -> p b d", p=P)[:, tiles, :]).then_inc(S[f"y_loaded{i}"], 16)
                if i == 0:
                    sp.dma_start(stage[:], wq.rearrange("(k p) w -> p k w", p=P)).then_inc(S["w_staged"], 16)

            def keep(t, i):
                col = sp.snap((R * t + i) * P)
                sp.wait_ge(S["xT_lo"], nth(t, i))
                for part in range(2):
                    sp.dma_start(xT_all[part].bitcast(F32)[:, :, bass.ds(col, P)], xTp[i][part][:].bitcast(F32)).then_inc(S[f"kept{i}"], 16)

            with sp.Fori(0, NB // R) as t:
                for i in range(R):
                    keep(t, i)
            for i in range(R):
                sp.wait_ge(S[f"kept{i}"], 32 * NB // R)

        @block.tensor
        def _(pe):
            def turn(t, i):
                pe.wait_ge(S["xn_ready"], nth(t, i))
                if not isinstance(t, int) or i >= 2:
                    pe.wait_ge(S["xT_lo"], nth(t, i) - 2)
                for k in range(KD):
                    tr = pe.transpose(bank[i % 2][:, k * P:(k + 1) * P], xn[i % 2][:, k * P:(k + 1) * P], ident[:])
                tr.then_inc(S["xT_turned"], 1)

            def queries(c):
                if c == 0:
                    pe.wait_ge(S["w_cut"], 1)
                if c >= 2:
                    pe.wait_ge(S["q_kept"], c - 1)
                for i in range(R):
                    pe.wait_ge(S[f"kept{i}"], 32 * (c + 1))
                pairs = [((wqp[0][:, k, :], wqp[1][:, k, :]), [x[:, k, c * CH:(c + 1) * CH] for x in xT_all]) for k in range(KD)]
                product(pe, bank[2 + c % 2][:], pairs).then_inc(S["q_made"], 1)

            for i in range(R):
                turn(0, i)
            with pe.Fori(1, NB // R) as t:
                for i in range(R):
                    turn(t, i)
            for c in range(T // CH):
                queries(c)

        @block.scalar
        def _(act):
            def step(t, i, first=False):
                act.wait_ge(S["xT_turned"], nth(t, i))
                if not first:
                    act.wait_ge(S[f"kept{i}"], 32 * t)
                act.activation(xTp[i][0][:].rearrange("p k t -> p (k t)"), bank[i % 2][:], ACT.Copy).then_inc(S["xT_hi"], 1)

            act.wait_ge(S["w_staged"], 16)
            act.activation(wqp[0][:], stage[:], ACT.Copy).then_inc(S["w_hi"], 1)
            def cut_hi(n):
                _, (hi, _), k = pieces[n]
                act.wait_ge(S[f"e_staged{n % 2}"], 16 * (n // 2 + 1))
                act.activation(hi, e_stage[n % 2][:].rearrange("p (k c) -> p k c", k=k), ACT.Copy).then_inc(S["e_hi"], 1)

            step(0, 0, True)
            step(0, 1, True)
            for n in range(len(pieces) // 2):
                cut_hi(n)
            step(0, 2, True)
            step(0, 3, True)
            with act.Fori(1, NB // R) as t:
                for i in range(R):
                    step(t, i)
            for n in range(len(pieces) // 2, len(pieces)):
                cut_hi(n)

        @block.gpsimd
        def _(pool):
            def fetch(n):
                if n >= 2:
                    pool.wait_ge(S["e_cut"], n - 1)
                pool.dma_start(e_stage[n % 2][:].rearrange("p (k c) -> p k c", k=pieces[n][2]), pieces[n][0]
                               ).then_inc(S[f"e_staged{n % 2}"], 16)

            pool.wait_ge(S["w_hi"], 1)
            pool.tensor_tensor(wqp[1][:], stage[:], wqp[0][:], ALU.subtract).then_inc(S["w_cut"], 1)
            fetch(0)
            for n, (_, (hi, lo), k) in enumerate(pieces):
                if n + 1 < len(pieces):
                    fetch(n + 1)
                raw = e_stage[n % 2][:].rearrange("p (k c) -> p k c", k=k)
                pool.wait_ge(S["e_hi"], n + 1)
                pool.tensor_tensor(lo, raw, hi, ALU.subtract).then_inc(S["e_cut"], 1)

        @block.vector
        def _(dve):
            chain = [0]

            def then(ins):
                chain[0] = chain[0] + 1
                ins.then_inc(S["s_turn"], 1)
                dve.wait_ge(S["s_turn"], chain[0])

            def norm(t, i):
                if not isinstance(t, int) or t > 0 or i >= 2:
                    dve.wait_ge(S["xT_turned"], nth(t, i) - 2)
                now = ln_now[i % 2]
                then(dve.tensor_copy(now[:], ln[:].rearrange("p b c -> p (b c)")[:, bass.ds((R * t + i) * 2, 2)]))
                dve.tensor_scalar(xn[i % 2][:], y[:].rearrange("p b d -> p (b d)")[:, bass.ds((R * t + i) * DM, DM)],
                                  now[:, 0:1], now[:, 1:2], ALU.subtract, ALU.mult).then_inc(S["xn_ready"], 1)

            def split(t, i):
                dve.wait_ge(S["xT_hi"], nth(t, i))
                hi, lo = (p[:].rearrange("p k t -> p (k t)") for p in xTp[i])
                dve.tensor_tensor(lo, bank[i % 2][:], hi, ALU.subtract).then_inc(S["xT_lo"], 1)

            def keep_q(c):
                dve.wait_ge(S["q_made"], c + 1)
                dve.tensor_copy(hqT[:, c * CH:(c + 1) * CH], bank[2 + c % 2][:]).then_inc(S["q_kept"], 1)

            def step(t, last=False):
                dve.sem_clear(S["s_turn"])
                chain[0] = 0
                for i in range(R):
                    split(t, i)
                    if not last or i < R - 2:
                        norm(t + (i + 2) // R, (i + 2) % R)

            for i, tiles in enumerate(AHEAD):
                dve.wait_ge(S[f"y_loaded{i}"], 16)
                norm_statistics(dve, then, tiles, y, bn, mv, ln, ln_t)
                if i == 0:
                    norm(0, 0)
                    norm(0, 1)
            with dve.Fori(0, NB // R - 1) as t:
                step(t)
            step(NB // R - 1, last=True)
            for c in range(T // CH):
                keep_q(c)


def l1_experts(nc, sb, sem, bank, ident, keys, iota, left, dep, uep, xT_all, hqT, y):
    K, NX, NE, TOP = 64, 16, 1024, 8
    KE = NE // P
    LOWEST = -3.0e38

    def parts(name, shape):
        return sb("e_" + name + "_hi", shape, F32R), sb("e_" + name + "_lo", shape, F32R)

    key_sb = sb("e_keys", [P, 2, K], F32)
    iota_sb = sb("e_iota", [P, K], F32)
    left_sb = sb("e_left", [P, TOP], F32)
    xTp = parts("xT", [P, KD, P])
    z = sb("e_z", [P, 2, K, 2], F32)
    r = sb("e_r", [P, 2, K], F32)
    top = sb("e_top", [P, 2, TOP], F32)
    idx = sb("e_idx", [P, 2, TOP], U32)
    idf = sb("e_idf", [P, 2, TOP], F32)
    pairs = sb("e_pairs", [P, 4, TOP, TOP], F32)
    best = sb("e_best", [P, TOP], F32)
    small = sb("e_small", [P, 8, TOP], F32)
    hotx = sb("e_hotx", [P, NX, TOP], F32)
    hoty = sb("e_hoty", [P, K, TOP], F32)
    least = sb("e_least", [P, NX], F32)
    rank = sb("e_rank", [P, K], F32)
    e_all = sb("e_all", [P, 2, K], F32)
    e_top = sb("e_etop", [P, 2, TOP], F32)
    ex = sb("e_ex", [P, NX], F32)
    w = sb("e_w", [P, NX, K], F32)
    g = sb("e_g", [P, NE], F32)
    gTp = parts("gT", [P, KE, P])

    names = """c_loaded xT_in z_zero z_ready routed shift_ready exps_ready
        w_ready ew_made silu_ready g_ready g_turned gT_hi gT_lo y_made y_added s_turn""".split()
    S = {n: sem("e_" + n) for n in names}

    def at(n, s):
        return S[n], s + 1

    def later(s):
        return not isinstance(s, int) or s > 0

    block = nc.Block()
    with block:
        @block.sync
        def _(sp):
            def load(s):
                col = sp.snap(s * P)
                if later(s):
                    sp.wait_ge(*at("ew_made", s - 1))
                for part in range(2):
                    sp.dma_start(xTp[part][:].bitcast(F32), xT_all[part].bitcast(F32)[:, :, bass.ds(col, P)]).then_inc(S["xT_in"], 16)

            load(0)
            for dst, src in ((key_sb, keys), (iota_sb, iota), (left_sb, left)):
                sp.dma_start(dst[:], src).then_inc(S["c_loaded"], 16)
            with sp.Fori(1, NB) as s:
                load(s)

        @block.gpsimd
        def _(pool):
            pool.memset(z[:], 0.0).then_inc(S["z_zero"], 1)

        @block.tensor
        def _(pe):
            def route(s):
                pe.wait_ge(*at("z_ready", s))
                if later(s):
                    pe.wait_ge(*at("shift_ready", s - 1))
                for i in range(2):
                    mm = pe.matmul(bank[5][:, i * K:(i + 1) * K], z[:, i].rearrange("p k e -> p (k e)"), key_sb[:, i, :],
                                   start=True, stop=True)
                mm.then_inc(S["routed"], 1)

            def downs(s):
                pe.wait_ge(S["xT_in"], 32 * (s + 1))
                if later(s):
                    pe.wait_ge(S["silu_ready"], 2 * s)
                for b in range(2):
                    cols = slice(512 * b, 512 * (b + 1))
                    mm = product(pe, bank[b][:], [((xTp[0][:, k, :], xTp[1][:, k, :]), (dep[0][:, k, cols], dep[1][:, k, cols]))
                                                  for k in range(KD)])
                mm.then_inc(S["ew_made"], 1)

            def turn_g(s):
                pe.wait_ge(*at("g_ready", s))
                if later(s):
                    pe.wait_ge(S["gT_lo"], 2 * s)
                for e in range(KE):
                    t = pe.transpose(bank[2 + e // 4][:, (e % 4) * P:(e % 4 + 1) * P], g[:, e * P:(e + 1) * P], ident[:])
                t.then_inc(S["g_turned"], 1)

            def ups(s):
                pe.wait_ge(S["gT_lo"], 2 * (s + 1))
                if later(s):
                    pe.wait_ge(*at("y_added", s - 1))
                product(pe, bank[4][:], [((gTp[0][:, e, :], gTp[1][:, e, :]), (uep[0][:, e, :], uep[1][:, e, :]))
                                         for e in range(KE)]).then_inc(S["y_made"], 1)

            def step(s, left=2):
                turn_g(s)
                if left > 0:
                    downs(s + 1)
                if left > 1:
                    route(s + 2)
                ups(s)

            pe.wait_ge(S["c_loaded"], 48)
            route(0)
            downs(0)
            route(1)
            step(0)
            with pe.Fori(1, NB - 2) as s:
                step(s)
            step(NB - 2, left=1)
            step(NB - 1, left=0)

        @block.scalar
        def _(act):
            def exps(s):
                act.wait_ge(*at("shift_ready", s))
                for i in range(2):
                    act.activation(e_all[:, i, :], r[:, i, :], ACT.Exp, bias=small[:, 7, i:i + 1])
                    a = act.activation(e_top[:, i, :], top[:, i, :], ACT.Exp, bias=small[:, 7, i:i + 1])
                a.then_inc(S["exps_ready"], 1)

            def silus(s):
                act.wait_ge(*at("ew_made", s))
                if later(s):
                    act.wait_ge(*at("g_turned", s - 1))
                for b in range(2):
                    act.activation(g[:, 512 * b:512 * (b + 1)], bank[b][:], ACT.Silu).then_inc(S["silu_ready"], 1)

            def split_g(s):
                act.wait_ge(*at("g_turned", s))
                if later(s):
                    act.wait_ge(*at("y_made", s - 1))
                for b in range(2):
                    act.activation(gTp[0][:, 4 * b:4 * b + 4, :].rearrange("p e t -> p (e t)"), bank[2 + b][:], ACT.Copy
                                   ).then_inc(S["gT_hi"], 1)

            def step(s, last=False):
                split_g(s)
                if not last:
                    exps(s + 1)
                    silus(s + 1)

            exps(0)
            silus(0)
            with act.Fori(0, NB - 1) as s:
                step(s)
            step(NB - 1, last=True)

        @block.vector
        def _(dve):
            chain = [0]

            def then(ins):
                chain[0] = chain[0] + 1
                ins.then_inc(S["s_turn"], 1)
                dve.wait_ge(S["s_turn"], chain[0])

            def interleave(s):
                if later(s):
                    dve.wait_ge(*at("routed", s - 1))
                for i in range(2):
                    for e in range(2):
                        rows = slice(K * e, K * (e + 1))
                        last = dve.tensor_scalar(z[rows, i, :, e], hqT[rows, bass.ds(s * K + i * (T // 2), K)], 1.0, None,
                                                 ALU.mult)
                last.then_inc(S["z_ready"], 1)

            sums, rest, chosen, wts = (pairs[:, n] for n in range(4))

            def choose(s):
                sx, sy = top[:, 0, :], top[:, 1, :]
                flat = lambda x: x.rearrange("p a b -> p (a b)")
                dve.wait_ge(*at("routed", s))
                if later(s):
                    dve.wait_ge(*at("exps_ready", s - 1))
                then(dve.tensor_copy(r[:], bank[5][:, 0:2 * K].rearrange("p (i k) -> p i k", i=2)))
                for i in range(2):
                    m = dve.max(top[:, i, :], r[:, i, :])
                then(m)
                for i in range(2):
                    dve.max_index(idx[:, i, :], top[:, i, :], r[:, i, :])
                dve.tensor_scalar(small[:, 7, 0:2], top[:, :, 0], -1.0, None, ALU.mult).then_inc(S["shift_ready"], 1)
                then(dve.tensor_tensor(sums, sx.unsqueeze(2).to_broadcast([P, TOP, TOP]),
                                       sy.unsqueeze(1).to_broadcast([P, TOP, TOP]), ALU.add))
                dve.tensor_copy(idf[:], idx[:])
                then(dve.max(best[:], flat(sums)))
                then(dve.match_replace(flat(rest), best[:], flat(sums), LOWEST))
                then(dve.tensor_tensor(flat(chosen), flat(rest), flat(sums), ALU.not_equal))

            def weigh(s):
                dve.tensor_tensor(hoty[:], iota_sb[:].unsqueeze(2).to_broadcast([P, K, TOP]),
                                  idf[:, 1, :].unsqueeze(1).to_broadcast([P, K, TOP]), ALU.is_equal)
                then(dve.tensor_tensor(hotx[:], iota_sb[:, 0:NX].unsqueeze(2).to_broadcast([P, NX, TOP]),
                                       idf[:, 0, :].unsqueeze(1).to_broadcast([P, NX, TOP]), ALU.is_equal))
                dve.tensor_tensor(hoty[:], hoty[:], left_sb[:].unsqueeze(1).to_broadcast([P, K, TOP]), ALU.mult)
                then(dve.tensor_reduce(small[:, 0, :], chosen, AX.X, ALU.add))
                then(dve.tensor_tensor(hotx[:], hotx[:], small[:, 0, :].unsqueeze(1).to_broadcast([P, NX, TOP]), ALU.mult))
                dve.tensor_reduce(rank[:], hoty[:], AX.X, ALU.add)
                then(dve.tensor_reduce(least[:], hotx[:], AX.X, ALU.add))
                then(dve.tensor_scalar(least[:], least[:], -1.0, float(TOP), ALU.mult, ALU.add))
                dve.wait_ge(*at("exps_ready", s))
                dve.tensor_tensor(wts, e_top[:, 0, :].unsqueeze(2).to_broadcast([P, TOP, TOP]),
                                  e_top[:, 1, :].unsqueeze(1).to_broadcast([P, TOP, TOP]), ALU.mult)
                then(dve.tensor_tensor(w[:], rank[:].unsqueeze(1).to_broadcast([P, NX, K]),
                                       least[:].unsqueeze(2).to_broadcast([P, NX, K]), ALU.is_gt))
                then(dve.tensor_tensor(wts, wts, chosen, ALU.mult))
                then(dve.tensor_reduce(small[:, 1, :], wts, AX.X, ALU.add))
                dve.tensor_reduce(small[:, 2, 0:1], small[:, 1, :], AX.X, ALU.add)
                then(dve.scalar_tensor_tensor(small[:, 3, :], idf[:, 0, :], float(NX), small[:, 1, :], ALU.is_ge, ALU.mult))
                dve.tensor_reduce(small[:, 2, 1:2], small[:, 3, :], AX.X, ALU.add)
                then(dve.reciprocal(small[:, 2, 2:3], small[:, 2, 0:1]))
                dve.tensor_tensor(w[:], w[:], e_all[:, 1, :].unsqueeze(1).to_broadcast([P, NX, K]), ALU.mult)
                then(dve.tensor_scalar(ex[:], e_all[:, 0, 0:NX], small[:, 2, 2:3], None, ALU.mult))
                then(dve.tensor_tensor(w[:], w[:], ex[:].unsqueeze(2).to_broadcast([P, NX, K]), ALU.mult))
                last = w[:].rearrange("p a b -> p (a b)")[:, NE - 1:NE]
                dve.scalar_tensor_tensor(last, small[:, 2, 1:2], small[:, 2, 2:3], last, ALU.mult, ALU.add
                                         ).then_inc(S["w_ready"], 1)

            def weight(s):
                dve.wait_ge(S["silu_ready"], 2 * (s + 1))
                dve.wait_ge(*at("w_ready", s))
                dve.tensor_tensor(g[:], g[:], w[:].rearrange("p a b -> p (a b)"), ALU.mult).then_inc(S["g_ready"], 1)

            def split_g(s):
                for b in range(2):
                    dve.wait_ge(S["gT_hi"], 2 * s + b + 1)
                    hi, lo = (x[:, 4 * b:4 * b + 4, :].rearrange("p e t -> p (e t)") for x in gTp)
                    dve.tensor_tensor(lo, bank[2 + b][:], hi, ALU.subtract).then_inc(S["gT_lo"], 1)

            def add_y(s):
                dve.wait_ge(*at("y_made", s))
                row = y[:].rearrange("p b d -> p (b d)")[:, bass.ds(s * DM, DM)]
                dve.tensor_tensor(row, row, bank[4][:], ALU.add).then_inc(S["y_added"], 1)

            def step(s, left=2):
                dve.sem_clear(S["s_turn"])
                chain[0] = 0
                weight(s)
                if left > 0:
                    choose(s + 1)
                split_g(s)
                if left > 1:
                    interleave(s + 2)
                if left > 0:
                    weigh(s + 1)
                add_y(s)

            dve.wait_ge(S["z_zero"], 1)
            dve.wait_ge(S["c_loaded"], 48)
            interleave(0)
            choose(0)
            interleave(1)
            weigh(0)
            with dve.Fori(0, NB - 2) as s:
                step(s)
            step(NB - 2, left=1)
            step(NB - 1, left=0)


def l1_mlp(nc, sb, sem, bank, gate, up, down, xT_all, y, out):
    INTER = 2048
    J, CH = 2, 512
    PAIRS, NC, TPC = INTER // (J * P), T // CH, CH // P
    W = J * P

    def parts(name, shape):
        return sb("m_" + name + "_hi", shape, F32R), sb("m_" + name + "_lo", shape, F32R)

    NG, ND = KD * W, J * DM
    wp = [parts(f"w{i}", [P, 2 * NG + ND]) for i in range(2)]
    stage = sb("m_stage", [P, 2 * NG + ND], F32)
    gated = [sb(f"m_gated{j}", [P, CH], F32) for j in range(J)]
    prod = [sb(f"m_prod{j}", [P, CH], F32) for j in range(J)]
    prodp = [parts(f"prod{j}", [P, CH]) for j in range(J)]

    names = """w_staged w_hi w_cut gate_made up_made silu_ready prod_ready prod_hi prod_lo y_made y_added stored""".split()
    S = {n: sem("m_" + n) for n in names}

    def gate_of(slot, part, k, j):
        return wp[slot][part][:, k * W + j * P:k * W + (j + 1) * P]

    def up_of(slot, part, k, j):
        return wp[slot][part][:, NG + k * W + j * P:NG + k * W + (j + 1) * P]

    def down_of(slot, part, j):
        return wp[slot][part][:, 2 * NG + j * DM:2 * NG + (j + 1) * DM]

    def turns(eng, step):
        with eng.Fori(0, PAIRS // 2) as o:
            for slot in range(2):
                with eng.Fori(0, NC) as c:
                    step((2 * o + slot) * NC + c, c, slot, 2 * o + slot)

    def before(n, each, i):
        return each * n + i + 1

    def now(n, each, i):
        return each * (n + 1) + i + 1

    block = nc.Block()
    with block:
        @block.sync
        def _(sp):
            g3, u3 = (w.rearrange("(k p) f -> p k f", p=P) for w in (gate, up))
            d3 = down.rearrange("(f p) d -> p f d", p=P)

            def load(pair):
                col, row = sp.snap(pair * W), sp.snap(pair * J)
                if not isinstance(pair, int) or pair > 0:
                    sp.wait_ge(S["w_cut"], pair)
                sp.dma_start(stage[:, 0:NG].rearrange("p (k f) -> p k f", k=KD), g3[:, :, bass.ds(col, W)]).then_inc(S["w_staged"], 16)
                sp.dma_start(stage[:, NG:2 * NG].rearrange("p (k f) -> p k f", k=KD), u3[:, :, bass.ds(col, W)]).then_inc(S["w_staged"], 16)
                sp.dma_start(stage[:, 2 * NG:].rearrange("p (j d) -> p j d", j=J), d3[:, bass.ds(row, J), :]).then_inc(S["w_staged"], 16)

            load(0)
            with sp.Fori(1, PAIRS) as pair:
                load(pair)
            for c in range(NC):
                sp.wait_ge(S["y_added"], now((PAIRS - 1) * NC + c, TPC, TPC - 1))
                sp.dma_start(out[c * CH:(c + 1) * CH, :].rearrange("(b p) d -> p b d", p=P), y[:, TPC * c:TPC * (c + 1), :]
                             ).then_inc(S["stored"], 16)
            sp.wait_ge(S["stored"], 16 * NC)

        @block.tensor
        def _(pe):
            def step(n, c, slot, pair):
                col = pe.snap(c * CH)
                xs = [[xT_all[part][:, k, bass.ds(col, CH)] for part in range(2)] for k in range(KD)]
                pe.wait_ge(S["w_cut"], pair + 1)
                for j in range(J):
                    pe.wait_ge(S["prod_ready"], before(n, J, j))
                    product(pe, bank[2 * j][:], [([gate_of(slot, q, k, j) for q in range(2)], xs[k]) for k in range(KD)]
                            ).then_inc(S["gate_made"], 1)
                    product(pe, bank[2 * j + 1][:], [([up_of(slot, q, k, j) for q in range(2)], xs[k]) for k in range(KD)]
                            ).then_inc(S["up_made"], 1)
                for j in range(J):
                    pe.wait_ge(S["prod_lo"], J * n + j + 1)
                    for b in range(TPC):
                        if j == 0:
                            pe.wait_ge(S["y_added"], before(n, TPC, b))
                        rows = slice(b * P, (b + 1) * P)
                        mm = product(pe, bank[4 + b][:], [([prodp[j][q][:, rows] for q in range(2)],
                                                           [down_of(slot, q, j) for q in range(2)])],
                                     first=j == 0, last=j == J - 1)
                        if j == J - 1:
                            mm.then_inc(S["y_made"], 1)

            turns(pe, step)

        @block.scalar
        def _(act):
            def cut(pair, slot):
                act.wait_ge(S["w_staged"], 48 * (pair + 1))
                act.activation(wp[slot][0][:], stage[:], ACT.Copy).then_inc(S["w_hi"], 1)

            def step(n, c, slot, pair):
                for j in range(J):
                    act.wait_ge(S["gate_made"], J * n + j + 1)
                    act.activation(gated[j][:], bank[2 * j][:], ACT.Silu).then_inc(S["silu_ready"], 1)
                    act.wait_ge(S["prod_ready"], now(n, J, j))
                    act.activation(prodp[j][0][:], prod[j][:], ACT.Copy).then_inc(S["prod_hi"], 1)

            def pair_steps(o, slot, last=False):
                pair = 2 * o + slot
                if not last:
                    act.wait_ge(S["y_added"], before(pair * NC, TPC, TPC - 1))
                    cut(pair + 1, 1 - slot)
                with act.Fori(0, NC) as c:
                    step(pair * NC + c, c, slot, pair)

            cut(0, 0)
            with act.Fori(0, PAIRS // 2 - 1) as o:
                pair_steps(o, 0)
                pair_steps(o, 1)
            pair_steps(PAIRS // 2 - 1, 0)
            pair_steps(PAIRS // 2 - 1, 1, last=True)

        @block.gpsimd
        def _(pool):
            def cut_lo(pair, slot):
                pool.wait_ge(S["w_hi"], pair + 1)
                pool.tensor_tensor(wp[slot][1][:], stage[:], wp[slot][0][:], ALU.subtract).then_inc(S["w_cut"], 1)

            cut_lo(1, 1)
            with pool.Fori(1, PAIRS // 2) as o:
                for slot in range(2):
                    cut_lo(2 * o + slot, slot)

        @block.vector
        def _(dve):
            def step(n, c, slot, pair):
                for j in range(J):
                    dve.wait_ge(S["silu_ready"], J * n + j + 1)
                    dve.wait_ge(S["up_made"], J * n + j + 1)
                    dve.tensor_tensor(prod[j][:], gated[j][:], bank[2 * j + 1][:], ALU.mult).then_inc(S["prod_ready"], 1)
                    dve.wait_ge(S["prod_hi"], J * n + j + 1)
                    dve.tensor_tensor(prodp[j][1][:], prod[j][:], prodp[j][0][:], ALU.subtract).then_inc(S["prod_lo"], 1)
                for b in range(TPC):
                    dve.wait_ge(S["y_made"], TPC * n + b + 1)
                    row = y[:].rearrange("p b d -> p (b d)")[:, bass.ds((c * TPC + b) * DM, DM)]
                    dve.tensor_tensor(row, row, bank[4 + b][:], ALU.add).then_inc(S["y_added"], 1)

            dve.wait_ge(S["w_hi"], 1)
            dve.tensor_tensor(wp[0][1][:], stage[:], wp[0][0][:], ALU.subtract).then_inc(S["w_cut"], 1)
            dve.sem_inc(S["prod_ready"], J)
            dve.sem_inc(S["y_added"], TPC)
            turns(dve, step)


def build(nc, a, out):
    x1 = nc.dram_tensor("x1", (T, DM), F32).ap()
    x2 = nc.dram_tensor("x2", (T, DM), F32).ap()
    x3 = nc.dram_tensor("x3", (T, DM), F32).ap()
    with ExitStack() as top:
        stage_sems = []

        def sem(name):
            stage_sems.append(nc.alloc_semaphore(name=name))
            return stage_sems[-1]

        def stage_ends():
            nc.clear_and_free_semaphores(stage_sems)
            nc.all_engine_barrier()
            stage_sems.clear()

        def holds(ctx):
            return lambda name, shape, dtype: ctx.enter_context(nc.sbuf_tensor(name, shape, dtype))

        bank = [top.enter_context(nc.psum_tensor(f"bank{i}", [P, 512], F32)) for i in range(8)]
        ident = top.enter_context(nc.sbuf_tensor("ident", [P, P], F32))
        ident_loaded = sem("ident_loaded")
        with nc.Block() as block:
            @block.sync
            def _(sp):
                sp.dma_start(ident[:], a["ident"]).then_inc(ident_loaded, 16)
                sp.wait_ge(ident_loaded, 16)
        with ExitStack() as c:
            l0_attention(nc, holds(c), sem, bank, ident, a["x"], a["ctxT"], a["wq0"], a["wk0"], a["wv0"], a["wo0"],
                         a["gq"], a["gk"], x1)
        stage_ends()
        with ExitStack() as c:
            l0_ffn(nc, holds(c), sem, bank, ident, x1, a["w1"], a["b1"], a["w2"], a["b2"], a["w3"], a["b3"], x2)
        stage_ends()
        with ExitStack() as c:
            l1_attention(nc, holds(c), sem, bank, ident, x2, a["ctxT"], a["pos"], a["wq1"], a["wkv"], a["wo1"], a["bo"], x3)
        stage_ends()
        with ExitStack() as kept:
            xT_all = [holds(kept)(f"xT_all{i}", [P, KD, T], F32R) for i in range(2)]
            y = holds(kept)("y_all", [P, NB, DM], F32)
            with ExitStack() as routing:
                hqT = holds(routing)("hqT", [P, T], F32)
                dep, uep = expert_weights(holds(routing))
                with ExitStack() as c:
                    l1_ffn_front(nc, holds(c), sem, bank, ident, x3, a["wr"], a["deT"], a["ue"], xT_all, hqT, y,
                                 dep, uep)
                with ExitStack() as c:
                    l1_experts(nc, holds(c), sem, bank, ident, a["keys"], a["iota"], a["left"], dep, uep,
                               xT_all, hqT, y)
            with ExitStack() as c:
                l1_mlp(nc, holds(c), sem, bank, a["gate"], a["up"], a["down"], xT_all, y, out)


def kernel(x, ctx_1024, fside_BxSx2_0, L0_xattn_Wq, L0_xattn_Wk, L0_xattn_Wv, L0_xattn_Wo, L0_xattn_gq, L0_xattn_gk,
           L0_ffn_W1, L0_ffn_b1, L0_ffn_W2, L0_ffn_b2, L0_ffn_W3, L0_ffn_b3, L1_xattn_Wq, L1_xattn_Wkv, L1_xattn_Wout,
           L1_xattn_bout, L1_ffn_W_q, L1_ffn_keys, L1_ffn_down_embed, L1_ffn_up_embed, L1_ffn_gate_w, L1_ffn_up_w,
           L1_ffn_down_w):
    import numpy as np
    import concourse.bacc as _bacc
    from concourse.bass_utils import run_bass_kernel_spmd as _run
    nc = _bacc.Bacc("TRN2", target_bir_lowering=False, num_devices=1)

    def halves(w):
        w = np.asarray(w)
        return w.reshape(w.shape[0], 2, 1024).transpose(1, 0, 2)

    def on_rows(b):
        return np.broadcast_to(b, (P, len(b)))

    laid_out = {
        "ident": np.eye(P, dtype=np.float32),
        "x": np.asarray(x).reshape(T, DM),
        "ctxT": np.asarray(ctx_1024).reshape(T, KC, P).transpose(2, 1, 0),
        "wq0": halves(L0_xattn_Wq), "wk0": halves(L0_xattn_Wk), "wv0": halves(L0_xattn_Wv),
        "wo0": np.asarray(L0_xattn_Wo).reshape(2, 1024, DM),
        "gq": np.asarray(L0_xattn_gq).reshape(P, 1), "gk": np.asarray(L0_xattn_gk).reshape(P, 1),
        "w1": np.asarray(L0_ffn_W1).T, "w2": np.asarray(L0_ffn_W2).T, "w3": np.asarray(L0_ffn_W3).T,
        "b1": np.asarray(L0_ffn_b1).reshape(8, P).T, "b2": np.asarray(L0_ffn_b2).reshape(8, P).T,
        "b3": on_rows(np.asarray(L0_ffn_b3)),
        "pos": np.asarray(fside_BxSx2_0).reshape(T, 2),
        "wq1": np.asarray(L1_xattn_Wq), "wkv": np.asarray(L1_xattn_Wkv), "wo1": np.asarray(L1_xattn_Wout),
        "bo": on_rows(np.asarray(L1_xattn_bout)),
        "wr": np.asarray(L1_ffn_W_q),
        "keys": np.concatenate([np.asarray(L1_ffn_keys)] * 2, 1).transpose(1, 0, 2),
        "iota": on_rows(np.arange(64, dtype=np.float32)), "left": on_rows(np.arange(8, 0, -1).astype(np.float32)),
        "deT": np.asarray(L1_ffn_down_embed).T, "ue": np.asarray(L1_ffn_up_embed),
        "gate": np.asarray(L1_ffn_gate_w), "up": np.asarray(L1_ffn_up_w), "down": np.asarray(L1_ffn_down_w),
    }
    arrays = {"in_" + name: np.ascontiguousarray(v) for name, v in laid_out.items()}
    given = {name[3:]: nc.dram_tensor(name, v.shape, mybir.dt.from_np(v.dtype), kind="ExternalInput").ap()
             for name, v in arrays.items()}
    build(nc, given, nc.dram_tensor("out_0", (T, DM), F32, kind="ExternalOutput").ap())
    return _run(nc, [arrays], core_ids=[0]).results[0]["out_0"].reshape(16, 128, 512)
```
